# Optimizing a Trainium2 kernel written in Bass

```python
import numpy as np
import jax
import jax.numpy as jnp

def _softmax(x, axis=-1):
    return jax.nn.softmax(x, axis=axis)

def _gelu(x):
    return jax.nn.gelu(x, approximate=True)

def _silu(x):
    return jax.nn.silu(x)

def _sigmoid(x):
    return jax.nn.sigmoid(x)

def _layernorm(x, axis=-1, eps=1e-05):
    m = jnp.mean(x, axis=axis, keepdims=True)
    v = jnp.var(x, axis=axis, keepdims=True)
    return (x - m) / jnp.sqrt(v + eps)

def _scatter_add(tgt, idx, src, axis=0):
    return tgt.at[idx].add(src)

def _segment_sum(src, seg, n):
    return jax.ops.segment_sum(src, seg, n)
kernel_name = 'mk_prb_d1_jaxref_r8_0edf3e'

def setup_inputs(seed: int=0):
    np.random.seed(seed)
    _w = jnp.asarray

    def _L0_attn_setup():
        import jax, jax.numpy as jnp
        import numpy as np
        import math
        H = 256
        B = 4
        T = 256
        LAYERS = 24
        INDEX = 3
        EPS = 1e-05

        def _layer_norm(x, g, b):
            m = jnp.mean(x, axis=-1, keepdims=True)
            v = jnp.mean((x - m) ** 2, axis=-1, keepdims=True)
            return (x - m) * jax.lax.rsqrt(v + EPS) * g + b

        def _time_shift(x):
            return jnp.pad(x, ((0, 0), (1, 0), (0, 0)))[:, :-1, :]

        def _wkv_run(k, v, tm_first, tm_decay):
            C = k.shape[-1]
            aa = jnp.zeros((C,), k.dtype)
            bb = jnp.zeros((C,), k.dtype)
            pp = jnp.full((C,), -1e+38, k.dtype)
            ww = tm_first + k
            p = jnp.maximum(pp, ww)
            e1 = jnp.exp(pp - p)
            e2 = jnp.exp(ww - p)
            a = e1 * aa + e2 * v
            b = e1 * bb + e2
            return a / b
        key = jax.random.key(seed)
        ks = jax.random.split(key, 9)
        i = jnp.arange(H, dtype=jnp.float32)
        r01 = INDEX / (LAYERS - 1)
        r1pz = 1.0 - INDEX / LAYERS
        tm_decay = -5.0 + 8.0 * (i / (H - 1)) ** (0.7 + 1.3 * r01)
        zigzag = ((jnp.arange(H) + 1) % 3 - 1).astype(jnp.float32) * 0.5
        tm_first = jnp.float32(math.log(0.3)) + zigzag
        xr = i / H
        tm_mk = (xr ** r1pz)[None, None, :]
        tm_mv = tm_mk + 0.3 * r01
        tm_mr = (xr ** (0.5 * r1pz))[None, None, :]
        cm_mk = (xr ** r1pz)[None, None, :]
        cm_mr = (xr ** r1pz)[None, None, :]
        s = 1.0 / math.sqrt(H)
        s4 = 1.0 / math.sqrt(4 * H)
        Wk = jax.random.normal(ks[0], (H, H), jnp.float32) * s
        Wv = jax.random.normal(ks[1], (H, H), jnp.float32) * s
        Wr = jax.random.normal(ks[2], (H, H), jnp.float32) * s
        Wo = jax.random.normal(ks[3], (H, H), jnp.float32) * s
        Wkey = jax.random.normal(ks[4], (4 * H, H), jnp.float32) * s
        Wval = jax.random.normal(ks[5], (H, 4 * H), jnp.float32) * s4
        Wcr = jax.random.normal(ks[6], (H, H), jnp.float32) * s
        x = jax.random.normal(ks[7], (B, T, H), jnp.float32)
        return {'x': x, 'ln1_g': jnp.ones((H,), jnp.float32), 'ln1_b': jnp.zeros((H,), jnp.float32), 'ln2_g': jnp.ones((H,), jnp.float32), 'ln2_b': jnp.zeros((H,), jnp.float32), 'tm_decay': tm_decay, 'tm_first': tm_first, 'tm_mk': tm_mk, 'tm_mv': tm_mv, 'tm_mr': tm_mr, 'Wk': Wk, 'Wv': Wv, 'Wr': Wr, 'Wo': Wo, 'cm_mk': cm_mk, 'cm_mr': cm_mr, 'Wkey': Wkey, 'Wval': Wval, 'Wcr': Wcr}
    _L0_attn_in = _L0_attn_setup()

    def _L0_ffn_setup():
        import jax, jax.numpy as jnp
        import numpy as np
        JITTER_EPS = 0.01
        NUM_EXPERTS = 8
        TOP_K = 2
        HIDDEN = 256
        INTER = 512

        def _routing(logits):
            top2_vals, top2_idx = jax.lax.top_k(logits, TOP_K)

            def one_multiplier(thresh, base_scores, sel):
                factor = jnp.maximum(jnp.abs(logits), thresh)
                jitter_mask = (thresh - logits) / factor > 2.0 * JITTER_EPS
                s = jnp.where(jitter_mask, -jnp.inf, base_scores)
                p = jax.nn.softmax(s, axis=-1)
                return jnp.take_along_axis(p, sel[:, None], axis=-1)
            m1 = one_multiplier(top2_vals[:, 0:1], logits, top2_idx[:, 0])
            sel0_onehot = jax.nn.one_hot(top2_idx[:, 0], logits.shape[-1], dtype=bool)
            scores2 = jnp.where(sel0_onehot, -jnp.inf, logits)
            m2 = one_multiplier(top2_vals[:, 1:2], scores2, top2_idx[:, 1])
            multiplier = jnp.concatenate([m1, m2], axis=-1)
            return (multiplier, top2_idx)
        key = jax.random.key(seed)
        ks = jax.random.split(key, 5)
        B, S = (2, 256)
        hidden_states = jax.random.normal(ks[0], (B, S, HIDDEN), dtype=jnp.float32)
        scale_h = 1.0 / np.sqrt(HIDDEN)
        scale_i = 1.0 / np.sqrt(INTER)
        gate_w = jax.random.normal(ks[1], (NUM_EXPERTS, HIDDEN), dtype=jnp.float32) * scale_h
        w1 = jax.random.normal(ks[2], (NUM_EXPERTS, INTER, HIDDEN), dtype=jnp.float32) * scale_h
        w3 = jax.random.normal(ks[3], (NUM_EXPERTS, INTER, HIDDEN), dtype=jnp.float32) * scale_h
        w2 = jax.random.normal(ks[4], (NUM_EXPERTS, HIDDEN, INTER), dtype=jnp.float32) * scale_i
        return {'hidden_states': hidden_states, 'gate_w': gate_w, 'w1': w1, 'w2': w2, 'w3': w3}
    _L0_ffn_in = _L0_ffn_setup()
    _d = {'L0_attn_x': _L0_attn_in['x'], 'L0_attn_ln1_g': _L0_attn_in['ln1_g'], 'L0_attn_ln1_b': _L0_attn_in['ln1_b'], 'L0_attn_ln2_g': _L0_attn_in['ln2_g'], 'L0_attn_ln2_b': _L0_attn_in['ln2_b'], 'L0_attn_tm_decay': _L0_attn_in['tm_decay'], 'L0_attn_tm_first': _L0_attn_in['tm_first'], 'L0_attn_tm_mk': _L0_attn_in['tm_mk'], 'L0_attn_tm_mv': _L0_attn_in['tm_mv'], 'L0_attn_tm_mr': _L0_attn_in['tm_mr'], 'L0_attn_Wk': _L0_attn_in['Wk'], 'L0_attn_Wv': _L0_attn_in['Wv'], 'L0_attn_Wr': _L0_attn_in['Wr'], 'L0_attn_Wo': _L0_attn_in['Wo'], 'L0_attn_cm_mk': _L0_attn_in['cm_mk'], 'L0_attn_cm_mr': _L0_attn_in['cm_mr'], 'L0_attn_Wkey': _L0_attn_in['Wkey'], 'L0_attn_Wval': _L0_attn_in['Wval'], 'L0_attn_Wcr': _L0_attn_in['Wcr'], 'L0_ffn_gate_w': _L0_ffn_in['gate_w'], 'L0_ffn_w1': _L0_ffn_in['w1'], 'L0_ffn_w2': _L0_ffn_in['w2'], 'L0_ffn_w3': _L0_ffn_in['w3']}
    _x0 = _d['L0_attn_x']
    _d['L0_attn_x'] = jax.random.normal(jax.random.fold_in(jax.random.key(seed), 1), (4, 1024, 256), dtype=_x0.dtype)
    del _x0
    return _d

def reference(L0_attn_x, L0_attn_ln1_g, L0_attn_ln1_b, L0_attn_ln2_g, L0_attn_ln2_b, L0_attn_tm_decay, L0_attn_tm_first, L0_attn_tm_mk, L0_attn_tm_mv, L0_attn_tm_mr, L0_attn_Wk, L0_attn_Wv, L0_attn_Wr, L0_attn_Wo, L0_attn_cm_mk, L0_attn_cm_mr, L0_attn_Wkey, L0_attn_Wval, L0_attn_Wcr, L0_ffn_gate_w, L0_ffn_w1, L0_ffn_w2, L0_ffn_w3):

    def _L0_attn_ref(x, ln1_g, ln1_b, ln2_g, ln2_b, tm_decay, tm_first, tm_mk, tm_mv, tm_mr, Wk, Wv, Wr, Wo, cm_mk, cm_mr, Wkey, Wval, Wcr):
        import jax, jax.numpy as jnp
        import numpy as np
        import math
        H = 256
        B = 4
        T = 256
        LAYERS = 24
        INDEX = 3
        EPS = 1e-05

        def _layer_norm(x, g, b):
            m = jnp.mean(x, axis=-1, keepdims=True)
            v = jnp.mean((x - m) ** 2, axis=-1, keepdims=True)
            return (x - m) * jax.lax.rsqrt(v + EPS) * g + b

        def _time_shift(x):
            return jnp.pad(x, ((0, 0), (1, 0), (0, 0)))[:, :-1, :]

        def _wkv_run(k, v, tm_first, tm_decay):
            C = k.shape[-1]
            aa = jnp.zeros((C,), k.dtype)
            bb = jnp.zeros((C,), k.dtype)
            pp = jnp.full((C,), -1e+38, k.dtype)
            ww = tm_first + k
            p = jnp.maximum(pp, ww)
            e1 = jnp.exp(pp - p)
            e2 = jnp.exp(ww - p)
            a = e1 * aa + e2 * v
            b = e1 * bb + e2
            return a / b
        h = _layer_norm(x, ln1_g, ln1_b)
        hh = _time_shift(h)
        k = (h * tm_mk + hh * (1 - tm_mk)) @ Wk.T
        v = (h * tm_mv + hh * (1 - tm_mv)) @ Wv.T
        r = (h * tm_mr + hh * (1 - tm_mr)) @ Wr.T
        wkv = _wkv_run(k, v, tm_first, tm_decay)
        x = x + jax.nn.sigmoid(r) * wkv @ Wo.T
        h = _layer_norm(x, ln2_g, ln2_b)
        hh = _time_shift(h)
        kk = (h * cm_mk + hh * (1 - cm_mk)) @ Wkey.T
        kv = jax.nn.silu(kk) @ Wval.T
        sr = jax.nn.sigmoid((h * cm_mr + hh * (1 - cm_mr)) @ Wcr.T)
        x = x + sr * kv
        return x

    def _L0_ffn_ref(hidden_states, gate_w, w1, w2, w3):
        import jax, jax.numpy as jnp
        import numpy as np
        JITTER_EPS = 0.01
        NUM_EXPERTS = 8
        TOP_K = 2
        HIDDEN = 256
        INTER = 512

        def _routing(logits):
            top2_vals, top2_idx = jax.lax.top_k(logits, TOP_K)

            def one_multiplier(thresh, base_scores, sel):
                factor = jnp.maximum(jnp.abs(logits), thresh)
                jitter_mask = (thresh - logits) / factor > 2.0 * JITTER_EPS
                s = jnp.where(jitter_mask, -jnp.inf, base_scores)
                p = jax.nn.softmax(s, axis=-1)
                return jnp.take_along_axis(p, sel[:, None], axis=-1)
            m1 = one_multiplier(top2_vals[:, 0:1], logits, top2_idx[:, 0])
            sel0_onehot = jax.nn.one_hot(top2_idx[:, 0], logits.shape[-1], dtype=bool)
            scores2 = jnp.where(sel0_onehot, -jnp.inf, logits)
            m2 = one_multiplier(top2_vals[:, 1:2], scores2, top2_idx[:, 1])
            multiplier = jnp.concatenate([m1, m2], axis=-1)
            return (multiplier, top2_idx)
        B, S, H = hidden_states.shape
        x = hidden_states.reshape(-1, H)
        logits = jnp.einsum('th,eh->te', x, gate_w)
        multiplier, top2_idx = _routing(logits)
        out = jnp.zeros_like(x)
        for e in range(NUM_EXPERTS):
            w_e = jnp.sum(multiplier * (top2_idx == e), axis=-1)
            h = jax.nn.silu(x @ w1[e].T) * (x @ w3[e].T)
            out = out + w_e[:, None] * (h @ w2[e].T)
        return out.reshape(B, S, H)
    x = L0_attn_x
    xn = _layernorm(x, axis=-1)
    x = x + _L0_attn_ref(xn, L0_attn_ln1_g, L0_attn_ln1_b, L0_attn_ln2_g, L0_attn_ln2_b, L0_attn_tm_decay, L0_attn_tm_first, L0_attn_tm_mk, L0_attn_tm_mv, L0_attn_tm_mr, L0_attn_Wk, L0_attn_Wv, L0_attn_Wr, L0_attn_Wo, L0_attn_cm_mk, L0_attn_cm_mr, L0_attn_Wkey, L0_attn_Wval, L0_attn_Wcr) + _L0_ffn_ref(xn, L0_ffn_gate_w, L0_ffn_w1, L0_ffn_w2, L0_ffn_w3)
    return x

_drawn_inputs = setup_inputs


def setup_inputs(seed=0):
    import zlib

    import numpy as np

    out = dict(_drawn_inputs(seed))
    spreads = {'L0_attn_ln1_g': (1.0, 0.2),
     'L0_attn_ln1_b': (0.0, 0.311),
     'L0_attn_ln2_g': (1.0, 0.6),
     'L0_attn_ln2_b': (0.0, 0.536)}
    factors = {}
    for name, (base, spread) in spreads.items():
        noise = np.random.default_rng([zlib.crc32(name.encode()), seed]).standard_normal(out[name].shape)
        drawn = base * np.exp(spread * noise) if base else spread * noise
        out[name] = jnp.asarray(drawn.astype(out[name].dtype))
    for name, factor in factors.items():
        out[name] = (out[name] * factor).astype(out[name].dtype)
    return out
```

```python
from contextlib import ExitStack

import concourse.bass as bass
from concourse import mybir

ALU = mybir.AluOpType
ACT = mybir.ActivationFunctionType
AX = mybir.AxisListType
F32 = mybir.dt.float32
F32R = mybir.dt.float32r
F16 = mybir.dt.float16
I32 = mybir.dt.int32
U32 = mybir.dt.uint32

P = 128
H = 256
HC = H // P
SEQ = 1024
NSEQ = 4
T = SEQ * NSEQ
BT = 512
BJ = BT // P
NB = T // BT
NJ = T // P
E = 8
F = 512
KEY = 4 * H
KQ = KEY // P
TOPK = 2
NT = T * TOPK // P + E - 1
EW = 2 * HC * F + (F // P) * H
W1, W3, W2 = 0, HC * F, 2 * HC * F
EPS = 1e-5
JITTER = 0.02
PP0 = 1e38
XS = 1024.0
WK, WV, WR, WO = 0, HC * H, 2 * HC * H, 3 * HC * H
WCR = 4 * HC * H
WKEY = 5 * HC * H
WVAL = WKEY + HC * KEY
WALL = WVAL + KQ * H
N_CONST = 14
R_EXP = (12, 24)
R_PICKS = 28
LG1, LB1, LG2, LB2, TF, MK, MV, MR, CMK, CMR = range(10)


def build(nc, x, vecs, gate, wmix, wexp, out):
    ctx = ExitStack()
    with ctx:
        place = [nc.sbuf_base]

        def sb(name, shape, dt, at=None):
            words = 1
            for n in shape[1:]:
                words *= n
            size = words * (2 if dt == F16 else 4)
            start = place[0] if at is None else at
            start = (start + 31) // 32 * 32
            if at is None:
                place[0] = start + size
            assert start + size <= nc.sbuf_top, (name, start + size)
            return nc.alloc_sbuf_tensor_at(name, shape, dt, offset=start), start + size

        def S(name):
            return ctx.enter_context(nc.semaphore(name))

        def tensor(name, shape, dt):
            return sb(name, shape, dt)[0]

        id32 = tensor("id32", [P, P], F32)
        id16 = tensor("id16", [P, P], F16)
        ones = tensor("ones", [P, NJ * E], F32)
        before = tensor("before", [P, P], F32)
        lane = tensor("lane", [P, P], F32)
        tokid = tensor("tokid", [P, NJ], F32)
        tile0 = tensor("tile0", [P, NT], F32)
        down = tensor("down", [P, NJ, E], F32)
        vec = tensor("vec", [P, HC, 10], F32)
        tfp = tensor("tfp", [P, HC], F32)
        gw = tensor("gw", [P, HC, E], F32)
        halfneg = tensor("halfneg", [P, BJ], F32)
        logit = tensor("logit", [P, NJ, E], F32)
        gain = tensor("gain", [P, TOPK, NJ], F32)
        slot = tensor("slot", [P, TOPK, NJ], I32)
        slot_tok = tensor("slot_tok", [P, NT], I32)
        tile_exp = tensor("tile_exp", [P, NT], F32)
        tile_off = tensor("tile_off", [P, NT], I32)
        unx = tensor("unx", [P, NT], F32)
        uny = tensor("uny", [P, NT], F32)
        unscale = tensor("unscale", [P, E, 3], F32)
        pbx = tensor("pbx", [P, E], F32)
        un32 = tensor("un32", [P, E], F32)
        picked = tensor("picked", [P, NT], F32)
        small0 = place[0]

        xx = [tensor(f"xx{u}", [P, BJ, H], F32) for u in range(2)]
        xn = [tensor(f"xn{u}", [P, BJ, H], F32) for u in range(2)]
        hn = tensor("hn", [P, BJ, H], F32)
        stats = tensor("stats", [P, BJ, 6], F32)
        mv = tensor("mv", [P, BJ, 2], F32)
        rstd = tensor("rstd", [P, BJ], F32)
        ht = [tensor(f"ht{u}", [P, HC, BT + 1], F32) for u in range(2)]
        h2t = [tensor(f"h2t{u}", [P, HC, BT + 1], F32) for u in range(2)]
        dif = tensor("dif", [P, HC, BT], F32)
        mixf = [tensor(f"mixf{u}", [P, HC, BT], F32) for u in range(2)]
        fhi = [tensor(f"fhi{u}", [P, HC, BT], F32R) for u in range(2)]
        flo = [tensor(f"flo{u}", [P, HC, BT], F32R) for u in range(2)]
        chi = [tensor(f"chi{u}", [P, HC, BT], F32R) for u in range(2)]
        clo = [tensor(f"clo{u}", [P, HC, BT], F32R) for u in range(2)]
        e2 = tensor("e2", [P, HC, BT], F32)
        rb = tensor("rb", [P, HC, BT], F32)
        at = place[0]
        av = tensor("av", [P, HC, BT], F32)
        tr = tensor("tr", [P, HC, BT], F32)
        tc = tensor("tc", [P, HC, BT], F32)
        uu = tensor("uu", [P, HC, BT], F32)
        skf = [tensor(f"skf{u}", [P, BT], F32) for u in range(2)]
        skhi = [tensor(f"skhi{u}", [P, BT], F32R) for u in range(2)]
        sklo = [tensor(f"sklo{u}", [P, BT], F32R) for u in range(2)]
        stage = tensor("stage", [P, 3, EW // 3], F32)
        ehi = tensor("ehi", [P, 3, EW // 3], F16)
        elo = tensor("elo", [P, 3, EW // 3], F16)
        big = tensor("big", [P, 3], F32)
        pw2 = tensor("pw2", [P, 3], F32)
        pwi = tensor("pwi", [P, 3], F32)
        scl = tensor("scl", [P, 3], F32)
        whi = tensor("whi", [P, WALL], F32R)
        wlo = tensor("wlo", [P, WALL], F32R)
        assert EW == 3 * (EW // 3) and W3 == EW // 3 and W2 == 2 * (EW // 3)

        place[0] = small0
        ewh = tensor("ewh", [P, E * EW], F16)
        ewl = tensor("ewl", [P, E * EW], F16)
        xg = [tensor(f"xg{u}", [P, H], F32) for u in range(3)]
        xthi = [tensor(f"xthi{u}", [P, H], F16) for u in range(2)]
        xtlo = [tensor(f"xtlo{u}", [P, H], F16) for u in range(2)]
        sa = [tensor(f"sa{u}", [P, F], F32) for u in range(2)]
        hh = [tensor(f"hh{u}", [P, F], F32) for u in range(2)]
        hhi = [tensor(f"hhi{u}", [P, F], F16) for u in range(2)]
        hlo = [tensor(f"hlo{u}", [P, F], F16) for u in range(2)]
        hthi = [tensor(f"hthi{u}", [P, F], F16) for u in range(2)]
        htlo = [tensor(f"htlo{u}", [P, F], F16) for u in range(2)]
        yb = [tensor(f"yb{u}", [P, H], F32) for u in range(2)]
        hmax = [tensor(f"hmax{u}", [P, 1], F32) for u in range(2)]
        hinv = [tensor(f"hinv{u}", [P, 1], F32) for u in range(2)]
        yscl = [tensor(f"yscl{u}", [P, 1], F32) for u in range(2)]
        gidx = [tensor(f"gidx{u}", [P, 1], I32) for u in range(2)]
        y1 = [tensor(f"y1{u}", [P, H], F32) for u in range(2)]
        y2 = [tensor(f"y2{u}", [P, H], F32) for u in range(2)]
        ac = [tensor(f"ac{u}", [P, H], F32) for u in range(2)]
        cidx = [tensor(f"cidx{u}", [P, TOPK], I32) for u in range(2)]

        routes = {}

        def rt(name, shape, dt=F32):
            nonlocal at
            routes[name], at = sb("rt_" + name, shape, dt, at)
            return routes[name]

        ps = ctx.enter_context(nc.psum_tensor("ps", [P, 8, 512], F32))
        xn_d = nc.dram_tensor("xn_scratch", (T, H), F32, kind="Internal").ap()
        acc_d = nc.dram_tensor("acc_scratch", (T, H), F32, kind="Internal").ap()
        y_d = nc.dram_tensor("y_scratch", (NT * P, H), F32, kind="Internal").ap()
        ehi_d = nc.dram_tensor("ehi_scratch", (E * P, EW), F16, kind="Internal").ap()
        elo_d = nc.dram_tensor("elo_scratch", (E * P, EW), F16, kind="Internal").ap()

        def block_rows(d, b):
            return d[bass.ds(b * BT, BT), :].rearrange("(j p) n -> p j n", p=P)

        class Signal:
            def __init__(self, name, credit=0, step=1):
                self.sem = ctx.enter_context(nc.semaphore(name))
                self.credit, self.step = credit, step
                self.one = (self.sem, step)

            def at(self, n):
                return self.sem, (n + self.credit) * self.step

        def D(name, credit=0):
            return Signal(name, credit, 16)

        passed = Signal("passed")
        const_ld, const_ok = D("const_ld"), Signal("const_ok")
        n_ld = [D(f"n_ld{u}") for u in range(2)]
        n_stats, n_mv, n_eps, n_rstd = Signal("n_stats"), Signal("n_mv"), Signal("n_eps"), Signal("n_rstd")
        n_xn = Signal("n_xn", 1)
        n_st = [D(f"n_st{u}", 1) for u in range(2)]
        n_tp = Signal("n_tp", 2)
        n_xt = Signal("n_xt", 2)
        n_lg = Signal("n_lg", 2)
        n_logit = Signal("n_logit", 2)
        r_dve, r_act, r_pe = Signal("r_dve"), Signal("r_act"), Signal("r_pe")
        r_hot = Signal("r_hot")
        r_perm = Signal("r_perm", 1)
        r_ready = Signal("r_ready")
        wst_ld, wst_hi, wst_lo = D("wst_ld"), Signal("wst_hi"), Signal("wst_lo")
        m_ldn = [D(f"m_ldn{u}") for u in range(2)]
        m_ldx = [D(f"m_ldx{u}") for u in range(2)]
        m_st = [D(f"m_st{u}") for u in range(2)]
        m_stats, m_mv, m_eps, m_rstd = (Signal(n) for n in ("m_stats", "m_mv", "m_eps", "m_rstd"))
        m_hn = Signal("m_hn", 1)
        m_tp = Signal("m_tp", 1)
        m_ht = Signal("m_ht", 1)
        m_dif = Signal("m_dif")
        m_mixf, m_mixhi, m_mixlo = Signal("m_mixf", 1), Signal("m_mixhi", 2), Signal("m_mixlo", 2)
        m_k, m_v = Signal("m_k"), Signal("m_v")
        m_r, m_wo, m_cr = (Signal(n, 1) for n in ("m_r", "m_wo", "m_cr"))
        m_delta, m_exp, m_tr = (Signal(n) for n in ("m_delta", "m_exp", "m_tr"))
        m_wkv, m_av = Signal("m_wkv", 1), Signal("m_av", 1)
        m_rw, m_tc = (Signal(n) for n in ("m_rw", "m_tc"))
        m_rwlo = Signal("m_rwlo", 1)
        m_rwhi, m_x1 = Signal("m_rwhi", 1), Signal("m_x1", 1)
        m_kk = Signal("m_kk", 1)
        m_sk = Signal("m_sk")
        m_skhi = Signal("m_skhi")
        m_sklo = Signal("m_sklo", 2)
        m_val = Signal("m_val", 2)
        m_u = Signal("m_u", 1)
        m_utp = Signal("m_utp", 1)
        m_x2 = Signal("m_x2", 1)
        m_acc = Signal("m_acc")
        w_ld, w_big, w_sum, w_pow, w_scl = D("w_ld"), Signal("w_big"), Signal("w_sum"), Signal("w_pow"), Signal("w_scl")
        w_inv = Signal("w_inv", 2)
        w_hi, w_lo, w_st = Signal("w_hi"), Signal("w_lo", 1), D("w_st", 2)
        e_w = [D(f"e_w{e}") for e in range(E)]
        e_idx = Signal("e_idx")
        e_g = [D(f"e_g{u}") for u in range(2)]
        e_xtp = Signal("e_xtp", 2)
        e_xthi, e_xtlo = Signal("e_xthi"), Signal("e_xtlo", 1)
        e_up = Signal("e_up", 2)
        e_sa = Signal("e_sa")
        e_h = Signal("e_h", 2)
        e_max, e_inv, e_hhi, e_hlo = Signal("e_max"), Signal("e_inv", 2), Signal("e_hhi"), Signal("e_hlo", 2)
        e_htp = Signal("e_htp", 2)
        e_hthi, e_htlo = Signal("e_hthi", 1), Signal("e_htlo", 1)
        e_dn = Signal("e_dn", 2)
        e_y = Signal("e_y", 2)
        e_yst = [D(f"e_yst{u}", 1) for u in range(2)]
        c_idx = Signal("c_idx")
        c_g = [D(f"c_g{u}") for u in range(2)]
        c_ld = [D(f"c_ld{u}") for u in range(2)]
        c_half, c_sum = Signal("c_half", 2), Signal("c_sum")
        c_st = [D(f"c_st{u}", 1) for u in range(2)]

        def credit(eng, *signals):
            for s in signals:
                eng.sem_inc(s.sem, s.credit * s.step)

        def tile_after(s, u, n):
            return s + (u + n) // 2, (u + n) % 2

        def tiles(eng, step):
            step(0, 0, True)
            with eng.Fori(0, (NT - 3) // 2) as s:
                step(s, 1, True)
                step(s + 1, 0, True)
            step((NT - 3) // 2, 1, False)
            step((NT - 1) // 2, 0, False)

        def alone(eng):
            eng.sem_inc(passed.sem, 1)

        CH = EW
        chunks = [(a, min(CH, WALL - a)) for a in range(0, WALL, CH)]
        stage_flat = stage[:, :, :].rearrange("p a b -> p (a b)")

        m1, m2 = rt("m1", [P, NJ]), rt("m2", [P, NJ])
        eq, iv, mx = rt("eq", [P, NJ, E]), rt("iv", [P, NJ, E]), rt("mx", [P, NJ])
        oh = [rt("oh0", [P, NJ, E]), rt("oh1", [P, NJ, E])]
        l2 = rt("l2", [P, NJ, E])
        labs, fac, df, keep = (rt(n, [P, NJ, E]) for n in ("labs", "fac", "df", "keep"))
        dfk = [rt(f"df{k}", [P, NJ, E]) for k in range(TOPK)]
        exk = [rt(f"ex{k}", [P, NJ, E]) for k in range(TOPK)]
        den = rt("den", [P, NJ])
        cc, tote, scan, pos, tmp = (rt(n, [P, NJ * E]) for n in ("cc", "tote", "scan", "pos", "tmp"))
        cnt, padf, pinc, dlt = (rt(n, [P, E]) for n in ("cnt", "padf", "pinc", "dlt"))
        cnti = rt("cnti", [P, E], I32)
        slotf = rt("slotf", [P, TOPK * NJ])
        hii = rt("hii", [P, TOPK * NJ], I32)
        hif, lof = rt("hif", [P, TOPK * NJ]), rt("lof", [P, TOPK * NJ])
        ohlo = [rt(f"ohlo{k}", [P, P]) for k in range(2)]
        ohhi = [rt(f"ohhi{k}", [P, NT]) for k in range(2)]
        assert at <= nc.sbuf_top

        block = ctx.enter_context(nc.Block())


        @block.sync
        def _(sp):
            credit(sp, n_st[0], n_st[1], w_st, e_yst[0], e_yst[1], c_st[0], c_st[1])
            sp.dma_start(xx[0][:], block_rows(x, 0)).then_inc(*n_ld[0].one)
            sp.dma_start(vec[:], vecs).then_inc(*const_ld.one)
            sp.dma_start(gw[:], gate).then_inc(*const_ld.one)
            sp.dma_start(xx[1][:], block_rows(x, 1)).then_inc(*n_ld[1].one)

            def norm_io(s, u, last):
                g = 2 * s + u
                sp.wait_ge(*n_xn.at(g + 1))
                alone(sp)
                sp.dma_start(block_rows(xn_d, g), xn[u][:]).then_inc(*n_st[u].one)
                if not last:
                    sp.dma_start(xx[u][:], block_rows(x, g + 2)).then_inc(*n_ld[u].one)

            with sp.Fori(0, NB // 2 - 1) as s:
                norm_io(s, 0, False)
                norm_io(s, 1, False)
            norm_io(NB // 2 - 1, 0, True)
            norm_io(NB // 2 - 1, 1, True)

            for i, (a, n) in enumerate(chunks):
                if i > 0:
                    sp.wait_ge(*wst_lo.at(i))
                sp.dma_start(stage_flat[:, 0:n], wmix[:, a:a + n]).then_inc(*wst_ld.one)
            for u in range(2):
                sp.wait_ge(*n_st[u].at(NB // 2))
                sp.wait_ge(*n_tp.at(NB))
                sp.dma_start(xn[u][:], block_rows(xn_d, u)).then_inc(*m_ldn[u].one)
                sp.dma_start(xx[u][:], block_rows(x, u)).then_inc(*m_ldx[u].one)
            sp.wait_ge(*wst_lo.at(len(chunks)))

            def mix_io(s, u, last):
                b = 2 * s + u
                sp.wait_ge(*w_lo.at(b))
                alone(sp)
                sp.dma_start(stage_flat, wexp[bass.ds(b * P, P), :]).then_inc(*w_ld.one)
                sp.wait_ge(*w_lo.at(b + 1))
                alone(sp)
                sp.dma_start(ehi_d[bass.ds(b * P, P), :],
                             ehi[:, :, :].rearrange("p a b -> p (a b)")).then_inc(*w_st.one)
                sp.dma_start(elo_d[bass.ds(b * P, P), :],
                             elo[:, :, :].rearrange("p a b -> p (a b)")).then_inc(*w_st.one)
                sp.wait_ge(*m_acc.at(b + 1))
                alone(sp)
                sp.dma_start(block_rows(acc_d, b), xx[u][:]).then_inc(*m_st[u].one)
                if not last:
                    sp.dma_start(xn[u][:], block_rows(xn_d, b + 2)).then_inc(*m_ldn[u].one)
                    sp.wait_ge(*m_st[u].at(s + 1))
                    alone(sp)
                    sp.dma_start(xx[u][:], block_rows(x, b + 2)).then_inc(*m_ldx[u].one)

            with sp.Fori(0, NB // 2 - 1) as s:
                mix_io(s, 0, False)
                mix_io(s, 1, False)
            mix_io(NB // 2 - 1, 0, True)
            mix_io(NB // 2 - 1, 1, True)
            for u in range(2):
                sp.wait_ge(*m_st[u].at(NB // 2))
            sp.wait_ge(*w_st.at(2 * E))
            sp.wait_ge(*m_utp.at(NB))
            for e in range(E):
                sp.dma_start(ewh[:, e * EW:(e + 1) * EW], ehi_d[e * P:(e + 1) * P, :]).then_inc(*e_w[e].one)
                sp.dma_start(ewl[:, e * EW:(e + 1) * EW], elo_d[e * P:(e + 1) * P, :]).then_inc(*e_w[e].one)

            def expert_io(i, u):
                sp.wait_ge(*e_y.at(i + 1))
                alone(sp)
                sp.dma_start(y_d[bass.ds(i * P, P), :], yb[u][:]).then_inc(*e_yst[u].one)

            with sp.Fori(0, NT // 2) as s:
                expert_io(2 * s, 0)
                expert_io(2 * s + 1, 1)
            expert_io(NT - 1, 0)
            for u in range(2):
                sp.dma_start(ac[u][:], acc_d[u * P:(u + 1) * P, :]).then_inc(*c_ld[u].one)

            def combine_io(s, u, last):
                j = 2 * s + u
                sp.wait_ge(*c_sum.at(j + 1))
                alone(sp)
                sp.dma_start(out[bass.ds(j * P, P), :], y1[u][:]).then_inc(*c_st[u].one)
                if not last:
                    sp.dma_start(ac[u][:], acc_d[bass.ds((j + 2) * P, P), :]).then_inc(*c_ld[u].one)

            with sp.Fori(0, NJ // 2 - 1) as s:
                combine_io(s, 0, False)
                combine_io(s, 1, False)
            combine_io(NJ // 2 - 1, 0, True)
            combine_io(NJ // 2 - 1, 1, True)
            for u in range(2):
                sp.wait_ge(*c_st[u].at(NJ // 2))

        @block.gpsimd
        def _(pool):
            credit(pool, m_wkv)
            n_const = 0
            for t, v in ((halfneg[:], -0.5), (id32[:], 0.0), (id16[:], 0.0), (before[:], 0.0), (ones[:], 1.0),
                         (ht[0][:, :, 0:1], 0.0), (h2t[0][:, :, 0:1], 0.0)):
                pool.memset(t, v).then_inc(*const_ok.one)
                n_const += 1
            for t, pattern, base, by in ((lane, [[1, P]], 0, 0), (tokid, [[P, NJ]], 0, 1),
                                         (tile0, [[P, NT]], 0, 0), (down, [[0, NJ], [-1, E]], E, 0)):
                pool.iota(t[:], pattern=pattern, base=base, channel_multiplier=by,
                          allow_small_or_imprecise_dtypes=True).then_inc(*const_ok.one)
                n_const += 1
            pool.wait_ge(*const_ok.at(n_const))
            for m in (id32, id16):
                pool.affine_select(out=m[:], in_=m[:], compare_op=ALU.not_equal, fill=1.0, base=0,
                                   pattern=[[-1, P]], channel_multiplier=1).then_inc(*const_ok.one)
            pool.affine_select(out=before[:], in_=before[:], compare_op=ALU.is_ge, fill=1.0, base=0,
                               pattern=[[-1, P]], channel_multiplier=1).then_inc(*const_ok.one)
            assert n_const + 3 == N_CONST

            def rstd_of(var, eps, done, n):
                pool.wait_ge(*var.at(n))
                alone(pool)
                pool.tensor_scalar(rstd[:], mv[:, :, 1:2].rearrange("p a b -> p (a b)"), EPS, None,
                                   ALU.add).then_inc(*eps.one)
                pool.wait_ge(*eps.at(n))
                pool.tensor_tensor(rstd[:], rstd[:], halfneg[:], ALU.pow).then_inc(*done.one)

            with pool.Fori(0, NB) as g:
                rstd_of(n_mv, n_eps, n_rstd, g + 1)

            def shifted(t, u, n, mixes):
                pool.wait_ge(*m_ht.at(n))
                pool.wait_ge(*m_mixf.at(mixes))
                pool.tensor_tensor(dif[:], t[u][:, :, 1:BT + 1], t[u][:, :, 0:BT],
                                   ALU.subtract).then_inc(*m_dif.one)

            def mix_pool(s, u):
                b = 2 * s + u
                rstd_of(m_mv, m_eps, m_rstd, 2 * b + 1)
                shifted(ht, u, 2 * b + 1, 5 * b)
                pool.wait_ge(*m_av.at(b + 1))
                pool.tensor_tensor(av[:], av[:], rb[:], ALU.mult).then_inc(*m_wkv.one)
                rstd_of(m_mv, m_eps, m_rstd, 2 * b + 2)
                shifted(h2t, u, 2 * b + 2, 5 * b + 3)
                pool.wait_ge(*m_ldx[u].at(s + 1))
                pool.wait_ge(*m_x2.at(b + 1))
                pool.tensor_tensor(xx[u][:], xx[u][:], xn[u][:], ALU.add).then_inc(*m_acc.one)

            with pool.Fori(0, NB // 2) as s:
                mix_pool(s, 0)
                mix_pool(s, 1)
            pool.wait_ge(*r_ready.at(1))

            def gather_slots(s, u):
                i = 2 * s + u
                pool.wait_ge(*e_xtp.at(i - 1))
                alone(pool)
                pool.tensor_copy(gidx[u][:], slot_tok[:, bass.ds(i, 1)]).then_inc(*e_idx.one)
                pool.wait_ge(*e_idx.at(i + 1))
                alone(pool)
                pool.indirect_dma_start(out=xg[u][:], out_offset=None, in_=xn_d,
                                        in_offset=bass.IndirectOffsetOnAxis(ap=gidx[u][:].bitcast(U32), axis=0)
                                        ).then_inc(*e_g[u].one)

            with pool.Fori(0, NT // 2) as s:
                gather_slots(s, 0)
                gather_slots(s, 1)
            gather_slots(NT // 2, 0)

            pool.wait_ge(*e_yst[0].at(NT // 2 + 1))
            pool.wait_ge(*e_yst[1].at(NT // 2))
            alone(pool)

            def gather_rows(s, u):
                j = 2 * s + u
                pool.wait_ge(*c_half.at(j - 1))
                pool.wait_ge(*c_st[u].at(s))
                alone(pool)
                for k in range(TOPK):
                    pool.tensor_copy(cidx[u][:, k:k + 1], slot[:, k, bass.ds(j, 1)]).then_inc(*c_idx.one)
                pool.wait_ge(*c_idx.at(TOPK * (j + 1)))
                alone(pool)
                for k, y in enumerate((y1, y2)):
                    pool.indirect_dma_start(
                        out=y[u][:], out_offset=None, in_=y_d,
                        in_offset=bass.IndirectOffsetOnAxis(ap=cidx[u][:, k:k + 1].bitcast(U32), axis=0)
                    ).then_inc(*c_g[u].one)

            with pool.Fori(0, NJ // 2) as s:
                gather_rows(s, 0)
                gather_rows(s, 1)

        @block.scalar
        def _(act):
            credit(act, n_xt, n_logit, m_ht, m_mixhi, m_rwhi, e_hthi, e_y)

            def norm_act(s, u):
                g = 2 * s + u
                xt = (e2, rb)[u]
                act.wait_ge(*n_tp.at(g + 1))
                act.wait_ge(*n_lg.at(g - 1))
                act.activation(xt[:], ps[:, 2 * u:2 * u + 2, :], ACT.Copy).then_inc(*n_xt.one)
                act.wait_ge(*n_lg.at(g + 1))
                act.activation(logit[:, bass.ds(g * BJ, BJ), :],
                               ps[:, 4 + u, 0:BJ * E].rearrange("p (a b) -> p a b", a=BJ),
                               ACT.Copy).then_inc(*n_logit.one)

            with act.Fori(0, NB // 2) as s:
                norm_act(s, 0)
                norm_act(s, 1)

            for k in range(TOPK):
                act.wait_ge(*r_dve.at(R_EXP[k]))
                act.activation(exk[k][:], dfk[k][:], ACT.Exp, scale=-1.0).then_inc(*r_act.one)
            for i, (a, n) in enumerate(chunks):
                act.wait_ge(*wst_ld.at(i + 1))
                act.activation(whi[:, a:a + n], stage_flat[:, 0:n], ACT.Copy).then_inc(*wst_hi.one)

            def turned(t, n, u, bank, g, bb):
                act.wait_ge(*m_tp.at(n))
                for c in range(HC):
                    last = act.activation(t[u][:, c, 1:BT + 1], ps[:, bank + c, :], ACT.Identity,
                                          scale=vec[:, c, g:g + 1], bias=vec[:, c, bb:bb + 1])
                if u == 1:
                    last = act.activation(t[1][:, :, 0:1], t[0][:, :, BT:BT + 1], ACT.Copy)
                last.then_inc(*m_ht.one)

            def high(m, b, u, dst):
                act.wait_ge(*m_mixf.at(5 * b + m + 1))
                act.activation(dst[:], mixf[(u + m) % 2][:], ACT.Copy).then_inc(*m_mixhi.one)

            def mix_act(s, u):
                b = 2 * s + u
                act.wait_ge(*w_scl.at(b + 1))
                act.wait_ge(*w_st.at(2 * b))
                for k in range(3):
                    last = act.activation(ehi[:, k, :], stage[:, k, :], ACT.Copy, scale=scl[:, k:k + 1])
                last.then_inc(*w_hi.one)
                turned(ht, 2 * b + 1, u, 2, LG1, LB1)
                act.wait_ge(*m_r.at(b))
                high(0, b, u, fhi[0])
                act.wait_ge(*m_wo.at(b))
                high(1, b, u, fhi[1])
                act.wait_ge(*m_k.at(b + 1))
                high(2, b, u, fhi[0])
                act.wait_ge(*m_delta.at(b + 1))
                act.wait_ge(*m_wkv.at(b))
                act.activation(rb[:], e2[:], ACT.Exp, scale=-1.0)
                act.activation(e2[:], e2[:], ACT.Exp).then_inc(*m_exp.one)
                act.wait_ge(*m_r.at(b + 1))
                act.activation(tr[:], ps[:, 4:6, :], ACT.Tanh, scale=0.5).then_inc(*m_tr.one)
                act.wait_ge(*m_rw.at(b + 1))
                act.activation(fhi[1][:], av[:], ACT.Copy).then_inc(*m_rwhi.one)
                turned(h2t, 2 * b + 2, u, 4, LG2, LB2)
                act.wait_ge(*m_kk.at(KQ * b))
                high(3, b, u, chi[0])
                act.wait_ge(*m_cr.at(b))
                high(4, b, u, chi[1])
                act.wait_ge(*m_cr.at(b + 1))
                act.activation(tc[:], ps[:, 6:8, :], ACT.Tanh, scale=0.5).then_inc(*m_tc.one)
                for q in range(KQ):
                    n = KQ * b + q
                    act.wait_ge(*m_kk.at(n + 1))
                    act.wait_ge(*m_sklo.at(n - 1))
                    act.activation(skf[q % 2][:], ps[:, 6 + q % 2, :], ACT.Silu).then_inc(*m_sk.one)
                    act.wait_ge(*m_sk.at(n + 1))
                    act.wait_ge(*m_val.at(n - 1))
                    act.activation(skhi[q % 2][:], skf[q % 2][:], ACT.Copy).then_inc(*m_skhi.one)

            with act.Fori(0, NB // 2) as s:
                mix_act(s, 0)
                mix_act(s, 1)

            def x_act(s, u):
                i = 2 * s + u
                act.wait_ge(*e_xtp.at(i + 1))
                act.wait_ge(*e_up.at(i - 1))
                act.activation(xthi[u][:], ps[:, 0, 0:H], ACT.Copy, scale=XS).then_inc(*e_xthi.one)

            def silu_act(s, u):
                i = 2 * s + u
                act.wait_ge(*e_up.at(i + 1))
                act.wait_ge(*e_h.at(i - 1))
                act.activation(sa[u][:], ps[:, 1 + 2 * u, :], ACT.Silu,
                               scale=unx[:, bass.ds(i, 1)]).then_inc(*e_sa.one)

            def y_act(s, u):
                i = 2 * s + u
                act.wait_ge(*e_dn.at(i + 1))
                act.wait_ge(*e_inv.at(i + 1))
                act.wait_ge(*e_yst[u].at(s))
                act.activation(yb[u][:], ps[:, 7, 0:H], ACT.Copy, scale=yscl[u][:]).then_inc(*e_y.one)

            def tile_act(s, u, inner, before=True):
                i = 2 * s + u
                silu_act(s, u)
                if before:
                    y_act(*tile_after(s, u, -1))
                if inner:
                    x_act(*tile_after(s, u, 2))
                act.wait_ge(*e_htp.at(i + 1))
                act.wait_ge(*e_dn.at(i - 1))
                act.activation(hthi[u][:], ps[:, 5, :].bitcast(F16)[:, 0:F], ACT.Copy).then_inc(*e_hthi.one)

            act.wait_ge(*r_ready.at(1))
            x_act(0, 0)
            x_act(0, 1)
            tiles(act, lambda s, u, inner: tile_act(s, u, inner, not (u == 0 and isinstance(s, int) and s == 0)))
            y_act((NT - 1) // 2, 0)

        @block.vector
        def _(dve):
            credit(dve, n_xn, m_hn, m_mixlo, m_av, m_rwlo, w_inv, e_inv, e_hlo, m_mixf, m_u, m_x1, m_x2, m_sklo, w_lo, e_h, e_xtlo, e_htlo, c_half)
            dve.wait_ge(*const_ok.at(N_CONST))
            dve.wait_ge(*const_ld.at(2))
            steps = [0]

            def done(ins):
                steps[0] += 1
                ins.then_inc(*r_dve.one)
                dve.wait_ge(*r_dve.at(steps[0]))

            def layer_norm(src, dst, n, s_stats, s_mv, s_rstd, s_dst):
                dve.wait_ge(*s_dst.at(n - 1))
                for j in range(BJ):
                    last = dve.bn_stats(stats[:, j, :], src[:, j, :])
                last.then_inc(*s_stats.one)
                dve.wait_ge(*s_stats.at(n))
                alone(dve)
                for j in range(BJ):
                    last = dve.bn_aggr(mv[:, j, :], stats[:, j, :])
                last.then_inc(*s_mv.one)
                dve.wait_ge(*s_rstd.at(n))
                for j in range(BJ):
                    last = dve.tensor_scalar(dst[:, j, :], src[:, j, :], mv[:, j, 0:1], rstd[:, j:j + 1],
                                             ALU.subtract, ALU.mult)
                last.then_inc(*s_dst.one)

            def norm_dve(s, u):
                g = 2 * s + u
                dve.wait_ge(*n_ld[u].at(s + 1))
                dve.wait_ge(*n_st[u].at(s))
                dve.wait_ge(*n_tp.at(g - 1))
                layer_norm(xx[u], xn[u], g + 1, n_stats, n_mv, n_rstd, n_xn)

            with dve.Fori(0, NB // 2) as s:
                norm_dve(s, 0)
                norm_dve(s, 1)

            done(dve.tensor_scalar(tfp[:], vec[:, :, TF:TF + 1].rearrange("p a b -> p (a b)"), PP0, None, ALU.add))
            dve.wait_ge(*n_logit.at(NB))

            def wide(t):
                return t[:, :].unsqueeze(2).to_broadcast([P, NJ, E])

            def flat(t):
                return t[:, :, :].rearrange("p a b -> p (a b)")

            done(dve.scalar_tensor_tensor(flat(labs), flat(logit), -1.0, flat(logit), ALU.mult, ALU.max))
            for k, (top, of) in enumerate(((m1, logit), (m2, l2))):
                done(dve.tensor_reduce(top[:], of[:], AX.X, ALU.max))
                done(dve.tensor_tensor(eq[:], of[:], wide(top), ALU.is_equal))
                done(dve.tensor_tensor(iv[:], eq[:], down[:], ALU.mult))
                done(dve.tensor_reduce(mx[:], iv[:], AX.X, ALU.max))
                done(dve.tensor_tensor(oh[k][:], iv[:], wide(mx), ALU.is_equal))
                done(dve.tensor_tensor(fac[:], labs[:], wide(top), ALU.max))
                done(dve.tensor_tensor(df[:], wide(top), logit[:], ALU.subtract))
                done(dve.scalar_tensor_tensor(flat(keep), flat(fac), JITTER, flat(df), ALU.mult, ALU.is_ge))
                if k == 0:
                    done(dve.scalar_tensor_tensor(flat(l2), flat(oh[0]), -3e38, flat(logit), ALU.mult, ALU.add))
                done(dve.tensor_tensor(dfk[k][:], wide(top), of[:], ALU.subtract))
                assert steps[0] == R_EXP[k], steps
                dve.wait_ge(*r_act.at(k + 1))
                done(dve.tensor_tensor(exk[k][:], exk[k][:], keep[:], ALU.mult))
                done(dve.tensor_reduce(den[:], exk[k][:], AX.X, ALU.add))
                done(dve.reciprocal(gain[:, k, :], den[:]))
            done(dve.tensor_tensor(cc[:], flat(oh[0]), flat(oh[1]), ALU.add))
            assert steps[0] == R_PICKS, steps
            dve.wait_ge(*r_pe.at(1))
            by_e = lambda t: t.rearrange("p (j e) -> p e j", e=E)
            done(dve.tensor_copy(tote[:, :].rearrange("p (e j) -> p e j", e=E), by_e(ps[:, 7, 0:NJ * E])))
            done(dve.tensor_tensor_scan(scan[:], ones[:], tote[:], 0.0, ALU.mult, ALU.add))
            done(dve.tensor_tensor(pos[:], scan[:], tote[:], ALU.subtract))
            s_ej, p_ej = (t[:, :].rearrange("p (e j) -> p e j", e=E) for t in (scan, pos))
            last_of = s_ej[:, :, NJ - 1:NJ].rearrange("p a b -> p (a b)")
            first_of = p_ej[:, :, 0:1].rearrange("p a b -> p (a b)")
            done(dve.tensor_tensor(cnt[:], last_of, first_of, ALU.subtract))
            done(dve.tensor_scalar(cnti[:], cnt[:], float(P - 1), None, ALU.add))
            done(dve.tensor_scalar(cnti[:], cnti[:], 7, 7, ALU.logical_shift_right, ALU.logical_shift_left))
            done(dve.tensor_copy(padf[:], cnti[:]))
            done(dve.tensor_tensor_scan(pinc[:], ones[:, 0:E], padf[:], 0.0, ALU.mult, ALU.add))
            done(dve.tensor_tensor(pbx[:], pinc[:], padf[:], ALU.subtract))
            done(dve.tensor_tensor(dlt[:], pbx[:], first_of, ALU.subtract))
            done(dve.tensor_tensor(p_ej, p_ej, dlt[:, :].unsqueeze(2).to_broadcast([P, E, NJ]), ALU.add))
            done(dve.tensor_tensor(tmp[:, :].rearrange("p (j e) -> p j e", e=E),
                                   ps[:, 6, 0:NJ * E].rearrange("p (j e) -> p j e", e=E),
                                   pos[:, :].rearrange("p (e j) -> p j e", e=E), ALU.add))
            for k in range(TOPK):
                done(dve.tensor_tensor(cc[:], tmp[:], flat(oh[k]), ALU.mult))
                done(dve.tensor_reduce(slotf[:, k * NJ:(k + 1) * NJ],
                                       cc[:, :].rearrange("p (j e) -> p j e", e=E), AX.X, ALU.add))
            done(dve.tensor_copy(slot[:, :, :].rearrange("p a b -> p (a b)"), slotf[:]))
            done(dve.tensor_scalar(hii[:], slot[:, :, :].rearrange("p a b -> p (a b)"), 7, None,
                                   ALU.logical_shift_right))
            done(dve.tensor_copy(hif[:], hii[:]))
            done(dve.scalar_tensor_tensor(lof[:], hif[:], -float(P), slotf[:], ALU.mult, ALU.add))
            done(dve.tensor_scalar(tile_exp[:], tile0[:], pbx[:, 1:2], None, ALU.is_ge))
            for e in range(2, E):
                done(dve.scalar_tensor_tensor(tile_exp[:], tile0[:], pbx[:, e:e + 1], tile_exp[:],
                                              ALU.is_ge, ALU.add))
            done(dve.tensor_scalar(tile_off[:], tile_exp[:], float(EW), None, ALU.mult))

            def hot(j):
                dve.wait_ge(*r_perm.at(j))
                for k in range(TOPK):
                    dve.tensor_scalar(ohlo[k][:], lane[:], lof[:, bass.ds(k * NJ + j, 1)], None, ALU.is_equal)
                    last = dve.tensor_scalar(ohhi[k][:], lane[:, 0:NT], hif[:, bass.ds(k * NJ + j, 1)],
                                             tokid[:, bass.ds(j, 1)], ALU.is_equal, ALU.mult)
                last.then_inc(*r_hot.one)

            with dve.Fori(0, NJ) as j:
                hot(j)
            dve.wait_ge(*r_perm.at(NJ))
            done(dve.tensor_copy(slot_tok[:], ps[:, 7, 0:NT]))

            for i, (a, n) in enumerate(chunks):
                dve.wait_ge(*wst_hi.at(i + 1))
                dve.tensor_tensor(wlo[:, a:a + n], stage_flat[:, 0:n], whi[:, a:a + n].bitcast(F32),
                                  ALU.subtract).then_inc(*wst_lo.one)

            def mixed(m, b, u, t, n_dif):
                dve.wait_ge(*m_dif.at(n_dif))
                dve.wait_ge(*m_mixhi.at(5 * b + m - 1))
                dve.wait_ge(*m_mixlo.at(5 * b + m - 1))
                for c in range(HC):
                    last = dve.scalar_tensor_tensor(mixf[(u + m) % 2][:, c, :], dif[:, c, :],
                                                    vec[:, c, MK + m:MK + m + 1], t[u][:, c, 0:BT],
                                                    ALU.mult, ALU.add)
                last.then_inc(*m_mixf.one)

            def low(m, b, u, dst, hi):
                dve.wait_ge(*m_mixhi.at(5 * b + m + 1))
                dve.tensor_tensor(dst[:], mixf[(u + m) % 2][:], hi[:].bitcast(F32),
                                  ALU.subtract).then_inc(*m_mixlo.one)

            def mix_dve(s, u):
                b = 2 * s + u
                dve.wait_ge(*w_ld.at(b + 1))
                dve.tensor_reduce(big[:], stage[:], AX.X, ALU.max, apply_absolute_value=True).then_inc(*w_big.one)
                dve.wait_ge(*w_sum.at(b + 1))
                dve.tensor_scalar(pw2[:], ps[:, 0, 0:3], 1e-30, None, ALU.max).then_inc(*w_pow.one)
                dve.wait_ge(*w_pow.at(2 * b + 1))
                dve.tensor_scalar(pw2[:].bitcast(I32), pw2[:].bitcast(I32), 0x7F800000, None,
                                  ALU.bitwise_and).then_inc(*w_pow.one)
                dve.wait_ge(*w_pow.at(2 * b + 2))
                dve.wait_ge(*w_inv.at(2 * b))
                dve.tensor_scalar(pwi[:], pw2[:], 2.0 ** -14, None, ALU.mult).then_inc(*w_inv.one)
                dve.wait_ge(*w_inv.at(2 * b + 1))
                dve.reciprocal(scl[:], pwi[:]).then_inc(*w_scl.one)
                dve.tensor_copy(unscale[:, bass.ds(b, 1), :].rearrange("p a b -> p (a b)"), pwi[:]
                                ).then_inc(*w_inv.one)
                dve.wait_ge(*w_hi.at(b + 1))
                for k in range(3):
                    last = dve.scalar_tensor_tensor(elo[:, k, :], stage[:, k, :], scl[:, k:k + 1],
                                                    ehi[:, k, :], ALU.mult, ALU.subtract)
                last.then_inc(*w_lo.one)

                dve.wait_ge(*m_ldn[u].at(s + 1))
                dve.wait_ge(*m_tp.at(2 * b))
                layer_norm(xn[u], hn, 2 * b + 1, m_stats, m_mv, m_rstd, m_hn)
                mixed(0, b, u, ht, 2 * b + 1)
                mixed(1, b, u, ht, 2 * b + 1)
                low(0, b, u, flo[0], fhi[0])
                mixed(2, b, u, ht, 2 * b + 1)
                low(1, b, u, flo[1], fhi[1])
                low(2, b, u, flo[0], fhi[0])
                dve.wait_ge(*m_k.at(b + 1))
                dve.wait_ge(*m_av.at(b))
                for c in range(HC):
                    last = dve.tensor_scalar(e2[:, c, :], ps[:, 4 + c, :], tfp[:, c:c + 1], 0.0, ALU.add, ALU.min)
                last.then_inc(*m_delta.one)
                dve.wait_ge(*m_exp.at(b + 1))
                dve.wait_ge(*m_v.at(b + 1))
                dve.wait_ge(*m_rwhi.at(b))
                dve.wait_ge(*m_rwlo.at(b))
                dve.scalar_tensor_tensor(av[:], ps[:, 2:4, :], 0.5, e2[:], ALU.mult, ALU.mult).then_inc(*m_av.one)
                dve.wait_ge(*m_wkv.at(b + 1))
                dve.wait_ge(*m_tr.at(b + 1))
                dve.scalar_tensor_tensor(av[:], tr[:], 1.0, av[:], ALU.add, ALU.mult).then_inc(*m_rw.one)
                dve.wait_ge(*m_rwhi.at(b + 1))
                dve.tensor_tensor(flo[1][:], av[:], fhi[1][:].bitcast(F32), ALU.subtract).then_inc(*m_rwlo.one)
                dve.wait_ge(*m_wo.at(b + 1))
                dve.tensor_tensor(xn[u][:], rows(2), xn[u][:], ALU.add).then_inc(*m_x1.one)

                dve.wait_ge(*m_x1.at(b + 1))
                dve.wait_ge(*m_tp.at(2 * b + 1))
                layer_norm(xn[u], hn, 2 * b + 2, m_stats, m_mv, m_rstd, m_hn)
                mixed(3, b, u, h2t, 2 * b + 2)
                mixed(4, b, u, h2t, 2 * b + 2)
                low(3, b, u, clo[0], chi[0])
                low(4, b, u, clo[1], chi[1])
                for q in range(KQ):
                    n = KQ * b + q
                    dve.wait_ge(*m_skhi.at(n + 1))
                    dve.wait_ge(*m_val.at(n - 1))
                    dve.tensor_tensor(sklo[q % 2][:], skf[q % 2][:], skhi[q % 2][:].bitcast(F32),
                                      ALU.subtract).then_inc(*m_sklo.one)
                dve.wait_ge(*m_tc.at(b + 1))
                dve.wait_ge(*m_val.at(KQ * (b + 1)))
                dve.wait_ge(*m_utp.at(b))
                dve.scalar_tensor_tensor(uu[:], tc[:], 1.0, ps[:, 0:2, :], ALU.add, ALU.mult).then_inc(*m_u.one)
                dve.wait_ge(*m_utp.at(b + 1))
                dve.scalar_tensor_tensor(xn[u][:], rows(6), 0.5, xn[u][:], ALU.mult, ALU.add).then_inc(*m_x2.one)

            def rows(bank):
                return ps[:, bank:bank + 2, :].rearrange("p b (j n) -> p (b j) n", n=H)

            with dve.Fori(0, NB // 2) as s:
                mix_dve(s, 0)
                mix_dve(s, 1)

            dve.memset(unx[:], 0.0)
            done(dve.memset(uny[:], 0.0))
            done(dve.tensor_tensor(un32[:], unscale[:, :, 1:2].rearrange("p a b -> p (a b)"),
                                   unscale[:, :, 2:3].rearrange("p a b -> p (a b)"), ALU.mult))
            for e in range(E):
                for dst, by in ((unx, unscale[:, e, 0:1]), (uny, un32[:, e:e + 1])):
                    done(dve.tensor_scalar(picked[:], tile_exp[:], float(e), by, ALU.is_equal, ALU.mult))
                    done(dve.scalar_tensor_tensor(dst[:], picked[:], 1.0 / XS, dst[:], ALU.mult, ALU.add))
            dve.memset(big[:], 0.0).then_inc(*r_ready.one)

            def x_dve(s, u):
                i = 2 * s + u
                dve.wait_ge(*e_xthi.at(i + 1))
                dve.wait_ge(*e_up.at(i - 1))
                dve.scalar_tensor_tensor(xtlo[u][:], ps[:, 0, 0:H], XS, xthi[u][:], ALU.mult,
                                         ALU.subtract).then_inc(*e_xtlo.one)

            def tile_dve(s, u, inner):
                i = 2 * s + u
                dve.wait_ge(*e_sa.at(i + 1))
                dve.wait_ge(*e_hlo.at(i - 1))
                dve.tensor_tensor(hh[u][:], ps[:, 2 + 2 * u, :], sa[u][:], ALU.mult).then_inc(*e_h.one)
                dve.wait_ge(*e_h.at(i + 1))
                dve.wait_ge(*e_y.at(i - 1))
                dve.wait_ge(*e_inv.at(i - 1))
                dve.tensor_reduce(hmax[u][:], hh[u][:], AX.X, ALU.max,
                                  apply_absolute_value=True).then_inc(*e_max.one)
                dve.wait_ge(*e_max.at(2 * i + 1))
                dve.tensor_scalar(hmax[u][:], hmax[u][:], 1e-30, 2.0 ** -14, ALU.max, ALU.mult).then_inc(*e_max.one)
                dve.wait_ge(*e_max.at(2 * i + 2))
                dve.reciprocal(hinv[u][:], hmax[u][:])
                dve.tensor_tensor(yscl[u][:], hmax[u][:], uny[:, bass.ds(i, 1)], ALU.mult).then_inc(*e_inv.one)
                dve.wait_ge(*e_inv.at(i + 1))
                dve.wait_ge(*e_htp.at(i - 1))
                dve.tensor_scalar(hhi[u][:], hh[u][:], hinv[u][:], None, ALU.mult).then_inc(*e_hhi.one)
                dve.wait_ge(*e_hhi.at(i + 1))
                dve.scalar_tensor_tensor(hlo[u][:], hh[u][:], hinv[u][:], hhi[u][:], ALU.mult,
                                         ALU.subtract).then_inc(*e_hlo.one)
                if inner:
                    x_dve(*tile_after(s, u, 2))
                dve.wait_ge(*e_htp.at(i + 1))
                dve.wait_ge(*e_dn.at(i - 1))
                dve.tensor_copy(htlo[u][:], ps[:, 6, :].bitcast(F16)[:, 0:F]).then_inc(*e_htlo.one)

            x_dve(0, 0)
            x_dve(0, 1)
            tiles(dve, tile_dve)

            def combine(s, u):
                j = 2 * s + u
                dve.wait_ge(*c_g[u].at(TOPK * (s + 1)))
                dve.wait_ge(*c_ld[u].at(s + 1))
                dve.scalar_tensor_tensor(ac[u][:], y2[u][:], gain[:, 1, bass.ds(j, 1)], ac[u][:],
                                         ALU.mult, ALU.add).then_inc(*c_half.one)
                dve.wait_ge(*c_half.at(j + 1))
                dve.scalar_tensor_tensor(y1[u][:], y1[u][:], gain[:, 0, bass.ds(j, 1)], ac[u][:],
                                         ALU.mult, ALU.add).then_inc(*c_sum.one)

            with dve.Fori(0, NJ // 2) as s:
                combine(s, 0)
                combine(s, 1)

        @block.tensor
        def _(pe):
            credit(pe, n_tp, n_lg, r_perm, m_tp, m_r, m_wo, m_cr, m_kk, m_val, m_utp, e_xtp, e_up, e_htp, e_dn)
            pe.wait_ge(*const_ok.at(N_CONST))
            pe.wait_ge(*const_ld.at(2))

            def turn(src, bank):
                for c in range(HC):
                    for j in range(BJ):
                        last = pe.transpose(ps[:, bank + c, j * P:(j + 1) * P], src[:, j, c * P:(c + 1) * P],
                                            id32[:])
                return last

            def norm_pe(s, u):
                g = 2 * s + u
                pe.wait_ge(*n_xn.at(g + 1))
                pe.wait_ge(*n_xt.at(g - 1))
                turn(xn[u], 2 * u).then_inc(*n_tp.one)
                pe.wait_ge(*n_xt.at(g + 1))
                pe.wait_ge(*n_logit.at(g - 1))
                xt = (e2, rb)[u]
                for j in range(BJ):
                    for c in range(HC):
                        last = pe.matmul(ps[:, 4 + u, j * E:(j + 1) * E], xt[:, c, j * P:(j + 1) * P],
                                         gw[:, c, :], start=(c == 0), stop=(c == HC - 1))
                last.then_inc(*n_lg.one)

            with pe.Fori(0, NB // 2) as s:
                norm_pe(s, 0)
                norm_pe(s, 1)

            pe.wait_ge(*r_dve.at(R_PICKS))
            pe.matmul(ps[:, 6, 0:NJ * E], before[:], cc[:], start=True, stop=True)
            pe.matmul(ps[:, 7, 0:NJ * E], ones[:, 0:P], cc[:], start=True, stop=True).then_inc(*r_pe.one)

            def permute(j, first, last):
                pe.wait_ge(*r_hot.at(j + 1))
                for k in range(TOPK):
                    mm = pe.matmul(ps[:, 7, 0:NT], ohlo[k][:], ohhi[k][:], start=first and k == 0,
                                   stop=last and k == TOPK - 1)
                mm.then_inc(*r_perm.one)

            permute(0, True, False)
            with pe.Fori(1, NJ - 1) as j:
                permute(j, False, False)
            permute(NJ - 1, False, True)

            pe.wait_ge(*wst_lo.at(len(chunks)))

            def product(bank, w, width, m, hi, lo):
                for c in range(HC):
                    a = w + c * width + m * P
                    for i, (ww, t) in enumerate(((whi, hi), (whi, lo), (wlo, hi))):
                        last = pe.matmul(ps[:, bank, :], ww[:, a:a + P], t[:, c, :],
                                         start=(c == 0 and i == 0), stop=(c == HC - 1 and i == 2))
                return last

            def mix_pe(s, u):
                b = 2 * s + u
                pe.wait_ge(*w_big.at(b + 1))
                pe.wait_ge(*m_u.at(b))
                pe.matmul(ps[:, 0, 0:3], ones[:, 0:P], big[:], start=True, stop=True).then_inc(*w_sum.one)
                pe.wait_ge(*m_hn.at(2 * b + 1))
                pe.wait_ge(*m_x1.at(b))
                turn(hn, 2).then_inc(*m_tp.one)
                pe.wait_ge(*m_ht.at(2 * b))
                pe.wait_ge(*m_mixlo.at(5 * b + 1))
                product(4, WK, H, 0, fhi[0], flo[0])
                product(5, WK, H, 1, fhi[0], flo[0]).then_inc(*m_k.one)
                pe.wait_ge(*m_ht.at(2 * b + 1))
                pe.wait_ge(*m_mixlo.at(5 * b + 2))
                product(2, WV, H, 0, fhi[1], flo[1])
                product(3, WV, H, 1, fhi[1], flo[1]).then_inc(*m_v.one)
                pe.wait_ge(*m_delta.at(b + 1))
                pe.wait_ge(*m_mixlo.at(5 * b + 3))
                product(4, WR, H, 0, fhi[0], flo[0])
                product(5, WR, H, 1, fhi[0], flo[0]).then_inc(*m_r.one)
                pe.wait_ge(*m_av.at(b + 1))
                pe.wait_ge(*m_rwlo.at(b + 1))
                for j in range(BJ):
                    o = ps[:, 2 + j // 2, (j % 2) * H:(j % 2 + 1) * H]
                    for c in range(HC):
                        for i, (t, ww) in enumerate(((fhi[1], whi), (fhi[1], wlo), (flo[1], whi))):
                            last = pe.matmul(o, t[:, c, j * P:(j + 1) * P], ww[:, WO + c * H:WO + (c + 1) * H],
                                             start=(c == 0 and i == 0), stop=(c == HC - 1 and i == 2))
                last.then_inc(*m_wo.one)
                pe.wait_ge(*m_hn.at(2 * b + 2))
                pe.wait_ge(*m_tr.at(b + 1))
                turn(hn, 4).then_inc(*m_tp.one)
                pe.wait_ge(*m_mixlo.at(5 * b + 5))
                pe.wait_ge(*m_x2.at(b))
                product(6, WCR, H, 0, chi[1], clo[1])
                product(7, WCR, H, 1, chi[1], clo[1]).then_inc(*m_cr.one)

                def key(q):
                    if q < 2:
                        pe.wait_ge(*m_tc.at(b + 1))
                    else:
                        pe.wait_ge(*m_sk.at(KQ * b + q - 1))
                    product(6 + q % 2, WKEY, KEY, q, chi[0], clo[0]).then_inc(*m_kk.one)

                def value(q):
                    if q == 0:
                        pe.wait_ge(*w_pow.at(2 * b + 1))
                        pe.wait_ge(*m_u.at(b))
                    pe.wait_ge(*m_sklo.at(KQ * b + q + 1))
                    for m in range(HC):
                        a = WVAL + q * H + m * P
                        for i, (ww, t) in enumerate(((whi, skhi), (whi, sklo), (wlo, skhi))):
                            last = pe.matmul(ps[:, m, :], ww[:, a:a + P], t[q % 2][:],
                                             start=(q == 0 and i == 0), stop=(q == KQ - 1 and i == 2))
                    last.then_inc(*m_val.one)

                key(0)
                for q in range(1, KQ):
                    key(q)
                    value(q - 1)
                value(KQ - 1)
                pe.wait_ge(*m_u.at(b + 1))
                pe.wait_ge(*m_sk.at(KQ * (b + 1)))
                for j in range(BJ):
                    for c in range(HC):
                        a = (j % 2) * H + c * P
                        last = pe.transpose(ps[:, 6 + j // 2, a:a + P], uu[:, c, j * P:(j + 1) * P], id32[:])
                last.then_inc(*m_utp.one)

            with pe.Fori(0, NB // 2) as s:
                mix_pe(s, 0)
                mix_pe(s, 1)

            pe.wait_ge(*r_ready.at(1))
            pe.wait_ge(*m_x2.at(NB))
            for e in range(E):
                pe.wait_ge(*e_w[e].at(2))
            alone(pe)

            def weights_of(s, u):
                return pe.value_load(tile_off[0:1, bass.ds(2 * s + u, 1)], min_val=0, max_val=(E - 1) * EW)

            def turn_slots(s, u):
                i = 2 * s + u
                pe.wait_ge(*e_g[u].at(s + 1))
                pe.wait_ge(*e_xtlo.at(i))
                for c in range(HC):
                    last = pe.transpose(ps[:, 0, c * P:(c + 1) * P], xg[u][:, c * P:(c + 1) * P], id32[:])
                last.then_inc(*e_xtp.one)

            def up(s, u):
                i = 2 * s + u
                off = weights_of(s, u)
                pe.wait_ge(*e_xtlo.at(i + 1))
                pe.wait_ge(*e_h.at(i - 1))
                for c in range(HC):
                    for n, (t, ww) in enumerate(((xthi, ewh), (xthi, ewl), (xtlo, ewh))):
                        for bank, w in ((1 + 2 * u, W1), (2 + 2 * u, W3)):
                            last = pe.matmul(ps[:, bank, :], t[u][:, c * P:(c + 1) * P],
                                             ww[:, bass.ds(off + (w + c * F), F)],
                                             start=(c == 0 and n == 0), stop=(c == HC - 1 and n == 2))
                last.then_inc(*e_up.one)

            def down(s, u):
                i = 2 * s + u
                off = weights_of(s, u)
                pe.wait_ge(*e_hlo.at(i + 1))
                pe.wait_ge(*e_hthi.at(i))
                pe.wait_ge(*e_htlo.at(i))
                for k in range(F // P):
                    for bank, t in ((5, hhi), (6, hlo)):
                        last = pe.transpose(ps[:, bank, :].bitcast(F16)[:, k * P:(k + 1) * P],
                                            t[u][:, k * P:(k + 1) * P], id16[:])
                last.then_inc(*e_htp.one)
                pe.wait_ge(*e_hthi.at(i + 1))
                pe.wait_ge(*e_htlo.at(i + 1))
                pe.wait_ge(*e_y.at(i))
                for k in range(F // P):
                    for n, (t, ww) in enumerate(((hthi, ewh), (hthi, ewl), (htlo, ewh))):
                        last = pe.matmul(ps[:, 7, 0:H], t[u][:, k * P:(k + 1) * P],
                                         ww[:, bass.ds(off + (W2 + k * H), H)],
                                         start=(k == 0 and n == 0), stop=(k == F // P - 1 and n == 2))
                last.then_inc(*e_dn.one)

            def tile_pe(s, u, inner):
                if inner or u == 1:
                    up(*tile_after(s, u, 1))
                if inner:
                    turn_slots(*tile_after(s, u, 2))
                down(s, u)

            turn_slots(0, 0)
            up(0, 0)
            turn_slots(0, 1)
            tiles(pe, tile_pe)


def kernel(**inputs):
    import numpy as np
    import concourse.bacc as bacc
    from concourse.bass_utils import run_bass_kernel_spmd

    def row(name):
        return np.asarray(inputs["L0_attn_" + name])

    def halves(w):
        k, n = w.shape
        return w.reshape(k // P, P, n).transpose(1, 0, 2).reshape(P, -1)

    vecs = np.stack([row(n).reshape(HC, P) for n in
                     ("ln1_g", "ln1_b", "ln2_g", "ln2_b", "tm_first", "tm_mk", "tm_mv", "tm_mr",
                      "cm_mk", "cm_mr")], axis=-1).transpose(1, 0, 2)
    gate = np.asarray(inputs["L0_ffn_gate_w"]).T.reshape(HC, P, E).transpose(1, 0, 2)
    wmix = np.concatenate([halves(row(n).T) for n in ("Wk", "Wv", "Wr", "Wo", "Wcr", "Wkey", "Wval")], axis=1)
    w1, w2, w3 = (np.asarray(inputs["L0_ffn_" + n]) for n in ("w1", "w2", "w3"))
    wexp = np.concatenate([np.concatenate([halves(w1[e].T), halves(w3[e].T), halves(w2[e].T)], axis=1)
                           for e in range(E)], axis=0)
    arrays = {"x": row("x").reshape(T, H), "vecs": vecs, "gate": gate, "wmix": wmix, "wexp": wexp}
    arrays = {n: np.ascontiguousarray(a) for n, a in arrays.items()}

    nc = bacc.Bacc("TRN2", target_bir_lowering=False, num_devices=1)
    args = [nc.dram_tensor(n + "_in", a.shape, F32, kind="ExternalInput").ap() for n, a in arrays.items()]
    out = nc.dram_tensor("out_0", (T, H), F32, kind="ExternalOutput").ap()
    build(nc, *args, out)
    r = run_bass_kernel_spmd(nc, [{n + "_in": a for n, a in arrays.items()}], core_ids=[0])
    return np.asarray(r.results[0]["out_0"]).reshape(NSEQ, SEQ, H)
```

```python
from contextlib import ExitStack

import concourse.bass as bass
from concourse import mybir

ALU = mybir.AluOpType
ACT = mybir.ActivationFunctionType
AX = mybir.AxisListType
F32 = mybir.dt.float32
F32R = mybir.dt.float32r
F16 = mybir.dt.float16
I32 = mybir.dt.int32
U32 = mybir.dt.uint32

P = 128
H = 256
HC = H // P
SEQ = 1024
NSEQ = 4
T = SEQ * NSEQ
BT = 512
BJ = BT // P
NB = T // BT
NJ = T // P
E = 8
F = 512
KEY = 4 * H
KQ = KEY // P
TOPK = 2
NT = T * TOPK // P + E - 1
EW = 2 * HC * F + (F // P) * H
W1, W3, W2 = 0, HC * F, 2 * HC * F
EPS = 1e-5
JITTER = 0.02
PP0 = 1e38
XS = 1024.0
WK, WV, WR, WO = 0, HC * H, 2 * HC * H, 3 * HC * H
WCR = 4 * HC * H
WKEY = 5 * HC * H
WVAL = WKEY + HC * KEY
WALL = WVAL + KQ * H
N_CONST = 16
R_EXP = (12, 24)
R_PICKS = 28
LG1, LB1, LG2, LB2, TF, MK, MV, MR, CMK, CMR = range(10)
MIXES = (MK, MV, MR, CMK, CMR)
AT = {MK: 0, MR: 0, MV: 1, CMK: 2, CMR: 2}


def build(nc, x, vecs, gate, wmix, wexp, out):
    ctx = ExitStack()
    with ctx:
        place = [nc.sbuf_base]

        def sb(name, shape, dt, at=None):
            words = 1
            for n in shape[1:]:
                words *= n
            size = words * (2 if dt == F16 else 4)
            start = place[0] if at is None else at
            start = (start + 31) // 32 * 32
            if at is None:
                place[0] = start + size
            assert start + size <= nc.sbuf_top, (name, start + size)
            return nc.alloc_sbuf_tensor_at(name, shape, dt, offset=start), start + size

        def S(name):
            return ctx.enter_context(nc.semaphore(name))

        def tensor(name, shape, dt):
            return sb(name, shape, dt)[0]

        id32 = tensor("id32", [P, P], F32)
        id16 = tensor("id16", [P, P], F16)
        ones = tensor("ones", [P, NJ * E], F32)
        before = tensor("before", [P, P], F32)
        lane = tensor("lane", [P, P], F32)
        tokid = tensor("tokid", [P, NJ], F32)
        tile0 = tensor("tile0", [P, NT], F32)
        down = tensor("down", [P, NJ, E], F32)
        vec = tensor("vec", [P, HC, 10], F32)
        tfp = tensor("tfp", [P, HC], F32)
        gw = tensor("gw", [P, HC, E], F32)
        halfneg = tensor("halfneg", [P, BJ], F32)
        logit = tensor("logit", [P, NJ, E], F32)
        gain = tensor("gain", [P, TOPK, NJ], F32)
        spare = tensor("spare", [P, 1], F32)
        slot_from = tensor("slot_from", [P, NT], I32)
        slot_to = tensor("slot_to", [P, NT], I32)
        slot_gain = tensor("slot_gain", [P, NT], F32)
        yscl = tensor("yscl", [P, NT], F32)
        tile_exp = tensor("tile_exp", [P, NT], F32)
        tile_off = tensor("tile_off", [P, NT], I32)
        unx = tensor("unx", [P, NT], F32)
        uny = tensor("uny", [P, NT], F32)
        unscale = tensor("unscale", [P, E, 3], F32)
        pbx = tensor("pbx", [P, E], F32)
        un32 = tensor("un32", [P, E], F32)
        picked = tensor("picked", [P, NT], F32)
        small0 = place[0]

        xx = [tensor(f"xx{u}", [P, BJ, H], F32) for u in range(2)]
        xn = [tensor(f"xn{u}", [P, BJ, H], F32) for u in range(2)]
        hn = tensor("hn", [P, BJ, H], F32)
        stats = [tensor(f"stats{k}", [P, BJ, 6], F32) for k in range(2)]
        mv = [tensor(f"mv{k}", [P, BJ, 2], F32) for k in range(2)]
        rstd = [tensor(f"rstd{k}", [P, BJ], F32) for k in range(2)]
        ht = [tensor(f"ht{u}", [P, HC, BT + 1], F32) for u in range(2)]
        h2t = [tensor(f"h2t{u}", [P, HC, BT + 1], F32) for u in range(2)]
        dif = tensor("dif", [P, HC, BT], F32)
        fhi = [tensor(f"fhi{u}", [P, HC, BT], F32R) for u in range(2)]
        flo = [tensor(f"flo{u}", [P, HC, BT], F32R) for u in range(2)]
        chi = [tensor(f"chi{u}", [P, HC, BT], F32R) for u in range(2)]
        clo = [tensor(f"clo{u}", [P, HC, BT], F32R) for u in range(2)]
        e2 = tensor("e2", [P, HC, BT], F32)
        rb = tensor("rb", [P, HC, BT], F32)
        at = place[0]
        mixf = [tensor(f"mixf{n}", [P, HC, BT], F32) for n in ("_kr", "_v", "_c")]
        av = tensor("av", [P, HC, BT], F32)
        tc = tensor("tc", [P, HC, BT], F32)
        skf = [tensor(f"skf{u}", [P, BT], F32) for u in range(2)]
        skhi = [tensor(f"skhi{u}", [P, BT], F32R) for u in range(3)]
        sklo = [tensor(f"sklo{u}", [P, BT], F32R) for u in range(3)]
        route_end = place[0]
        stage = tensor("stage", [P, 3, EW // 3], F32)
        ehi = tensor("ehi", [P, 3, EW // 3], F16)
        elo = tensor("elo", [P, 3, EW // 3], F16)
        big = tensor("big", [P, 3], F32)
        pw2 = tensor("pw2", [P, 3], F32)
        pwi = tensor("pwi", [P, 3], F32)
        scl = tensor("scl", [P, 3], F32)
        whi = tensor("whi", [P, WALL], F32R)
        wlo = tensor("wlo", [P, WALL], F32R)
        assert EW == 3 * (EW // 3) and W3 == EW // 3 and W2 == 2 * (EW // 3)

        place[0] = small0
        ewh = tensor("ewh", [P, E * EW], F16)
        ewl = tensor("ewl", [P, E * EW], F16)
        xg = [tensor(f"xg{u}", [P, H], F32) for u in range(2)]
        xthi = [tensor(f"xthi{u}", [P, H], F16) for u in range(2)]
        xtlo = [tensor(f"xtlo{u}", [P, H], F16) for u in range(2)]
        sa = [tensor(f"sa{u}", [P, F], F32) for u in range(2)]
        hh = [tensor(f"hh{u}", [P, F], F32) for u in range(2)]
        hhi = [tensor(f"hhi{u}", [P, F], F16) for u in range(2)]
        hlo = [tensor(f"hlo{u}", [P, F], F16) for u in range(2)]
        hthi = [tensor(f"hthi{u}", [P, F], F16) for u in range(2)]
        htlo = [tensor(f"htlo{u}", [P, F], F16) for u in range(2)]
        yb = [tensor(f"yb{u}", [P, H], F32) for u in range(2)]
        hmax = [tensor(f"hmax{u}", [P, 1], F32) for u in range(2)]
        hinv = [tensor(f"hinv{u}", [P, 1], F32) for u in range(2)]
        gidx = [tensor(f"gidx{u}", [P, 1], I32) for u in range(2)]
        sidx = [tensor(f"sidx{u}", [P, 1], I32) for u in range(2)]

        routes = {}

        def rt(name, shape, dt=F32):
            nonlocal at
            routes[name], at = sb("rt_" + name, shape, dt, at)
            return routes[name]

        ps = ctx.enter_context(nc.psum_tensor("ps", [P, 8, 512], F32))
        xn_d = nc.dram_tensor("xn_scratch", (T, H), F32, kind="Internal").ap()
        ehi_d = nc.dram_tensor("ehi_scratch", (E * P, EW), F16, kind="Internal").ap()
        elo_d = nc.dram_tensor("elo_scratch", (E * P, EW), F16, kind="Internal").ap()

        def block_rows(d, b):
            return d[bass.ds(b * BT, BT), :].rearrange("(j p) n -> p j n", p=P)

        class Signal:
            def __init__(self, name, credit=0, step=1):
                self.sem = ctx.enter_context(nc.semaphore(name))
                self.credit, self.step = credit, step
                self.one = (self.sem, step)

            def at(self, n):
                return self.sem, (n + self.credit) * self.step

        def D(name, credit=0):
            return Signal(name, credit, 16)

        passed = Signal("passed")
        const_ld, const_ok = D("const_ld"), Signal("const_ok")
        n_ld = [D(f"n_ld{u}") for u in range(2)]
        n_stats, n_mv, n_eps, n_rstd = Signal("n_stats"), Signal("n_mv"), Signal("n_eps"), Signal("n_rstd")
        n_xn = Signal("n_xn", 1)
        n_st = [D(f"n_st{u}", 1) for u in range(2)]
        n_tp = Signal("n_tp", 2)
        n_xt = Signal("n_xt", 2)
        n_lg = Signal("n_lg", 2)
        n_logit = Signal("n_logit", 2)
        r_dve, r_act, r_pe = Signal("r_dve"), Signal("r_act"), Signal("r_pe")
        r_hot = Signal("r_hot")
        r_perm = Signal("r_perm", 2)
        r_ready = Signal("r_ready")
        wst_ld, wst_hi, wst_lo = D("wst_ld"), Signal("wst_hi"), Signal("wst_lo")
        m_ldn = [D(f"m_ldn{u}") for u in range(2)]
        m_ldx = [D(f"m_ldx{u}") for u in range(2)]
        m_st = [D(f"m_st{u}") for u in range(2)]
        m_stats, m_mv, m_eps, m_rstd, m_hn, m_ht, m_dif = (
            [Signal(f"{n}{k}") for k in (1, 2)] for n in ("m_stats", "m_mv", "m_eps", "m_rstd", "m_hn", "m_ht", "m_dif"))
        m_tp = [Signal(f"m_tp{k}", 2) for k in (1, 2)]
        m_mix, m_high, m_low = ({m: Signal(f"{n}{m}", 2) for m in MIXES} for n in ("m_mix", "m_high", "m_low"))
        m_k, m_v, m_r, m_wo, m_cr = (Signal(n, 1) for n in ("m_k", "m_v", "m_r", "m_wo", "m_cr"))
        m_delta, m_exp, m_tr, m_wkv, m_av = (Signal(n, 1) for n in ("m_delta", "m_exp", "m_tr", "m_wkv", "m_av"))
        m_rw, m_rwhi, m_rwlo, m_x1, m_tc = (Signal(n, 1) for n in ("m_rw", "m_rwhi", "m_rwlo", "m_x1", "m_tc"))
        m_u, m_utp, m_x2, m_acc = (Signal(n, 1) for n in ("m_u", "m_utp", "m_x2", "m_acc"))
        m_kk, m_sk, m_sklo, m_val = Signal("m_kk", 1), Signal("m_sk", 1), Signal("m_sklo", 2), Signal("m_val", 3)
        w_ld, w_big, w_sum, w_top, w_pow, w_scl = (D("w_ld"), Signal("w_big"), Signal("w_sum"), Signal("w_top"),
                                                   Signal("w_pow"), Signal("w_scl"))
        w_inv = Signal("w_inv")
        w_hi, w_lo, w_st = Signal("w_hi"), Signal("w_lo"), D("w_st", 2)
        e_w = [D(f"e_w{e}") for e in range(E)]
        e_idx = Signal("e_idx")
        e_g = [D(f"e_g{u}") for u in range(2)]
        e_xtp = Signal("e_xtp", 2)
        e_xthi, e_xtlo = Signal("e_xthi"), Signal("e_xtlo", 1)
        e_up = Signal("e_up", 2)
        e_sa = Signal("e_sa")
        e_h = Signal("e_h", 2)
        e_max, e_inv, e_hhi, e_hlo = Signal("e_max"), Signal("e_inv", 2), Signal("e_hhi"), Signal("e_hlo", 2)
        e_htp = Signal("e_htp", 2)
        e_hthi, e_htlo = Signal("e_hthi", 1), Signal("e_htlo", 1)
        e_dn = Signal("e_dn", 2)
        e_y = Signal("e_y", 2)
        e_to = Signal("e_to")
        e_add = D("e_add")
        e_added = Signal("e_added", 2)
        o_zero, zeros = D("o_zero"), Signal("zeros")

        def credit(eng, *signals):
            for s in signals:
                eng.sem_inc(s.sem, s.credit * s.step)

        def tile_after(s, u, n):
            return s + (u + n) // 2, (u + n) % 2

        def tiles(eng, step, ahead):
            pairs = (NT - ahead) // 2
            with eng.Fori(0, pairs) as s:
                step(s, 0, ahead)
                step(s, 1, ahead)
            for i in range(2 * pairs, NT):
                step(i // 2, i % 2, min(ahead, NT - 1 - i))

        def periods(eng, step):
            for p in (-1, 0, 1):
                step(p // 2, p % 2)
            with eng.Fori(1, NB // 2 - 1) as s:
                step(s, 0)
                step(s, 1)
            for p in range(NB - 2, NB + 2):
                step(p // 2, p % 2)

        def there(b):
            return not isinstance(b, int) or 0 <= b < NB

        def alone(eng):
            eng.sem_inc(passed.sem, 1)

        CH = EW
        chunks = [(a, min(CH, WALL - a)) for a in range(0, WALL, CH)]
        stage_flat = stage[:, :, :].rearrange("p a b -> p (a b)")

        m1, m2 = rt("m1", [P, NJ]), rt("m2", [P, NJ])
        eq, iv, mx = rt("eq", [P, NJ, E]), rt("iv", [P, NJ, E]), rt("mx", [P, NJ])
        oh = [rt("oh0", [P, NJ, E]), rt("oh1", [P, NJ, E])]
        l2 = rt("l2", [P, NJ, E])
        labs, fac, df, keep = (rt(n, [P, NJ, E]) for n in ("labs", "fac", "df", "keep"))
        dfk = [rt(f"df{k}", [P, NJ, E]) for k in range(TOPK)]
        exk = [rt(f"ex{k}", [P, NJ, E]) for k in range(TOPK)]
        den = rt("den", [P, NJ])
        cc, tote, scan, pos, tmp = (rt(n, [P, NJ * E]) for n in ("cc", "tote", "scan", "pos", "tmp"))
        cnt, padf, pinc, dlt = (rt(n, [P, E]) for n in ("cnt", "padf", "pinc", "dlt"))
        cnti = rt("cnti", [P, E], I32)
        slotf = rt("slotf", [P, TOPK * NJ])
        slot, hii = rt("slot", [P, TOPK * NJ], I32), rt("hii", [P, TOPK * NJ], I32)
        hif, lof = rt("hif", [P, TOPK * NJ]), rt("lof", [P, TOPK * NJ])
        ohlo = [[rt(f"ohlo{u}{k}", [P, P]) for k in range(TOPK)] for u in range(2)]
        ohhi = [[rt(f"ohhi{u}{k}", [P, 2 * NT]) for k in range(TOPK)] for u in range(2)]
        empty = rt("empty", [P, NT])
        tok1 = rt("tok1", [P, NT])
        assert at <= route_end

        block = ctx.enter_context(nc.Block())


        @block.sync
        def _(sp):
            credit(sp, n_st[0], n_st[1], w_st)
            sp.dma_start(xx[0][:], block_rows(x, 0)).then_inc(*n_ld[0].one)
            sp.dma_start(vec[:], vecs).then_inc(*const_ld.one)
            sp.dma_start(gw[:], gate).then_inc(*const_ld.one)
            sp.dma_start(xx[1][:], block_rows(x, 1)).then_inc(*n_ld[1].one)
            sp.wait_ge(*zeros.at(1))
            sp.dma_start(out[T:T + P, :], hn[:, 0, :]).then_inc(*o_zero.one)

            def norm_io(s, u, last):
                g = 2 * s + u
                sp.wait_ge(*n_xn.at(g + 1))
                alone(sp)
                sp.dma_start(block_rows(xn_d, g), xn[u][:]).then_inc(*n_st[u].one)
                if not last:
                    sp.dma_start(xx[u][:], block_rows(x, g + 2)).then_inc(*n_ld[u].one)

            with sp.Fori(0, NB // 2 - 1) as s:
                norm_io(s, 0, False)
                norm_io(s, 1, False)
            norm_io(NB // 2 - 1, 0, True)
            norm_io(NB // 2 - 1, 1, True)

            for i, (a, n) in enumerate(chunks):
                if i > 0:
                    sp.wait_ge(*wst_lo.at(i))
                sp.dma_start(stage_flat[:, 0:n], wmix[:, a:a + n]).then_inc(*wst_ld.one)
            for u in range(2):
                sp.wait_ge(*n_st[u].at(NB // 2))
                sp.wait_ge(*n_tp.at(NB))
                sp.dma_start(xn[u][:], block_rows(xn_d, u)).then_inc(*m_ldn[u].one)
                sp.dma_start(xx[u][:], block_rows(x, u)).then_inc(*m_ldx[u].one)
            sp.wait_ge(*wst_lo.at(len(chunks)))

            sp.dma_start(stage_flat, wexp[0:P, :]).then_inc(*w_ld.one)

            def mix_io(s, u):
                p = 2 * s + u
                if there(p - 2):
                    sp.wait_ge(*m_x2.at(p - 1))
                    alone(sp)
                    sp.dma_start(block_rows(out, p - 2), xx[u][:]).then_inc(*m_st[u].one)
                    if there(p):
                        sp.wait_ge(*m_st[u].at(s))
                        alone(sp)
                        sp.dma_start(xx[u][:], block_rows(x, p)).then_inc(*m_ldx[u].one)
                if there(p) and there(p + 2):
                    sp.wait_ge(*m_hn[1].at(p + 1))
                    alone(sp)
                    sp.wait_ge(*m_acc.at(p + 1))
                    alone(sp)
                    sp.dma_start(xn[u][:], block_rows(xn_d, p + 2)).then_inc(*m_ldn[u].one)
                if there(p + 1):
                    sp.wait_ge(*w_lo.at(p + 2))
                    alone(sp)
                    sp.dma_start(ehi_d[bass.ds((p + 1) * P, P), :],
                                 ehi[:, :, :].rearrange("p a b -> p (a b)")).then_inc(*w_st.one)
                    sp.dma_start(elo_d[bass.ds((p + 1) * P, P), :],
                                 elo[:, :, :].rearrange("p a b -> p (a b)")).then_inc(*w_st.one)
                    if there(p + 2):
                        sp.dma_start(stage_flat, wexp[bass.ds((p + 2) * P, P), :]).then_inc(*w_ld.one)

            periods(sp, mix_io)
            for u in range(2):
                sp.wait_ge(*m_st[u].at(NB // 2))
            sp.wait_ge(*w_st.at(2 * E))
            sp.wait_ge(*m_utp.at(NB))
            for e in range(E):
                sp.dma_start(ewh[:, e * EW:(e + 1) * EW], ehi_d[e * P:(e + 1) * P, :]).then_inc(*e_w[e].one)
                sp.dma_start(ewl[:, e * EW:(e + 1) * EW], elo_d[e * P:(e + 1) * P, :]).then_inc(*e_w[e].one)

        @block.gpsimd
        def _(pool):
            credit(pool, m_wkv, m_acc, e_added, *(m_low[m] for m in (MV, CMR, CMK)))
            n_const = 0
            for t, v in ((halfneg[:], -0.5), (id32[:], 0.0), (id16[:], 0.0), (before[:], 0.0), (ones[:], 1.0),
                         (hn[:, 0, :], 0.0), (ht[0][:, :, 0:1], 0.0), (h2t[0][:, :, 0:1], 0.0)):
                pool.memset(t, v).then_inc(*const_ok.one)
                n_const += 1
            for t, pattern, base, by in ((lane, [[1, P]], 0, 0), (tokid, [[P, NJ]], 1, 1), (spare, [[0, 1]], T + 1, 1),
                                         (tile0, [[P, NT]], 0, 0), (down, [[0, NJ], [-1, E]], E, 0)):
                pool.iota(t[:], pattern=pattern, base=base, channel_multiplier=by,
                          allow_small_or_imprecise_dtypes=True).then_inc(*const_ok.one)
                n_const += 1
            pool.wait_ge(*const_ok.at(n_const))
            pool.sem_inc(zeros.sem, 1)
            for m in (id32, id16):
                pool.affine_select(out=m[:], in_=m[:], compare_op=ALU.not_equal, fill=1.0, base=0,
                                   pattern=[[-1, P]], channel_multiplier=1).then_inc(*const_ok.one)
            pool.affine_select(out=before[:], in_=before[:], compare_op=ALU.is_ge, fill=1.0, base=0,
                               pattern=[[-1, P]], channel_multiplier=1).then_inc(*const_ok.one)
            assert n_const + 3 == N_CONST

            def rstd_of(k, var, eps, done, n):
                pool.wait_ge(*var.at(n))
                alone(pool)
                pool.tensor_scalar(rstd[k][:], mv[k][:, :, 1:2].rearrange("p a b -> p (a b)"), EPS, None,
                                   ALU.add).then_inc(*eps.one)
                pool.wait_ge(*eps.at(n))
                pool.tensor_tensor(rstd[k][:], rstd[k][:], halfneg[:], ALU.pow).then_inc(*done.one)

            with pool.Fori(0, NB) as g:
                rstd_of(0, n_mv, n_eps, n_rstd, g + 1)

            def shifted(k, t, u, b):
                pool.wait_ge(*m_ht[k].at(b + 1))
                pool.tensor_tensor(dif[:], t[u][:, :, 1:BT + 1], t[u][:, :, 0:BT],
                                   ALU.subtract).then_inc(*m_dif[k].one)

            def low_pool(m, b, dst, hi):
                pool.wait_ge(*m_high[m].at(b + 1))
                pool.tensor_tensor(dst[:], mixf[AT[m]][:], hi[:].bitcast(F32), ALU.subtract).then_inc(*m_low[m].one)

            def mix_pool(s, u):
                p = 2 * s + u
                if there(p + 1):
                    rstd_of(0, m_mv[0], m_eps[0], m_rstd[0], p + 2)
                if there(p):
                    rstd_of(1, m_mv[1], m_eps[1], m_rstd[1], p + 1)
                if there(p + 1):
                    pool.wait_ge(*m_mix[CMK].at(p))
                    shifted(0, ht, 1 - u, p + 1)
                if there(p):
                    pool.wait_ge(*m_ldx[u].at(s + 1))
                    pool.wait_ge(*m_x1.at(p + 1))
                    pool.tensor_tensor(xx[u][:], xx[u][:], xn[u][:], ALU.add).then_inc(*m_acc.one)
                    if there(p + 1):
                        pool.wait_ge(*m_mix[MR].at(p + 2))
                    pool.wait_ge(*m_mix[CMK].at(p))
                    shifted(1, h2t, u, p)
                if there(p + 1):
                    pool.wait_ge(*m_wo.at(p + 1))
                    low_pool(MV, p + 1, flo[1], fhi[1])
                if there(p):
                    pool.wait_ge(*m_cr.at(p))
                    low_pool(CMR, p, clo[1], chi[1])
                if there(p + 1):
                    pool.wait_ge(*m_av.at(p + 2))
                    pool.tensor_tensor(av[:], av[:], rb[:], ALU.mult).then_inc(*m_wkv.one)
                if there(p):
                    pool.wait_ge(*m_kk.at(KQ * p))
                    low_pool(CMK, p, clo[0], chi[0])

            periods(pool, mix_pool)
            pool.wait_ge(*r_ready.at(1))

            def row_of_slot(i, idx, of, signal, n):
                pool.tensor_copy(idx[:], of[:, bass.ds(i, 1)]).then_inc(*signal.one)
                pool.wait_ge(*signal.at(n))
                alone(pool)
                return bass.IndirectOffsetOnAxis(ap=idx[:].bitcast(U32), axis=0)

            def gather_slots(s, u):
                i = 2 * s + u
                pool.wait_ge(*e_xtp.at(i - 1))
                alone(pool)
                rows = row_of_slot(i, gidx[u], slot_from, e_idx, i + 1)
                pool.indirect_dma_start(out=xg[u][:], out_offset=None, in_=xn_d,
                                        in_offset=rows).then_inc(*e_g[u].one)

            def add_slots(s, u):
                i = 2 * s + u
                pool.wait_ge(*e_y.at(i + 1))
                alone(pool)
                rows = row_of_slot(i, sidx[u], slot_to, e_to, i + 1)
                pool.indirect_dma_start(out=out, out_offset=rows, in_=yb[u][:], in_offset=None,
                                        compute_op=ALU.add).then_inc(*e_add.one)

            AHEAD = 5
            for i in range(AHEAD):
                gather_slots(i // 2, i % 2)
            for u in range(2):
                pool.wait_ge(*m_st[u].at(NB // 2))
            pool.wait_ge(*o_zero.at(1))

            def step_pool(s, u, left):
                add_slots(s, u)
                if left == AHEAD:
                    gather_slots(*tile_after(s, u, AHEAD))
                pool.wait_ge(*e_add.at(2 * s + u + 1))
                pool.sem_inc(e_added.sem, 1)

            tiles(pool, step_pool, AHEAD)

        @block.scalar
        def _(act):
            credit(act, n_xt, n_logit, m_exp, m_tr, m_rwhi, m_tc, m_sk, e_hthi, e_y, *m_high.values())

            def norm_act(s, u):
                g = 2 * s + u
                xt = (e2, rb)[u]
                act.wait_ge(*n_tp.at(g + 1))
                act.wait_ge(*n_lg.at(g - 1))
                act.activation(xt[:], ps[:, 2 * u:2 * u + 2, :], ACT.Copy).then_inc(*n_xt.one)
                act.wait_ge(*n_lg.at(g + 1))
                act.activation(logit[:, bass.ds(g * BJ, BJ), :],
                               ps[:, 4 + u, 0:BJ * E].rearrange("p (a b) -> p a b", a=BJ),
                               ACT.Copy).then_inc(*n_logit.one)

            with act.Fori(0, NB // 2) as s:
                norm_act(s, 0)
                norm_act(s, 1)

            for k in range(TOPK):
                act.wait_ge(*r_dve.at(R_EXP[k]))
                act.activation(exk[k][:], dfk[k][:], ACT.Exp, scale=-1.0).then_inc(*r_act.one)
            for i, (a, n) in enumerate(chunks):
                act.wait_ge(*wst_ld.at(i + 1))
                act.activation(whi[:, a:a + n], stage_flat[:, 0:n], ACT.Copy).then_inc(*wst_hi.one)

            def turned(k, t, b, u, bank, g, bb):
                act.wait_ge(*m_tp[k].at(b + 1))
                for c in range(HC):
                    last = act.activation(t[u][:, c, 1:BT + 1], ps[:, bank + c, :], ACT.Identity,
                                          scale=vec[:, c, g:g + 1], bias=vec[:, c, bb:bb + 1])
                if u == 1:
                    last = act.activation(t[1][:, :, 0:1], t[0][:, :, BT:BT + 1], ACT.Copy)
                last.then_inc(*m_ht[k].one)

            def high(m, b, dst):
                act.wait_ge(*m_mix[m].at(b + 1))
                act.activation(dst[:], mixf[AT[m]][:], ACT.Copy).then_inc(*m_high[m].one)

            def mix_act(s, u):
                p = 2 * s + u

                def keys(*qs):
                    for q in qs if there(p - 1) else ():
                        n = KQ * (p - 1) + q
                        act.wait_ge(*m_kk.at(n + 1))
                        act.wait_ge(*m_val.at(n - min(q, 2)))
                        act.activation(skhi[q % 3][:], ps[:, 6 + q % 2, :], ACT.Silu)
                        act.wait_ge(*m_sklo.at(n - 1))
                        act.activation(skf[q % 2][:], ps[:, 6 + q % 2, :], ACT.Silu).then_inc(*m_sk.one)

                if there(p - 1):
                    act.wait_ge(*m_cr.at(p))
                    act.wait_ge(*m_utp.at(p - 1))
                    act.activation(tc[:], ps[:, 6:8, :], ACT.Tanh, scale=0.5).then_inc(*m_tc.one)
                keys(0, 1)
                if there(p + 1):
                    turned(0, ht, p + 1, 1 - u, 2, LG1, LB1)
                keys(2, 3)
                if there(p + 1):
                    act.wait_ge(*m_r.at(p + 1))
                    high(MK, p + 1, fhi[0])
                if there(p):
                    turned(1, h2t, p, u, 4, LG2, LB2)
                keys(4)
                if there(p + 1):
                    act.wait_ge(*m_wo.at(p + 1))
                    high(MV, p + 1, fhi[1])
                    act.wait_ge(*w_scl.at(p + 2))
                    act.wait_ge(*w_st.at(2 * (p + 1)))
                    for k in range(3):
                        last = act.activation(ehi[:, k, :], stage[:, k, :], ACT.Copy, scale=scl[:, k:k + 1])
                    last.then_inc(*w_hi.one)
                    act.wait_ge(*m_k.at(p + 2))
                    high(MR, p + 1, fhi[0])
                if there(p):
                    act.wait_ge(*m_cr.at(p))
                    high(CMR, p, chi[1])
                keys(5)
                if there(p + 1):
                    act.wait_ge(*m_delta.at(p + 2))
                    act.wait_ge(*m_wkv.at(p + 1))
                    act.activation(rb[:], e2[:], ACT.Exp, scale=-1.0)
                    act.activation(e2[:], e2[:], ACT.Exp).then_inc(*m_exp.one)
                keys(6)
                if there(p + 1):
                    act.wait_ge(*m_av.at(p + 2))
                    act.wait_ge(*m_r.at(p + 2))
                    act.activation(e2[:], ps[:, 4:6, :], ACT.Tanh, scale=0.5).then_inc(*m_tr.one)
                keys(7)
                if there(p + 1):
                    act.wait_ge(*m_rw.at(p + 2))
                    act.activation(fhi[1][:], av[:], ACT.Copy).then_inc(*m_rwhi.one)
                if there(p):
                    act.wait_ge(*m_kk.at(KQ * p))
                    high(CMK, p, chi[0])

            periods(act, mix_act)

            def x_act(s, u):
                i = 2 * s + u
                act.wait_ge(*e_xtp.at(i + 1))
                act.wait_ge(*e_up.at(i - 1))
                act.activation(xthi[u][:], ps[:, 0, 0:H], ACT.Copy, scale=XS).then_inc(*e_xthi.one)

            def silu_act(s, u):
                i = 2 * s + u
                act.wait_ge(*e_up.at(i + 1))
                act.wait_ge(*e_h.at(i - 1))
                act.activation(sa[u][:], ps[:, 1 + 2 * u, :], ACT.Silu,
                               scale=unx[:, bass.ds(i, 1)]).then_inc(*e_sa.one)

            def hidden_act(s, u):
                i = 2 * s + u
                act.wait_ge(*e_inv.at(i + 1))
                act.wait_ge(*e_htp.at(i - 1))
                act.activation(hhi[u][:], hh[u][:], ACT.Copy, scale=hinv[u][:]).then_inc(*e_hhi.one)

            def y_act(s, u):
                i = 2 * s + u
                act.wait_ge(*e_dn.at(i + 1))
                act.wait_ge(*e_added.at(i - 1))
                act.activation(yb[u][:], ps[:, 7, 0:H], ACT.Copy, scale=yscl[:, bass.ds(i, 1)]).then_inc(*e_y.one)

            def step_act(s, u, left):
                i = 2 * s + u
                act.wait_ge(*e_htp.at(i + 1))
                act.wait_ge(*e_dn.at(i - 1))
                act.activation(hthi[u][:], ps[:, 5, :].bitcast(F16)[:, 0:F], ACT.Copy).then_inc(*e_hthi.one)
                if left >= 1:
                    hidden_act(*tile_after(s, u, 1))
                if left >= 2:
                    silu_act(*tile_after(s, u, 2))
                if left >= 3:
                    x_act(*tile_after(s, u, 3))
                y_act(s, u)

            act.wait_ge(*r_ready.at(1))
            x_act(0, 0)
            silu_act(0, 0)
            x_act(0, 1)
            hidden_act(0, 0)
            silu_act(0, 1)
            x_act(1, 0)
            tiles(act, step_act, 3)

        @block.vector
        def _(dve):
            credit(dve, n_xn, m_delta, m_av, m_rw, m_rwlo, m_x1, m_u, m_x2, m_sklo, *m_mix.values(), m_low[MK], m_low[MR],
                   e_inv, e_hlo, e_h, e_xtlo, e_htlo)
            dve.wait_ge(*const_ok.at(N_CONST))
            dve.wait_ge(*const_ld.at(2))
            steps = [0]

            def done(ins):
                steps[0] += 1
                ins.then_inc(*r_dve.one)
                dve.wait_ge(*r_dve.at(steps[0]))

            def spread(k, src, s_stats, s_mv, n):
                for j in range(BJ):
                    last = dve.bn_stats(stats[k][:, j, :], src[:, j, :])
                last.then_inc(*s_stats.one)
                dve.wait_ge(*s_stats.at(n))
                alone(dve)
                for j in range(BJ):
                    last = dve.bn_aggr(mv[k][:, j, :], stats[k][:, j, :])
                last.then_inc(*s_mv.one)

            def normalise(k, src, dst, s_rstd, n, s_dst):
                dve.wait_ge(*s_rstd.at(n))
                for j in range(BJ):
                    last = dve.tensor_scalar(dst[:, j, :], src[:, j, :], mv[k][:, j, 0:1], rstd[k][:, j:j + 1],
                                             ALU.subtract, ALU.mult)
                last.then_inc(*s_dst.one)

            def norm_dve(s, u):
                g = 2 * s + u
                dve.wait_ge(*n_ld[u].at(s + 1))
                dve.wait_ge(*n_st[u].at(s))
                dve.wait_ge(*n_tp.at(g - 1))
                dve.wait_ge(*n_xn.at(g))
                spread(0, xx[u], n_stats, n_mv, g + 1)
                normalise(0, xx[u], xn[u], n_rstd, g + 1, n_xn)

            with dve.Fori(0, NB // 2) as s:
                norm_dve(s, 0)
                norm_dve(s, 1)

            done(dve.tensor_scalar(tfp[:], vec[:, :, TF:TF + 1].rearrange("p a b -> p (a b)"), PP0, None, ALU.add))
            dve.wait_ge(*n_logit.at(NB))

            def wide(t):
                return t[:, :].unsqueeze(2).to_broadcast([P, NJ, E])

            def flat(t):
                return t[:, :, :].rearrange("p a b -> p (a b)")

            done(dve.scalar_tensor_tensor(flat(labs), flat(logit), -1.0, flat(logit), ALU.mult, ALU.max))
            for k, (top, of) in enumerate(((m1, logit), (m2, l2))):
                done(dve.tensor_reduce(top[:], of[:], AX.X, ALU.max))
                done(dve.tensor_tensor(eq[:], of[:], wide(top), ALU.is_equal))
                done(dve.tensor_tensor(iv[:], eq[:], down[:], ALU.mult))
                done(dve.tensor_reduce(mx[:], iv[:], AX.X, ALU.max))
                done(dve.tensor_tensor(oh[k][:], iv[:], wide(mx), ALU.is_equal))
                done(dve.tensor_tensor(fac[:], labs[:], wide(top), ALU.max))
                done(dve.tensor_tensor(df[:], wide(top), logit[:], ALU.subtract))
                done(dve.scalar_tensor_tensor(flat(keep), flat(fac), JITTER, flat(df), ALU.mult, ALU.is_ge))
                if k == 0:
                    done(dve.scalar_tensor_tensor(flat(l2), flat(oh[0]), -3e38, flat(logit), ALU.mult, ALU.add))
                done(dve.tensor_tensor(dfk[k][:], wide(top), of[:], ALU.subtract))
                assert steps[0] == R_EXP[k], steps
                dve.wait_ge(*r_act.at(k + 1))
                done(dve.tensor_tensor(exk[k][:], exk[k][:], keep[:], ALU.mult))
                done(dve.tensor_reduce(den[:], exk[k][:], AX.X, ALU.add))
                done(dve.reciprocal(gain[:, k, :], den[:]))
            done(dve.tensor_tensor(cc[:], flat(oh[0]), flat(oh[1]), ALU.add))
            assert steps[0] == R_PICKS, steps
            dve.wait_ge(*r_pe.at(1))
            by_e = lambda t: t.rearrange("p (j e) -> p e j", e=E)
            done(dve.tensor_copy(tote[:, :].rearrange("p (e j) -> p e j", e=E), by_e(ps[:, 7, 0:NJ * E])))
            done(dve.tensor_tensor_scan(scan[:], ones[:], tote[:], 0.0, ALU.mult, ALU.add))
            done(dve.tensor_tensor(pos[:], scan[:], tote[:], ALU.subtract))
            s_ej, p_ej = (t[:, :].rearrange("p (e j) -> p e j", e=E) for t in (scan, pos))
            last_of = s_ej[:, :, NJ - 1:NJ].rearrange("p a b -> p (a b)")
            first_of = p_ej[:, :, 0:1].rearrange("p a b -> p (a b)")
            done(dve.tensor_tensor(cnt[:], last_of, first_of, ALU.subtract))
            done(dve.tensor_scalar(cnti[:], cnt[:], float(P - 1), None, ALU.add))
            done(dve.tensor_scalar(cnti[:], cnti[:], 7, 7, ALU.logical_shift_right, ALU.logical_shift_left))
            done(dve.tensor_copy(padf[:], cnti[:]))
            done(dve.tensor_tensor_scan(pinc[:], ones[:, 0:E], padf[:], 0.0, ALU.mult, ALU.add))
            done(dve.tensor_tensor(pbx[:], pinc[:], padf[:], ALU.subtract))
            done(dve.tensor_tensor(dlt[:], pbx[:], first_of, ALU.subtract))
            done(dve.tensor_tensor(p_ej, p_ej, dlt[:, :].unsqueeze(2).to_broadcast([P, E, NJ]), ALU.add))
            done(dve.tensor_tensor(tmp[:, :].rearrange("p (j e) -> p j e", e=E),
                                   ps[:, 6, 0:NJ * E].rearrange("p (j e) -> p j e", e=E),
                                   pos[:, :].rearrange("p (e j) -> p j e", e=E), ALU.add))
            for k in range(TOPK):
                done(dve.tensor_tensor(cc[:], tmp[:], flat(oh[k]), ALU.mult))
                done(dve.tensor_reduce(slotf[:, k * NJ:(k + 1) * NJ],
                                       cc[:, :].rearrange("p (j e) -> p j e", e=E), AX.X, ALU.add))
            done(dve.tensor_copy(slot[:], slotf[:]))
            done(dve.tensor_scalar(hii[:], slot[:], 7, None, ALU.logical_shift_right))
            done(dve.tensor_copy(hif[:], hii[:]))
            done(dve.scalar_tensor_tensor(lof[:], hif[:], -float(P), slotf[:], ALU.mult, ALU.add))
            done(dve.tensor_scalar(tile_exp[:], tile0[:], pbx[:, 1:2], None, ALU.is_ge))
            for e in range(2, E):
                done(dve.scalar_tensor_tensor(tile_exp[:], tile0[:], pbx[:, e:e + 1], tile_exp[:],
                                              ALU.is_ge, ALU.add))
            done(dve.tensor_scalar(tile_off[:], tile_exp[:], float(EW), None, ALU.mult))

            def hot(s, u):
                j = 2 * s + u
                dve.wait_ge(*r_perm.at(j - 1))
                for k in range(TOPK):
                    dve.tensor_scalar(ohlo[u][k][:], lane[:], lof[:, bass.ds(k * NJ + j, 1)], None, ALU.is_equal)
                    for part, value in enumerate((tokid[:, bass.ds(j, 1)], gain[:, k, bass.ds(j, 1)])):
                        last = dve.tensor_scalar(ohhi[u][k][:, part * NT:(part + 1) * NT], lane[:, 0:NT],
                                                 hif[:, bass.ds(k * NJ + j, 1)], value, ALU.is_equal, ALU.mult)
                last.then_inc(*r_hot.one)

            with dve.Fori(0, NJ // 2) as s:
                hot(s, 0)
                hot(s, 1)
            dve.wait_ge(*r_perm.at(NJ))
            done(dve.tensor_copy(slot_gain[:], ps[:, 7, NT:2 * NT]))
            done(dve.tensor_copy(tok1[:], ps[:, 7, 0:NT]))
            done(dve.tensor_scalar(slot_from[:], tok1[:], -1.0, 0.0, ALU.add, ALU.max))
            done(dve.tensor_scalar(empty[:], tok1[:], 0.0, spare[:], ALU.is_equal, ALU.mult))
            done(dve.scalar_tensor_tensor(slot_to[:], tok1[:], -1.0, empty[:], ALU.add, ALU.add))

            for i, (a, n) in enumerate(chunks):
                dve.wait_ge(*wst_hi.at(i + 1))
                dve.tensor_tensor(wlo[:, a:a + n], stage_flat[:, 0:n], whi[:, a:a + n].bitcast(F32),
                                  ALU.subtract).then_inc(*wst_lo.one)

            def mixed(m, b, k, h):
                dve.wait_ge(*m_dif[k].at(b + 1))
                for c in range(HC):
                    last = dve.scalar_tensor_tensor(mixf[AT[m]][:, c, :], dif[:, c, :], vec[:, c, m:m + 1],
                                                    h[:, c, 0:BT], ALU.mult, ALU.add)
                last.then_inc(*m_mix[m].one)

            def low(m, b, dst, hi):
                dve.wait_ge(*m_high[m].at(b + 1))
                dve.tensor_tensor(dst[:], mixf[AT[m]][:], hi[:].bitcast(F32), ALU.subtract).then_inc(*m_low[m].one)

            def mix_dve(s, u):
                p = 2 * s + u

                def keys(*qs):
                    for q in qs if there(p - 1) else ():
                        n = KQ * (p - 1) + q
                        dve.wait_ge(*m_sk.at(n + 1))
                        dve.wait_ge(*m_val.at(n - min(q, 2)))
                        dve.tensor_tensor(sklo[q % 3][:], skf[q % 2][:], skhi[q % 3][:].bitcast(F32),
                                          ALU.subtract).then_inc(*m_sklo.one)

                if there(p - 2):
                    dve.wait_ge(*m_tc.at(p - 1))
                    dve.wait_ge(*m_val.at(KQ * (p - 1)))
                    dve.scalar_tensor_tensor(tc[:], tc[:], 1.0, ps[:, 0:2, :], ALU.add, ALU.mult).then_inc(*m_u.one)
                if there(p + 1):
                    dve.wait_ge(*m_ldn[1 - u].at(s + 1 + u))
                    spread(0, xn[1 - u], m_stats[0], m_mv[0], p + 2)
                if there(p):
                    dve.wait_ge(*m_wo.at(p + 1))
                    dve.tensor_tensor(xn[u][:], rows(2), xn[u][:], ALU.add).then_inc(*m_x1.one)
                if there(p - 2):
                    dve.wait_ge(*m_utp.at(p - 1))
                    dve.wait_ge(*m_acc.at(p - 1))
                    dve.scalar_tensor_tensor(xx[u][:], rows(0), 0.5, xx[u][:], ALU.mult, ALU.add).then_inc(*m_x2.one)
                if there(p + 1):
                    dve.wait_ge(*m_tp[1].at(p))
                    normalise(0, xn[1 - u], hn, m_rstd[0], p + 2, m_hn[0])
                if there(p):
                    dve.wait_ge(*m_x1.at(p + 1))
                    spread(1, xn[u], m_stats[1], m_mv[1], p + 1)
                if there(p + 1):
                    dve.wait_ge(*w_ld.at(p + 2))
                    dve.tensor_reduce(big[:], stage[:], AX.X, ALU.max, apply_absolute_value=True).then_inc(*w_big.one)
                keys(0)
                if there(p):
                    if there(p + 1):
                        dve.wait_ge(*m_tp[0].at(p + 2))
                    dve.wait_ge(*m_tp[1].at(p))
                    normalise(1, xn[u], hn, m_rstd[1], p + 1, m_hn[1])
                if there(p + 1):
                    e = p + 1
                    dve.wait_ge(*w_sum.at(e + 1))
                    dve.tensor_scalar(pw2[:], ps[:, 4, 0:3], 1e-30, None, ALU.max).then_inc(*w_top.one)
                    dve.wait_ge(*w_top.at(e + 1))
                    dve.tensor_scalar(pw2[:].bitcast(I32), pw2[:].bitcast(I32), 0x7F800000, None,
                                      ALU.bitwise_and).then_inc(*w_pow.one)
                    dve.wait_ge(*w_pow.at(e + 1))
                    dve.tensor_scalar(pwi[:], pw2[:], 2.0 ** -14, None, ALU.mult).then_inc(*w_inv.one)
                    dve.wait_ge(*w_inv.at(e + 1))
                    dve.reciprocal(scl[:], pwi[:]).then_inc(*w_scl.one)
                    dve.tensor_copy(unscale[:, bass.ds(e, 1), :].rearrange("p a b -> p (a b)"), pwi[:])
                keys(1)
                if there(p + 1):
                    dve.wait_ge(*m_low[MR].at(p + 1))
                    mixed(MK, p + 1, 0, ht[1 - u])
                    dve.wait_ge(*m_low[MV].at(p + 1))
                    mixed(MV, p + 1, 0, ht[1 - u])
                keys(2)
                if there(p + 1):
                    dve.wait_ge(*m_r.at(p + 1))
                    low(MK, p + 1, flo[0], fhi[0])
                    dve.wait_ge(*m_low[MK].at(p + 2))
                    mixed(MR, p + 1, 0, ht[1 - u])
                keys(3)
                if there(p):
                    dve.wait_ge(*m_low[CMK].at(p))
                    mixed(CMR, p, 1, h2t[u])
                keys(4)
                if there(p + 1):
                    dve.wait_ge(*m_k.at(p + 2))
                    dve.wait_ge(*m_rw.at(p + 1))
                    for c in range(HC):
                        last = dve.tensor_scalar(e2[:, c, :], ps[:, 4 + c, :], tfp[:, c:c + 1], 0.0, ALU.add, ALU.min)
                    last.then_inc(*m_delta.one)
                    low(MR, p + 1, flo[0], fhi[0])
                keys(5)
                if there(p + 1):
                    dve.wait_ge(*w_hi.at(p + 2))
                    for k in range(3):
                        last = dve.scalar_tensor_tensor(elo[:, k, :], stage[:, k, :], scl[:, k:k + 1],
                                                        ehi[:, k, :], ALU.mult, ALU.subtract)
                    last.then_inc(*w_lo.one)
                    dve.wait_ge(*m_exp.at(p + 2))
                    dve.wait_ge(*m_v.at(p + 2))
                    dve.wait_ge(*m_rwlo.at(p + 1))
                    dve.scalar_tensor_tensor(av[:], ps[:, 2:4, :], 0.5, e2[:], ALU.mult, ALU.mult).then_inc(*m_av.one)
                keys(6)
                if there(p):
                    dve.wait_ge(*m_low[CMR].at(p + 1))
                    mixed(CMK, p, 1, h2t[u])
                if there(p + 1):
                    dve.wait_ge(*m_wkv.at(p + 2))
                    dve.wait_ge(*m_tr.at(p + 2))
                    dve.scalar_tensor_tensor(av[:], e2[:], 1.0, av[:], ALU.add, ALU.mult).then_inc(*m_rw.one)
                    dve.wait_ge(*m_rwhi.at(p + 2))
                    dve.tensor_tensor(flo[1][:], av[:], fhi[1][:].bitcast(F32), ALU.subtract).then_inc(*m_rwlo.one)
                keys(7)

            def rows(bank):
                return ps[:, bank:bank + 2, :].rearrange("p b (j n) -> p (b j) n", n=H)

            dve.wait_ge(*o_zero.at(1))
            periods(dve, mix_dve)

            dve.memset(unx[:], 0.0)
            done(dve.memset(uny[:], 0.0))
            done(dve.tensor_tensor(un32[:], unscale[:, :, 1:2].rearrange("p a b -> p (a b)"),
                                   unscale[:, :, 2:3].rearrange("p a b -> p (a b)"), ALU.mult))
            for e in range(E):
                for dst, by in ((unx, unscale[:, e, 0:1]), (uny, un32[:, e:e + 1])):
                    done(dve.tensor_scalar(picked[:], tile_exp[:], float(e), by, ALU.is_equal, ALU.mult))
                    done(dve.scalar_tensor_tensor(dst[:], picked[:], 1.0 / XS, dst[:], ALU.mult, ALU.add))
            dve.tensor_tensor(uny[:], uny[:], slot_gain[:], ALU.mult).then_inc(*r_ready.one)

            def x_dve(s, u):
                i = 2 * s + u
                dve.wait_ge(*e_xthi.at(i + 1))
                dve.wait_ge(*e_up.at(i - 1))
                dve.scalar_tensor_tensor(xtlo[u][:], ps[:, 0, 0:H], XS, xthi[u][:], ALU.mult,
                                         ALU.subtract).then_inc(*e_xtlo.one)

            def hidden_dve(s, u):
                i = 2 * s + u
                dve.wait_ge(*e_sa.at(i + 1))
                dve.wait_ge(*e_hlo.at(i - 1))
                dve.tensor_tensor(hh[u][:], ps[:, 2 + 2 * u, :], sa[u][:], ALU.mult).then_inc(*e_h.one)
                dve.wait_ge(*e_h.at(i + 1))
                dve.wait_ge(*e_inv.at(i - 1))
                dve.tensor_reduce(hmax[u][:], hh[u][:], AX.X, ALU.max,
                                  apply_absolute_value=True).then_inc(*e_max.one)
                dve.wait_ge(*e_max.at(2 * i + 1))
                dve.tensor_scalar(hmax[u][:], hmax[u][:], 1e-30, 2.0 ** -14, ALU.max, ALU.mult).then_inc(*e_max.one)
                dve.wait_ge(*e_max.at(2 * i + 2))
                dve.reciprocal(hinv[u][:], hmax[u][:])
                dve.tensor_tensor(yscl[:, bass.ds(i, 1)], hmax[u][:], uny[:, bass.ds(i, 1)],
                                  ALU.mult).then_inc(*e_inv.one)

            def hidden_low(s, u):
                i = 2 * s + u
                dve.wait_ge(*e_hhi.at(i + 1))
                dve.wait_ge(*e_htp.at(i - 1))
                dve.scalar_tensor_tensor(hlo[u][:], hh[u][:], hinv[u][:], hhi[u][:], ALU.mult,
                                         ALU.subtract).then_inc(*e_hlo.one)

            def step_dve(s, u, left):
                i = 2 * s + u
                dve.wait_ge(*e_htp.at(i + 1))
                dve.wait_ge(*e_dn.at(i - 1))
                dve.tensor_copy(htlo[u][:], ps[:, 6, :].bitcast(F16)[:, 0:F]).then_inc(*e_htlo.one)
                if left >= 1:
                    hidden_low(*tile_after(s, u, 1))
                if left >= 3:
                    x_dve(*tile_after(s, u, 3))
                if left >= 2:
                    hidden_dve(*tile_after(s, u, 2))

            x_dve(0, 0)
            x_dve(0, 1)
            hidden_dve(0, 0)
            x_dve(1, 0)
            hidden_low(0, 0)
            hidden_dve(0, 1)
            tiles(dve, step_dve, 3)

        @block.tensor
        def _(pe):
            credit(pe, n_tp, n_lg, r_perm, *m_tp, m_k, m_v, m_r, m_wo, m_cr, m_kk, m_val, m_utp, e_xtp, e_up, e_htp, e_dn)
            pe.wait_ge(*const_ok.at(N_CONST))
            pe.wait_ge(*const_ld.at(2))

            def turn(src, bank):
                for c in range(HC):
                    for j in range(BJ):
                        last = pe.transpose(ps[:, bank + c, j * P:(j + 1) * P], src[:, j, c * P:(c + 1) * P],
                                            id32[:])
                return last

            def norm_pe(s, u):
                g = 2 * s + u
                pe.wait_ge(*n_xn.at(g + 1))
                pe.wait_ge(*n_xt.at(g - 1))
                turn(xn[u], 2 * u).then_inc(*n_tp.one)
                pe.wait_ge(*n_xt.at(g + 1))
                pe.wait_ge(*n_logit.at(g - 1))
                xt = (e2, rb)[u]
                for j in range(BJ):
                    for c in range(HC):
                        last = pe.matmul(ps[:, 4 + u, j * E:(j + 1) * E], xt[:, c, j * P:(j + 1) * P],
                                         gw[:, c, :], start=(c == 0), stop=(c == HC - 1))
                last.then_inc(*n_lg.one)

            with pe.Fori(0, NB // 2) as s:
                norm_pe(s, 0)
                norm_pe(s, 1)

            pe.wait_ge(*r_dve.at(R_PICKS))
            pe.matmul(ps[:, 6, 0:NJ * E], before[:], cc[:], start=True, stop=True)
            pe.matmul(ps[:, 7, 0:NJ * E], ones[:, 0:P], cc[:], start=True, stop=True).then_inc(*r_pe.one)

            def permute(j, u, first, last):
                pe.wait_ge(*r_hot.at(j + 1))
                for k in range(TOPK):
                    mm = pe.matmul(ps[:, 7, 0:2 * NT], ohlo[u][k][:], ohhi[u][k][:], start=first and k == 0,
                                   stop=last and k == TOPK - 1)
                mm.then_inc(*r_perm.one)

            permute(0, 0, True, False)
            with pe.Fori(0, NJ // 2 - 1) as s:
                permute(2 * s + 1, 1, False, False)
                permute(2 * s + 2, 0, False, False)
            permute(NJ - 1, 1, False, True)

            pe.wait_ge(*wst_lo.at(len(chunks)))

            def product(bank, w, width, m, hi, lo):
                for c in range(HC):
                    a = w + c * width + m * P
                    for i, (ww, t) in enumerate(((whi, hi), (whi, lo), (wlo, hi))):
                        last = pe.matmul(ps[:, bank, :], ww[:, a:a + P], t[:, c, :],
                                         start=(c == 0 and i == 0), stop=(c == HC - 1 and i == 2))
                return last

            def mix_pe(s, u):
                p = 2 * s + u

                def keys(q):
                    if there(p - 1):
                        if q == 0:
                            pe.wait_ge(*m_low[CMK].at(p))
                            pe.wait_ge(*m_tc.at(p))
                        if q >= 2:
                            pe.wait_ge(*m_sk.at(KQ * (p - 1) + q - 1))
                        product(6 + q % 2, WKEY, KEY, q, chi[0], clo[0]).then_inc(*m_kk.one)

                def value(q):
                    if there(p - 1):
                        if q == 0:
                            pe.wait_ge(*m_x2.at(p - 1))
                        pe.wait_ge(*m_sklo.at(KQ * (p - 1) + q + 1))
                        for m in range(HC):
                            a = WVAL + q * H + m * P
                            for i, (ww, t) in enumerate(((whi, skhi), (whi, sklo), (wlo, skhi))):
                                last = pe.matmul(ps[:, m, :], ww[:, a:a + P], t[q % 3][:],
                                                 start=(q == 0 and i == 0), stop=(q == KQ - 1 and i == 2))
                        last.then_inc(*m_val.one)

                if there(p):
                    pe.wait_ge(*m_av.at(p + 1))
                    pe.wait_ge(*m_rwlo.at(p + 1))
                    for j in range(BJ):
                        o = ps[:, 2 + j // 2, (j % 2) * H:(j % 2 + 1) * H]
                        for c in range(HC):
                            for i, (t, ww) in enumerate(((fhi[1], whi), (fhi[1], wlo), (flo[1], whi))):
                                last = pe.matmul(o, t[:, c, j * P:(j + 1) * P], ww[:, WO + c * H:WO + (c + 1) * H],
                                                 start=(c == 0 and i == 0), stop=(c == HC - 1 and i == 2))
                    last.then_inc(*m_wo.one)
                if there(p - 2):
                    pe.wait_ge(*m_u.at(p - 1))
                    for j in range(BJ):
                        for c in range(HC):
                            a = (j % 2) * H + c * P
                            last = pe.transpose(ps[:, j // 2, a:a + P], tc[:, c, j * P:(j + 1) * P], id32[:])
                    last.then_inc(*m_utp.one)
                if there(p - 1):
                    pe.wait_ge(*m_low[CMR].at(p))
                    pe.wait_ge(*m_sk.at(KQ * (p - 1)))
                    product(6, WCR, H, 0, chi[1], clo[1])
                    product(7, WCR, H, 1, chi[1], clo[1]).then_inc(*m_cr.one)
                keys(0)
                keys(1)
                if there(p + 1):
                    pe.wait_ge(*m_hn[0].at(p + 2))
                    pe.wait_ge(*m_x1.at(p + 1))
                    turn(hn, 2).then_inc(*m_tp[0].one)
                keys(2)
                if there(p + 1):
                    pe.wait_ge(*w_big.at(p + 2))
                    pe.wait_ge(*m_tr.at(p + 1))
                    pe.matmul(ps[:, 4, 0:3], ones[:, 0:P], big[:], start=True, stop=True).then_inc(*w_sum.one)
                value(0)
                keys(3)
                value(1)
                if there(p):
                    pe.wait_ge(*m_hn[1].at(p + 1))
                    pe.wait_ge(*m_tr.at(p + 1))
                    if there(p + 1):
                        pe.wait_ge(*w_top.at(p + 2))
                    turn(hn, 4).then_inc(*m_tp[1].one)
                keys(4)
                value(2)
                if there(p + 1):
                    pe.wait_ge(*m_low[MK].at(p + 2))
                    pe.wait_ge(*w_top.at(p + 2))
                    if there(p):
                        pe.wait_ge(*m_ht[1].at(p + 1))
                    product(4, WK, H, 0, fhi[0], flo[0])
                    product(5, WK, H, 1, fhi[0], flo[0]).then_inc(*m_k.one)
                keys(5)
                value(3)
                if there(p + 1):
                    pe.wait_ge(*m_low[MV].at(p + 2))
                    pe.wait_ge(*m_ht[0].at(p + 2))
                    product(2, WV, H, 0, fhi[1], flo[1])
                    product(3, WV, H, 1, fhi[1], flo[1]).then_inc(*m_v.one)
                keys(6)
                value(4)
                if there(p + 1):
                    pe.wait_ge(*m_low[MR].at(p + 2))
                    pe.wait_ge(*m_delta.at(p + 2))
                    product(4, WR, H, 0, fhi[0], flo[0])
                    product(5, WR, H, 1, fhi[0], flo[0]).then_inc(*m_r.one)
                keys(7)
                value(5)
                value(6)
                value(7)

            periods(pe, mix_pe)

            pe.wait_ge(*r_ready.at(1))
            pe.wait_ge(*m_x2.at(NB))
            for e in range(E):
                pe.wait_ge(*e_w[e].at(2))
            alone(pe)

            def weights_of(s, u):
                return pe.value_load(tile_off[0:1, bass.ds(2 * s + u, 1)], min_val=0, max_val=(E - 1) * EW)

            def turn_slots(s, u):
                i = 2 * s + u
                pe.wait_ge(*e_g[u].at(s + 1))
                pe.wait_ge(*e_xtlo.at(i))
                for c in range(HC):
                    last = pe.transpose(ps[:, 0, c * P:(c + 1) * P], xg[u][:, c * P:(c + 1) * P], id32[:])
                last.then_inc(*e_xtp.one)

            def up(s, u):
                i = 2 * s + u
                off = weights_of(s, u)
                pe.wait_ge(*e_xtlo.at(i + 1))
                pe.wait_ge(*e_h.at(i - 1))
                for c in range(HC):
                    for n, (t, ww) in enumerate(((xthi, ewh), (xthi, ewl), (xtlo, ewh))):
                        for bank, w in ((1 + 2 * u, W1), (2 + 2 * u, W3)):
                            last = pe.matmul(ps[:, bank, :], t[u][:, c * P:(c + 1) * P],
                                             ww[:, bass.ds(off + (w + c * F), F)],
                                             start=(c == 0 and n == 0), stop=(c == HC - 1 and n == 2))
                last.then_inc(*e_up.one)

            def turn_hidden(s, u):
                i = 2 * s + u
                pe.wait_ge(*e_hlo.at(i + 1))
                pe.wait_ge(*e_hthi.at(i))
                pe.wait_ge(*e_htlo.at(i))
                for k in range(F // P):
                    for bank, t in ((5, hhi), (6, hlo)):
                        last = pe.transpose(ps[:, bank, :].bitcast(F16)[:, k * P:(k + 1) * P],
                                            t[u][:, k * P:(k + 1) * P], id16[:])
                last.then_inc(*e_htp.one)

            def down(s, u):
                i = 2 * s + u
                off = weights_of(s, u)
                pe.wait_ge(*e_hthi.at(i + 1))
                pe.wait_ge(*e_htlo.at(i + 1))
                pe.wait_ge(*e_y.at(i))
                for k in range(F // P):
                    for n, (t, ww) in enumerate(((hthi, ewh), (hthi, ewl), (htlo, ewh))):
                        last = pe.matmul(ps[:, 7, 0:H], t[u][:, k * P:(k + 1) * P],
                                         ww[:, bass.ds(off + (W2 + k * H), H)],
                                         start=(k == 0 and n == 0), stop=(k == F // P - 1 and n == 2))
                last.then_inc(*e_dn.one)

            def step_pe(s, u, left):
                turn_hidden(s, u)
                if left >= 2:
                    up(*tile_after(s, u, 2))
                if left >= 3:
                    turn_slots(*tile_after(s, u, 3))
                down(s, u)

            turn_slots(0, 0)
            up(0, 0)
            turn_slots(0, 1)
            up(0, 1)
            turn_slots(1, 0)
            tiles(pe, step_pe, 3)


def kernel(**inputs):
    import numpy as np
    import concourse.bacc as bacc
    from concourse.bass_utils import run_bass_kernel_spmd

    def row(name):
        return np.asarray(inputs["L0_attn_" + name])

    def halves(w):
        k, n = w.shape
        return w.reshape(k // P, P, n).transpose(1, 0, 2).reshape(P, -1)

    vecs = np.stack([row(n).reshape(HC, P) for n in
                     ("ln1_g", "ln1_b", "ln2_g", "ln2_b", "tm_first", "tm_mk", "tm_mv", "tm_mr",
                      "cm_mk", "cm_mr")], axis=-1).transpose(1, 0, 2)
    gate = np.asarray(inputs["L0_ffn_gate_w"]).T.reshape(HC, P, E).transpose(1, 0, 2)
    wmix = np.concatenate([halves(row(n).T) for n in ("Wk", "Wv", "Wr", "Wo", "Wcr", "Wkey", "Wval")], axis=1)
    w1, w2, w3 = (np.asarray(inputs["L0_ffn_" + n]) for n in ("w1", "w2", "w3"))
    wexp = np.concatenate([np.concatenate([halves(w1[e].T), halves(w3[e].T), halves(w2[e].T)], axis=1)
                           for e in range(E)], axis=0)
    arrays = {"x": row("x").reshape(T, H), "vecs": vecs, "gate": gate, "wmix": wmix, "wexp": wexp}
    arrays = {n: np.ascontiguousarray(a) for n, a in arrays.items()}

    nc = bacc.Bacc("TRN2", target_bir_lowering=False, num_devices=1)
    args = [nc.dram_tensor(n + "_in", a.shape, F32, kind="ExternalInput").ap() for n, a in arrays.items()]
    out = nc.dram_tensor("out_0", (T + P, H), F32, kind="ExternalOutput").ap()
    build(nc, *args, out)
    r = run_bass_kernel_spmd(nc, [{n + "_in": a for n, a in arrays.items()}], core_ids=[0])
    return np.asarray(r.results[0]["out_0"])[:T].reshape(NSEQ, SEQ, H)
```

```python
from contextlib import ExitStack

import concourse.bass as bass
from concourse import mybir

ALU = mybir.AluOpType
ACT = mybir.ActivationFunctionType
AX = mybir.AxisListType
F32 = mybir.dt.float32
F32R = mybir.dt.float32r
F16 = mybir.dt.float16
I32 = mybir.dt.int32
U32 = mybir.dt.uint32

P = 128
H = 256
HC = H // P
SEQ = 1024
NSEQ = 4
T = SEQ * NSEQ
BT = 512
BJ = BT // P
NB = T // BT
NJ = T // P
E = 8
F = 512
KEY = 4 * H
KQ = KEY // P
TOPK = 2
NT = T * TOPK // P + E - 1
EW = 2 * HC * F + (F // P) * H
W1, W3, W2 = 0, HC * F, 2 * HC * F
UNROLL = 8
EPS = 1e-5
JITTER = 0.02
PP0 = 1e38
XS = 1024.0
WK, WV, WR, WO = 0, HC * H, 2 * HC * H, 3 * HC * H
WCR = 4 * HC * H
WKEY = 5 * HC * H
WVAL = WKEY + HC * KEY
WALL = WVAL + KQ * H
N_CONST = 16
R_EXP = (12, 24)
R_PICKS = 28
LG1, LB1, LG2, LB2, TF, MK, MV, MR, CMK, CMR = range(10)
MIXES = (MK, MV, MR, CMK, CMR)
AT = {MK: 0, MR: 0, MV: 1, CMK: 2, CMR: 2}


def build(nc, x, vecs, gate, wmix, wexp, out):
    ctx = ExitStack()
    with ctx:
        place = [nc.sbuf_base]

        def sb(name, shape, dt, at=None):
            words = 1
            for n in shape[1:]:
                words *= n
            size = words * (2 if dt == F16 else 4)
            start = place[0] if at is None else at
            start = (start + 31) // 32 * 32
            if at is None:
                place[0] = start + size
            assert start + size <= nc.sbuf_top, (name, start + size)
            return nc.alloc_sbuf_tensor_at(name, shape, dt, offset=start), start + size

        def S(name):
            return ctx.enter_context(nc.semaphore(name))

        def tensor(name, shape, dt):
            return sb(name, shape, dt)[0]

        def tensor_at(name, shape, dt, start):
            return sb(name, shape, dt, start)[0]

        id32 = tensor("id32", [P, P], F32)
        id16 = tensor("id16", [P, P], F16)
        ones = tensor("ones", [P, NJ * E], F32)
        lane = tensor("lane", [P, P], F32)
        tokid = tensor("tokid", [P, NJ], F32)
        tile0 = tensor("tile0", [P, NT], F32)
        vec = tensor("vec", [P, HC, 10], F32)
        tfp = tensor("tfp", [P, HC], F32)
        gw = tensor("gw", [P, HC, E], F32)
        halfneg = tensor("halfneg", [P, BJ], F32)
        spare = tensor("spare", [P, 1], F32)
        slot_from = tensor("slot_from", [P, NT], I32)
        slot_to = tensor("slot_to", [P, NT], I32)
        slot_gain = tensor("slot_gain", [P, NT], F32)
        yscl = tensor("yscl", [P, NT], F32)
        tile_exp = tensor("tile_exp", [P, NT], F32)
        tile_off = tensor("tile_off", [P, NT], I32)
        unx = tensor("unx", [P, NT], F32)
        uny = tensor("uny", [P, NT], F32)
        unscale = tensor("unscale", [P, E, 3], F32)
        pbx = tensor("pbx", [P, E], F32)
        un32 = tensor("un32", [P, E], F32)
        picked = tensor("picked", [P, NT], F32)
        tile_need = tensor("tile_need", [P, NT], I32)
        xg = [tensor(f"xg{u}", [P, H], F32) for u in range(2)]
        gidx = [tensor(f"gidx{u}", [P, 1], I32) for u in range(2)]

        xx = [tensor(f"xx{u}", [P, BJ, H], F32) for u in range(2)]
        late = place[0]
        chi = [tensor(f"chi{u}", [P, HC, BT], F32R) for u in range(2)]
        clo = [tensor(f"clo{u}", [P, HC, BT], F32R) for u in range(2)]
        tc = tensor("tc", [P, HC, BT], F32)
        uu = tensor("uu", [P, HC, BT], F32)
        skf = [tensor(f"skf{u}", [P, BT], F32) for u in range(2)]
        skhi = [tensor(f"skhi{u}", [P, BT], F32R) for u in range(3)]
        sklo = [tensor(f"sklo{u}", [P, BT], F32R) for u in range(3)]
        early = place[0]
        stage = tensor("stage", [P, 3, EW // 3], F32)
        stage_b_at = place[0]
        ehi = tensor("ehi", [P, 3, EW // 3], F16)
        elo = tensor("elo", [P, 3, EW // 3], F16)
        stage_b = tensor_at("stage_b", [P, EW], F32, stage_b_at)
        e2 = tensor("e2", [P, HC, BT], F32)
        rb = tensor("rb", [P, HC, BT], F32)
        xn = [tensor(f"xn{u}", [P, BJ, H], F32) for u in range(2)]
        hn = tensor("hn", [P, BJ, H], F32)
        ht = [tensor(f"ht{u}", [P, HC, BT + 1], F32) for u in range(2)]
        h2t = [tensor(f"h2t{u}", [P, HC, BT + 1], F32) for u in range(2)]
        dif = tensor("dif", [P, HC, BT], F32)
        fhi = [tensor(f"fhi{u}", [P, HC, BT], F32R) for u in range(2)]
        flo = [tensor(f"flo{u}", [P, HC, BT], F32R) for u in range(2)]
        mixf = [tensor(f"mixf{n}", [P, HC, BT], F32) for n in ("_kr", "_v", "_c")]
        av = tensor("av", [P, HC, BT], F32)
        stats = [tensor(f"stats{k}", [P, BJ, 6], F32) for k in range(2)]
        mv = [tensor(f"mv{k}", [P, BJ, 2], F32) for k in range(2)]
        rstd = [tensor(f"rstd{k}", [P, BJ], F32) for k in range(2)]
        big = tensor("big", [P, 3], F32)
        pw2 = tensor("pw2", [P, 3], F32)
        pwi = tensor("pwi", [P, 3], F32)
        scl = tensor("scl", [P, 3], F32)
        whi_at = place[0]
        whi = tensor("whi", [P, WALL], F32R)
        wlo = tensor("wlo", [P, WALL], F32R)
        assert E == KQ and EW == 3 * (EW // 3) and W3 == EW // 3 and W2 == 2 * (EW // 3)

        RING = 4
        place[0] = late
        x0 = [tensor(f"x0_{v}", [P, BJ, H], F32) for v in range(RING)]
        xq = [tensor(f"xq{v}", [P, BJ, H], F32) for v in range(RING)]
        before = tensor("before", [P, P], F32)
        down = tensor("down", [P, NJ, E], F32)
        logit = tensor("logit", [P, NJ, E], F32)
        assert place[0] <= early

        HG = 4
        NX = NT + 1
        place[0] = late + 3 * 4 * HC * BT
        onelo = [[tensor(f"onelo{u}{k}", [P, HG, P], F32R) for k in range(TOPK)] for u in range(2)]
        onehi = [[tensor(f"onehi{u}{k}", [P, HG, NX], F32) for k in range(TOPK)] for u in range(2)]
        hirow = [[tensor(f"hirow{u}{k}", [P, HG, 3, NX], F32R) for k in range(TOPK)] for u in range(2)]
        assert place[0] <= early

        ew = tensor_at("ew", [P, E * 2 * EW], F16, early)
        place[0] = late
        xthi = [tensor(f"xthi{u}", [P, H], F16) for u in range(2)]
        xtlo = [tensor(f"xtlo{u}", [P, H], F16) for u in range(2)]
        sa = [tensor(f"sa{u}", [P, F], F32) for u in range(2)]
        hh = [tensor(f"hh{u}", [P, F], F32) for u in range(2)]
        hhi = [tensor(f"hhi{u}", [P, F], F16) for u in range(2)]
        hlo = [tensor(f"hlo{u}", [P, F], F16) for u in range(2)]
        hthi = [tensor(f"hthi{u}", [P, F], F16) for u in range(2)]
        htlo = [tensor(f"htlo{u}", [P, F], F16) for u in range(2)]
        yb = [tensor(f"yb{u}", [P, H], F32) for u in range(2)]
        hmax = [tensor(f"hmax{u}", [P, 1], F32) for u in range(2)]
        hinv = [tensor(f"hinv{u}", [P, 1], F32) for u in range(2)]
        sidx = [tensor(f"sidx{u}", [P, 1], I32) for u in range(2)]
        assert place[0] <= early and early + E * 4 * EW <= whi_at

        at = late
        routes = {}

        def rt(name, shape, dt=F32):
            nonlocal at
            routes[name], at = sb("rt_" + name, shape, dt, at)
            return routes[name]

        ps = ctx.enter_context(nc.psum_tensor("ps", [P, 8, 512], F32))
        xn_d = nc.dram_tensor("xn_scratch", (T, H), F32, kind="Internal").ap()
        ew_d = nc.dram_tensor("ew_scratch", (E * P, 2 * EW), F16, kind="Internal").ap()

        def block_rows(d, b):
            return d[bass.ds(b * BT, BT), :].rearrange("(j p) n -> p j n", p=P)

        class Signal:
            def __init__(self, name, credit=0, step=1):
                self.sem = ctx.enter_context(nc.semaphore(name))
                self.credit, self.step = credit, step
                self.one = (self.sem, step)

            def at(self, n):
                return self.sem, (n + self.credit) * self.step

        def D(name, credit=0):
            return Signal(name, credit, 16)

        passed = Signal("passed")
        const_ld, const_ok = D("const_ld"), Signal("const_ok")
        n_ld = [D(f"n_ld{v}") for v in range(RING)]
        n_stats, n_mv, n_eps, n_rstd = Signal("n_stats"), Signal("n_mv"), Signal("n_eps"), Signal("n_rstd")
        n_xn = Signal("n_xn", 2)
        n_st = [D(f"n_st{v}", 1) for v in range(RING)]
        n_tp = Signal("n_tp", 4)
        n_xt = Signal("n_xt", 2)
        n_lg = Signal("n_lg", 2)
        n_logit = Signal("n_logit", 2)
        r_dve, r_act, r_pe = Signal("r_dve"), Signal("r_act"), Signal("r_pe")
        r_one = Signal("r_one")
        r_hot = Signal("r_hot")
        r_part = Signal("r_part")
        r_perm = Signal("r_perm", 2)
        r_slots = Signal("r_slots")
        r_ready = Signal("r_ready")
        wst_ld, wst_hi, wst_lo = [D(f"wst_ld{i}") for i in range(3)], Signal("wst_hi"), Signal("wst_lo")
        m_ldn = [D(f"m_ldn{u}") for u in range(2)]
        m_ldx = [D(f"m_ldx{u}") for u in range(2)]
        m_st = [D(f"m_st{u}") for u in range(2)]
        m_stats, m_mv, m_eps, m_rstd, m_hn, m_ht, m_dif = (
            [Signal(f"{n}{k}") for k in (1, 2)] for n in ("m_stats", "m_mv", "m_eps", "m_rstd", "m_hn", "m_ht", "m_dif"))
        m_tp = [Signal(f"m_tp{k}", 2) for k in (1, 2)]
        m_mix, m_high, m_low = ({m: Signal(f"{n}{m}", 2) for m in MIXES} for n in ("m_mix", "m_high", "m_low"))
        m_k, m_v, m_r, m_wo, m_cr = (Signal(n, 1) for n in ("m_k", "m_v", "m_r", "m_wo", "m_cr"))
        m_delta, m_exp, m_tr, m_wkv, m_av = (Signal(n, 1) for n in ("m_delta", "m_exp", "m_tr", "m_wkv", "m_av"))
        m_rw, m_rwhi, m_rwlo, m_x1, m_tc = (Signal(n, 1) for n in ("m_rw", "m_rwhi", "m_rwlo", "m_x1", "m_tc"))
        m_u, m_utp, m_x2, m_acc = (Signal(n, 1) for n in ("m_u", "m_utp", "m_x2", "m_acc"))
        m_kk, m_sk, m_sklo, m_val = Signal("m_kk", 1), Signal("m_sk", 1), Signal("m_sklo", 2), Signal("m_val", 3)
        w_ld, w_big, w_sum, w_top, w_pow, w_scl = (D("w_ld"), Signal("w_big"), Signal("w_sum"), Signal("w_top"),
                                                   Signal("w_pow"), Signal("w_scl"))
        w_inv = Signal("w_inv")
        w_hi, w_lo, w_st = Signal("w_hi"), Signal("w_lo"), D("w_st", 2)
        e_w = [D(f"e_w{e}") for e in range(E)]
        e_here = Signal("e_here")
        e_idx = Signal("e_idx")
        e_g = [D(f"e_g{u}") for u in range(2)]
        e_xtp = Signal("e_xtp", 2)
        e_xthi, e_xtlo = Signal("e_xthi"), Signal("e_xtlo", 1)
        e_up = Signal("e_up", 2)
        e_sa = Signal("e_sa")
        e_h = Signal("e_h", 2)
        e_max, e_inv, e_hhi, e_hlo = Signal("e_max"), Signal("e_inv", 2), Signal("e_hhi"), Signal("e_hlo", 2)
        e_htp = Signal("e_htp", 2)
        e_hthi, e_htlo = Signal("e_hthi", 1), Signal("e_htlo", 1)
        e_dn = Signal("e_dn", 2)
        e_y = Signal("e_y", 2)
        e_to = Signal("e_to")
        e_add = D("e_add")
        e_added = Signal("e_added", 2)
        o_zero, zeros = D("o_zero"), Signal("zeros")

        def credit(eng, *signals):
            for s in signals:
                eng.sem_inc(s.sem, s.credit * s.step)

        def tile_after(s, u, n):
            return s + (u + n) // 2, (u + n) % 2

        def tiles(eng, step, ahead, rounds=None, rest=True):
            every = (NT - ahead) // UNROLL
            with eng.Fori(*(rounds or (0, every))) as s:
                for i in range(UNROLL):
                    step(UNROLL // 2 * s + i // 2, i % 2, ahead)
            for i in range(UNROLL * every, NT) if rest else ():
                step(i // 2, i % 2, min(ahead, NT - 1 - i))

        def periods(eng, step):
            for p in (-1, 0, 1):
                step(p // 2, p % 2)
            with eng.Fori(1, NB // 2 - 1) as s:
                step(s, 0)
                step(s, 1)
            for p in range(NB - 2, NB + 2):
                step(p // 2, p % 2)

        def there(b):
            return not isinstance(b, int) or 0 <= b < NB

        def at_period(p, n):
            return isinstance(p, int) and p == n

        def alone(eng):
            eng.sem_inc(passed.sem, 1)

        CH = EW
        chunks = [(a, min(CH, WALL - a)) for a in range(0, WALL, CH)]
        stage_flat = stage[:, :, :].rearrange("p a b -> p (a b)")
        stages = (stage_flat, stage_b[:, :])

        def each(column, n):
            return column.unsqueeze(2).to_broadcast([P, HG, n])

        def to_each(row, n):
            return row.unsqueeze(1).to_broadcast([P, HG, n])

        hif, lof = rt("hif", [P, TOPK * NJ]), rt("lof", [P, TOPK * NJ])
        ghi, glo = rt("ghi", [P, TOPK, NJ], F32R), rt("glo", [P, TOPK, NJ], F32R)
        m1, m2 = rt("m1", [P, NJ]), rt("m2", [P, NJ])
        eq, iv, mx = rt("eq", [P, NJ, E]), rt("iv", [P, NJ, E]), rt("mx", [P, NJ])
        oh = [rt("oh0", [P, NJ, E]), rt("oh1", [P, NJ, E])]
        l2 = rt("l2", [P, NJ, E])
        labs, fac, df, keep = (rt(n, [P, NJ, E]) for n in ("labs", "fac", "df", "keep"))
        dfk = [rt(f"df{k}", [P, NJ, E]) for k in range(TOPK)]
        exk = [rt(f"ex{k}", [P, NJ, E]) for k in range(TOPK)]
        den = rt("den", [P, NJ])
        cc, tote, scan, pos, tmp = (rt(n, [P, NJ * E]) for n in ("cc", "tote", "scan", "pos", "tmp"))
        cnt, padf, pinc, dlt = (rt(n, [P, E]) for n in ("cnt", "padf", "pinc", "dlt"))
        cnti = rt("cnti", [P, E], I32)
        slotf = rt("slotf", [P, TOPK * NJ])
        slot, hii = rt("slot", [P, TOPK * NJ], I32), rt("hii", [P, TOPK * NJ], I32)
        gain = rt("gain", [P, TOPK, NJ])
        assert at <= late + 2 * RING * 4 * BJ * H

        block = ctx.enter_context(nc.Block())

        @block.sync
        def _(sp):
            credit(sp, *n_st, w_st)

            def load_chunk(i):
                a, n = chunks[i]
                sp.dma_start(stages[i % 2][:, 0:n], wmix[:, a:a + n]).then_inc(*wst_ld[i].one)

            for v in range(RING):
                sp.dma_start(x0[v][:], block_rows(x, v)).then_inc(*n_ld[v].one)
                if v == 0:
                    sp.dma_start(vec[:], vecs).then_inc(*const_ld.one)
                    sp.dma_start(gw[:], gate).then_inc(*const_ld.one)
                if v == 1:
                    load_chunk(0)
            load_chunk(1)
            sp.wait_ge(*zeros.at(1))
            sp.dma_start(out[T:T + P, :], hn[:, 0, :]).then_inc(*o_zero.one)

            def norm_io(g, v, last):
                sp.wait_ge(*n_xn.at(g + 1))
                alone(sp)
                sp.dma_start(block_rows(xn_d, g), xq[v][:]).then_inc(*n_st[v].one)
                if not last:
                    sp.dma_start(x0[v][:], block_rows(x, g + RING)).then_inc(*n_ld[v].one)

            with sp.Fori(0, NB // RING - 1) as s:
                for v in range(RING):
                    norm_io(RING * s + v, v, False)
            for v in range(RING):
                norm_io(NB - RING + v, v, True)

            for u in range(2):
                sp.dma_start(xx[u][:], block_rows(x, u)).then_inc(*m_ldx[u].one)
            for v in range(RING):
                sp.wait_ge(*n_st[v].at(NB // RING))
            for u in range(2):
                sp.dma_start(xn[u][:], block_rows(xn_d, u)).then_inc(*m_ldn[u].one)
            for i in range(2, len(chunks)):
                sp.wait_ge(*wst_lo.at(i - 1))
                load_chunk(i)
            sp.wait_ge(*wst_lo.at(len(chunks)))
            sp.dma_start(stage_flat, wexp[0:P, :]).then_inc(*w_ld.one)

            EARLY = 5

            def load_expert(e):
                for a in (0, EW):
                    sp.dma_start(ew[:, e * 2 * EW + a:e * 2 * EW + a + EW],
                                 ew_d[e * P:(e + 1) * P, a:a + EW]).then_inc(*e_w[e].one)

            def mix_io(s, u):
                p = 2 * s + u
                if there(p - 2):
                    sp.wait_ge(*m_x2.at(p - 1))
                    alone(sp)
                    sp.dma_start(block_rows(out, p - 2), xx[u][:]).then_inc(*m_st[u].one)
                    if there(p):
                        sp.wait_ge(*m_st[u].at(s))
                        alone(sp)
                        sp.dma_start(xx[u][:], block_rows(x, p)).then_inc(*m_ldx[u].one)
                if at_period(p, NB):
                    sp.wait_ge(*w_st.at(2 * E))
                    sp.wait_ge(*m_wo.at(NB))
                    sp.wait_ge(*m_low[CMK].at(NB))
                    sp.wait_ge(*m_acc.at(NB))
                    for e in range(EARLY):
                        load_expert(e)
                if there(p) and there(p + 2):
                    sp.wait_ge(*m_hn[1].at(p + 1))
                    alone(sp)
                    sp.wait_ge(*m_acc.at(p + 1))
                    alone(sp)
                    sp.dma_start(xn[u][:], block_rows(xn_d, p + 2)).then_inc(*m_ldn[u].one)
                if there(p):
                    sp.wait_ge(*w_lo.at(p + 1))
                    alone(sp)
                    sp.dma_start(ew_d[bass.ds(p * P, P), 0:EW],
                                 ehi[:, :, :].rearrange("p a b -> p (a b)")).then_inc(*w_st.one)
                    sp.dma_start(ew_d[bass.ds(p * P, P), EW:2 * EW],
                                 elo[:, :, :].rearrange("p a b -> p (a b)")).then_inc(*w_st.one)
                    if there(p + 1):
                        sp.dma_start(stage_flat, wexp[bass.ds((p + 1) * P, P), :]).then_inc(*w_ld.one)

            periods(sp, mix_io)
            for e in range(E):
                sp.wait_ge(*e_w[e].at(2))
                sp.sem_inc(e_here.sem, 1)
                if EARLY - 1 <= e < E - 1:
                    load_expert(e + 1)

        @block.gpsimd
        def _(pool):
            credit(pool, m_wkv, m_acc, e_added, *(m_low[m] for m in (MV, MR, CMR, CMK)))
            n_const = 0
            for t, v in ((halfneg[:], -0.5), (id32[:], 0.0), (id16[:], 0.0), (before[:], 0.0), (ones[:], 1.0),
                         (hn[:, 0, :], 0.0), (ht[0][:, :, 0:1], 0.0), (h2t[0][:, :, 0:1], 0.0)):
                pool.memset(t, v).then_inc(*const_ok.one)
                n_const += 1
            for t, pattern, base, by in ((lane, [[1, P]], 0, 0), (tokid, [[P, NJ]], 1, 1), (spare, [[0, 1]], T + 1, 1),
                                         (tile0, [[P, NT]], 0, 0), (down, [[0, NJ], [-1, E]], E, 0)):
                pool.iota(t[:], pattern=pattern, base=base, channel_multiplier=by,
                          allow_small_or_imprecise_dtypes=True).then_inc(*const_ok.one)
                n_const += 1
            pool.wait_ge(*const_ok.at(n_const))
            pool.sem_inc(zeros.sem, 1)
            for m in (id32, id16):
                pool.affine_select(out=m[:], in_=m[:], compare_op=ALU.not_equal, fill=1.0, base=0,
                                   pattern=[[-1, P]], channel_multiplier=1).then_inc(*const_ok.one)
            pool.affine_select(out=before[:], in_=before[:], compare_op=ALU.is_ge, fill=1.0, base=0,
                               pattern=[[-1, P]], channel_multiplier=1).then_inc(*const_ok.one)
            assert n_const + 3 == N_CONST

            def rstd_of(k, var, eps, done, n):
                pool.wait_ge(*var.at(n))
                alone(pool)
                pool.tensor_scalar(rstd[k][:], mv[k][:, :, 1:2].rearrange("p a b -> p (a b)"), EPS, None,
                                   ALU.add).then_inc(*eps.one)
                pool.wait_ge(*eps.at(n))
                pool.tensor_tensor(rstd[k][:], rstd[k][:], halfneg[:], ALU.pow).then_inc(*done.one)

            with pool.Fori(0, NB // 2) as s:
                for u in range(2):
                    rstd_of(u, n_mv, n_eps, n_rstd, 2 * s + u + 1)

            def weights_low(i):
                a, n = chunks[i]
                pool.wait_ge(*wst_hi.at(i + 1))
                pool.tensor_tensor(wlo[:, a:a + n], stages[i % 2][:, 0:n], whi[:, a:a + n].bitcast(F32),
                                   ALU.subtract).then_inc(*wst_lo.one)

            weights_low(0)
            weights_low(1)

            def hot_gains(g):
                u = g % 2
                pool.wait_ge(*r_one.at(g + 1))
                for k in range(TOPK):
                    for part, t in enumerate((ghi, glo)):
                        last = pool.tensor_tensor(hirow[u][k][:, :, part + 1, :], onehi[u][k][:],
                                                  each(t[:, k, bass.ds(g * HG, HG)].bitcast(F32), NX), ALU.mult)
                last.then_inc(*r_part.one)

            def shifted(k, t, u, b):
                pool.wait_ge(*m_ht[k].at(b + 1))
                pool.tensor_tensor(dif[:], t[u][:, :, 1:BT + 1], t[u][:, :, 0:BT],
                                   ALU.subtract).then_inc(*m_dif[k].one)

            def low_pool(m, b, dst, hi):
                pool.wait_ge(*m_high[m].at(b + 1))
                pool.tensor_tensor(dst[:], mixf[AT[m]][:], hi[:].bitcast(F32), ALU.subtract).then_inc(*m_low[m].one)

            def mix_pool(s, u):
                p = 2 * s + u
                first, second = at_period(p, -1), at_period(p, 0)
                if there(p + 1):
                    rstd_of(0, m_mv[0], m_eps[0], m_rstd[0], p + 2)
                if second:
                    hot_gains(0)
                    hot_gains(1)
                if there(p):
                    rstd_of(1, m_mv[1], m_eps[1], m_rstd[1], p + 1)
                if second:
                    hot_gains(2)
                if there(p + 1):
                    pool.wait_ge(*m_mix[CMK].at(p))
                    shifted(0, ht, 1 - u, p + 1)
                if second:
                    hot_gains(3)
                if there(p):
                    pool.wait_ge(*m_ldx[u].at(s + 1))
                    pool.wait_ge(*m_x1.at(p + 1))
                    pool.tensor_tensor(xx[u][:], xx[u][:], xn[u][:], ALU.add).then_inc(*m_acc.one)
                if there(p + 1):
                    pool.wait_ge(*m_wo.at(p + 1))
                    low_pool(MV, p + 1, flo[1], fhi[1])
                if first:
                    weights_low(2)
                if there(p):
                    if there(p + 1):
                        pool.wait_ge(*m_mix[MR].at(p + 2))
                    pool.wait_ge(*m_mix[CMK].at(p))
                    shifted(1, h2t, u, p)
                if there(p + 1) and not first and not second:
                    low_pool(MR, p + 1, flo[0], fhi[0])
                if second:
                    hot_gains(4)
                    hot_gains(5)
                if there(p) and not second:
                    pool.wait_ge(*m_cr.at(p))
                    low_pool(CMR, p, clo[1], chi[1])
                if there(p + 1):
                    pool.wait_ge(*m_av.at(p + 2))
                    pool.tensor_tensor(av[:], av[:], rb[:], ALU.mult).then_inc(*m_wkv.one)
                if second:
                    hot_gains(6)
                    hot_gains(7)
                    pool.wait_ge(*r_perm.at(NJ // HG))
                    low_pool(CMR, p, clo[1], chi[1])
                if there(p):
                    pool.wait_ge(*m_kk.at(KQ * p))
                    low_pool(CMK, p, clo[0], chi[0])

            periods(pool, mix_pool)

            def row_of_slot(i, idx, of, signal, n):
                pool.tensor_copy(idx[:], of[:, bass.ds(i, 1)]).then_inc(*signal.one)
                pool.wait_ge(*signal.at(n))
                alone(pool)
                return bass.IndirectOffsetOnAxis(ap=idx[:].bitcast(U32), axis=0)

            def gather_slots(s, u):
                i = 2 * s + u
                pool.wait_ge(*e_xtp.at(i - 1))
                alone(pool)
                rows = row_of_slot(i, gidx[u], slot_from, e_idx, i + 1)
                pool.indirect_dma_start(out=xg[u][:], out_offset=None, in_=xn_d,
                                        in_offset=rows).then_inc(*e_g[u].one)

            def add_slots(s, u):
                i = 2 * s + u
                pool.wait_ge(*e_y.at(i + 1))
                alone(pool)
                rows = row_of_slot(i, sidx[u], slot_to, e_to, i + 1)
                pool.indirect_dma_start(out=out, out_offset=rows, in_=yb[u][:], in_offset=None,
                                        compute_op=ALU.add).then_inc(*e_add.one)

            pool.wait_ge(*r_slots.at(1))
            AHEAD = 5
            for i in range(AHEAD):
                gather_slots(i // 2, i % 2)
            for u in range(2):
                pool.wait_ge(*m_st[u].at(NB // 2))
            pool.wait_ge(*o_zero.at(1))

            def step_pool(s, u, left):
                add_slots(s, u)
                if left == AHEAD:
                    gather_slots(*tile_after(s, u, AHEAD))
                pool.wait_ge(*e_add.at(2 * s + u + 1))
                pool.sem_inc(e_added.sem, 1)

            tiles(pool, step_pool, AHEAD)

        @block.scalar
        def _(act):
            credit(act, n_xt, n_logit, m_exp, m_tr, m_rwhi, m_tc, m_sk, e_hthi, e_y, *m_high.values())

            def weights_high(i):
                a, n = chunks[i]
                act.wait_ge(*wst_ld[i].at(1))
                act.activation(whi[:, a:a + n], stages[i % 2][:, 0:n], ACT.Copy).then_inc(*wst_hi.one)

            weights_high(0)

            def norm_turned(g, u):
                act.wait_ge(*n_tp.at(g + 1))
                act.wait_ge(*n_lg.at(g - 1))
                act.activation((e2, rb)[u][:], ps[:, 2 * u:2 * u + 2, :], ACT.Copy).then_inc(*n_xt.one)

            def norm_logits(g, u):
                act.wait_ge(*n_lg.at(g + 1))
                act.activation(logit[:, bass.ds(g * BJ, BJ), :],
                               ps[:, 4 + u, 0:BJ * E].rearrange("p (a b) -> p a b", a=BJ),
                               ACT.Copy).then_inc(*n_logit.one)

            for s in range(NB // RING):
                norm_turned(RING * s, 0)
                for v in range(1, RING):
                    norm_turned(RING * s + v, v % 2)
                    norm_logits(RING * s + v - 1, (v - 1) % 2)
                norm_logits(RING * s + RING - 1, (RING - 1) % 2)
                if s == 0:
                    weights_high(1)

            def route_exp(k):
                act.wait_ge(*r_dve.at(R_EXP[k]))
                act.activation(exk[k][:], dfk[k][:], ACT.Exp, scale=-1.0).then_inc(*r_act.one)

            def turned(k, t, b, u, bank, g, bb):
                act.wait_ge(*m_tp[k].at(b + 1))
                for c in range(HC):
                    last = act.activation(t[u][:, c, 1:BT + 1], ps[:, bank + c, :], ACT.Identity,
                                          scale=vec[:, c, g:g + 1], bias=vec[:, c, bb:bb + 1])
                if u == 1:
                    last = act.activation(t[1][:, :, 0:1], t[0][:, :, BT:BT + 1], ACT.Copy)
                last.then_inc(*m_ht[k].one)

            def high(m, b, dst):
                act.wait_ge(*m_mix[m].at(b + 1))
                act.activation(dst[:], mixf[AT[m]][:], ACT.Copy).then_inc(*m_high[m].one)

            def mix_act(s, u):
                p = 2 * s + u

                def keys(*qs):
                    for q in qs if there(p - 1) else ():
                        n = KQ * (p - 1) + q
                        act.wait_ge(*m_kk.at(n + 1))
                        act.wait_ge(*m_val.at(n - min(q, 2)))
                        act.activation(skhi[q % 3][:], ps[:, 6 + q % 2, :], ACT.Silu)
                        act.wait_ge(*m_sklo.at(n - 1))
                        act.activation(skf[q % 2][:], ps[:, 6 + q % 2, :], ACT.Silu).then_inc(*m_sk.one)

                def expert_high(k):
                    if there(p):
                        if k == 0:
                            act.wait_ge(*w_scl.at(p + 1))
                            act.wait_ge(*w_st.at(2 * p))
                        act.activation(ehi[:, k, :], stage[:, k, :], ACT.Copy,
                                       scale=scl[:, k:k + 1]).then_inc(*w_hi.one)

                if there(p - 1):
                    act.wait_ge(*m_cr.at(p))
                    act.wait_ge(*m_u.at(p - 1))
                    act.activation(tc[:], ps[:, 6:8, :], ACT.Tanh, scale=0.5).then_inc(*m_tc.one)
                keys(0, 1)
                if there(p + 1):
                    turned(0, ht, p + 1, 1 - u, 2, LG1, LB1)
                if at_period(p, -1):
                    route_exp(0)
                keys(2, 3)
                if there(p + 1):
                    act.wait_ge(*m_r.at(p + 1))
                    high(MK, p + 1, fhi[0])
                if there(p):
                    turned(1, h2t, p, u, 4, LG2, LB2)
                keys(4)
                if there(p + 1):
                    act.wait_ge(*m_wo.at(p + 1))
                    high(MV, p + 1, fhi[1])
                if at_period(p, -1):
                    route_exp(1)
                    weights_high(2)
                if there(p + 1):
                    act.wait_ge(*m_k.at(p + 2))
                    high(MR, p + 1, fhi[0])
                if there(p + 1):
                    act.wait_ge(*m_delta.at(p + 2))
                    act.wait_ge(*m_wkv.at(p + 1))
                    act.activation(rb[:], e2[:], ACT.Exp, scale=-1.0)
                    act.activation(e2[:], e2[:], ACT.Exp).then_inc(*m_exp.one)
                keys(5)
                if there(p):
                    act.wait_ge(*m_cr.at(p))
                    high(CMR, p, chi[1])
                keys(6)
                expert_high(0)
                expert_high(1)
                if there(p + 1):
                    act.wait_ge(*m_av.at(p + 2))
                    act.wait_ge(*m_r.at(p + 2))
                    act.activation(e2[:], ps[:, 4:6, :], ACT.Tanh, scale=0.5).then_inc(*m_tr.one)
                keys(7)
                if there(p + 1):
                    act.wait_ge(*m_rw.at(p + 2))
                    act.activation(fhi[1][:], av[:], ACT.Copy).then_inc(*m_rwhi.one)
                expert_high(2)
                if there(p):
                    act.wait_ge(*m_kk.at(KQ * p))
                    high(CMK, p, chi[0])

            periods(act, mix_act)

            def x_act(s, u):
                i = 2 * s + u
                act.wait_ge(*e_xtp.at(i + 1))
                act.wait_ge(*e_up.at(i - 1))
                act.activation(xthi[u][:], ps[:, 6, 0:H], ACT.Copy, scale=XS).then_inc(*e_xthi.one)

            def silu_act(s, u):
                i = 2 * s + u
                act.wait_ge(*e_up.at(i + 1))
                act.wait_ge(*e_h.at(i - 1))
                act.activation(sa[u][:], ps[:, 3 - 2 * u, :], ACT.Silu,
                               scale=unx[:, bass.ds(i, 1)]).then_inc(*e_sa.one)

            def hidden_act(s, u):
                i = 2 * s + u
                act.wait_ge(*e_inv.at(i + 1))
                act.wait_ge(*e_htp.at(i - 1))
                act.activation(hhi[u][:], hh[u][:], ACT.Copy, scale=hinv[u][:]).then_inc(*e_hhi.one)

            def y_act(s, u):
                i = 2 * s + u
                act.wait_ge(*e_dn.at(i + 1))
                act.wait_ge(*e_added.at(i - 1))
                act.activation(yb[u][:], ps[:, 7, 0:H], ACT.Copy, scale=yscl[:, bass.ds(i, 1)]).then_inc(*e_y.one)

            def step_act(s, u, left):
                i = 2 * s + u
                act.wait_ge(*e_htp.at(i + 1))
                act.wait_ge(*e_dn.at(i - 1))
                act.activation(hthi[u][:], ps[:, 5, :].bitcast(F16)[:, 0:F], ACT.Copy).then_inc(*e_hthi.one)
                if left >= 1:
                    hidden_act(*tile_after(s, u, 1))
                if left >= 2:
                    silu_act(*tile_after(s, u, 2))
                if left >= 3:
                    x_act(*tile_after(s, u, 3))
                y_act(s, u)

            act.wait_ge(*r_ready.at(1))
            x_act(0, 0)
            x_act(0, 1)
            silu_act(0, 0)
            hidden_act(0, 0)
            silu_act(0, 1)
            x_act(1, 0)
            tiles(act, step_act, 3)

        @block.vector
        def _(dve):
            credit(dve, n_xn, m_delta, m_av, m_rw, m_rwlo, m_x1, m_u, m_x2, m_sklo, *m_mix.values(), m_low[MK],
                   e_inv, e_hlo, e_h, e_xtlo, e_htlo)
            dve.wait_ge(*const_ok.at(N_CONST))
            dve.wait_ge(*const_ld.at(2))
            steps = [0]

            def done(ins):
                steps[0] += 1
                ins.then_inc(*r_dve.one)
                dve.wait_ge(*r_dve.at(steps[0]))

            def spread(k, src, s_stats, s_mv, n):
                for j in range(BJ):
                    last = dve.bn_stats(stats[k][:, j, :], src[:, j, :])
                last.then_inc(*s_stats.one)
                dve.wait_ge(*s_stats.at(n))
                alone(dve)
                for j in range(BJ):
                    last = dve.bn_aggr(mv[k][:, j, :], stats[k][:, j, :])
                last.then_inc(*s_mv.one)

            def normalise(k, src, dst, s_rstd, n, s_dst):
                dve.wait_ge(*s_rstd.at(n))
                for j in range(BJ):
                    last = dve.tensor_scalar(dst[:, j, :], src[:, j, :], mv[k][:, j, 0:1], rstd[k][:, j:j + 1],
                                             ALU.subtract, ALU.mult)
                last.then_inc(*s_dst.one)

            def norm_spread(g, s, v):
                dve.wait_ge(*n_ld[v].at(s + 1))
                dve.wait_ge(*n_xn.at(g - 1))
                spread(v % 2, x0[v], n_stats, n_mv, g + 1)

            def norm_out(g, s, v):
                dve.wait_ge(*n_st[v].at(s))
                dve.wait_ge(*n_tp.at(g - 3))
                normalise(v % 2, x0[v], xq[v], n_rstd, g + 1, n_xn)

            with dve.Fori(0, NB // RING) as s:
                norm_spread(RING * s, s, 0)
                for v in range(1, RING):
                    norm_spread(RING * s + v, s, v)
                    norm_out(RING * s + v - 1, s, v - 1)
                norm_out(RING * s + RING - 1, s, RING - 1)

            done(dve.tensor_scalar(tfp[:], vec[:, :, TF:TF + 1].rearrange("p a b -> p (a b)"), PP0, None, ALU.add))

            def wide(t):
                return t[:, :].unsqueeze(2).to_broadcast([P, NJ, E])

            def flat(t):
                return t[:, :, :].rearrange("p a b -> p (a b)")

            def route_pick(k):
                top, of = ((m1, logit), (m2, l2))[k]
                if k == 0:
                    dve.wait_ge(*n_logit.at(NB))
                    for v in range(RING):
                        dve.wait_ge(*n_st[v].at(NB // RING))
                    done(dve.scalar_tensor_tensor(flat(labs), flat(logit), -1.0, flat(logit), ALU.mult, ALU.max))
                done(dve.tensor_reduce(top[:], of[:], AX.X, ALU.max))
                done(dve.tensor_tensor(eq[:], of[:], wide(top), ALU.is_equal))
                done(dve.tensor_tensor(iv[:], eq[:], down[:], ALU.mult))
                done(dve.tensor_reduce(mx[:], iv[:], AX.X, ALU.max))
                done(dve.tensor_tensor(oh[k][:], iv[:], wide(mx), ALU.is_equal))
                done(dve.tensor_tensor(fac[:], labs[:], wide(top), ALU.max))
                done(dve.tensor_tensor(df[:], wide(top), logit[:], ALU.subtract))
                done(dve.scalar_tensor_tensor(flat(keep), flat(fac), JITTER, flat(df), ALU.mult, ALU.is_ge))
                if k == 0:
                    done(dve.scalar_tensor_tensor(flat(l2), flat(oh[0]), -3e38, flat(logit), ALU.mult, ALU.add))
                done(dve.tensor_tensor(dfk[k][:], wide(top), of[:], ALU.subtract))
                assert steps[0] == R_EXP[k], steps

            def route_gain(k):
                dve.wait_ge(*r_act.at(k + 1))
                done(dve.tensor_tensor(exk[k][:], exk[k][:], keep[:], ALU.mult))
                done(dve.tensor_reduce(den[:], exk[k][:], AX.X, ALU.add))
                done(dve.reciprocal(gain[:, k, :], den[:]))
                if k == TOPK - 1:
                    done(dve.tensor_tensor(cc[:], flat(oh[0]), flat(oh[1]), ALU.add))
                    assert steps[0] == R_PICKS, steps

            by_e = lambda t: t.rearrange("p (j e) -> p e j", e=E)

            def route_bases():
                dve.wait_ge(*r_pe.at(1))
                done(dve.tensor_copy(tote[:, :].rearrange("p (e j) -> p e j", e=E), by_e(ps[:, 7, 0:NJ * E])))
                done(dve.tensor_tensor_scan(scan[:], ones[:], tote[:], 0.0, ALU.mult, ALU.add))
                done(dve.tensor_tensor(pos[:], scan[:], tote[:], ALU.subtract))
                s_ej, p_ej = (t[:, :].rearrange("p (e j) -> p e j", e=E) for t in (scan, pos))
                last_of = s_ej[:, :, NJ - 1:NJ].rearrange("p a b -> p (a b)")
                first_of = p_ej[:, :, 0:1].rearrange("p a b -> p (a b)")
                done(dve.tensor_tensor(cnt[:], last_of, first_of, ALU.subtract))
                done(dve.tensor_scalar(cnti[:], cnt[:], float(P - 1), None, ALU.add))
                done(dve.tensor_scalar(cnti[:], cnti[:], 7, 7, ALU.logical_shift_right, ALU.logical_shift_left))
                done(dve.tensor_copy(padf[:], cnti[:]))
                done(dve.tensor_tensor_scan(pinc[:], ones[:, 0:E], padf[:], 0.0, ALU.mult, ALU.add))
                done(dve.tensor_tensor(pbx[:], pinc[:], padf[:], ALU.subtract))
                done(dve.tensor_tensor(dlt[:], pbx[:], first_of, ALU.subtract))
                done(dve.tensor_tensor(p_ej, p_ej, dlt[:, :].unsqueeze(2).to_broadcast([P, E, NJ]), ALU.add))

            def route_slots():
                done(dve.tensor_tensor(tmp[:, :].rearrange("p (j e) -> p j e", e=E),
                                       ps[:, 6, 0:NJ * E].rearrange("p (j e) -> p j e", e=E),
                                       pos[:, :].rearrange("p (e j) -> p j e", e=E), ALU.add))
                for k in range(TOPK):
                    done(dve.tensor_tensor(cc[:], tmp[:], flat(oh[k]), ALU.mult))
                    done(dve.tensor_reduce(slotf[:, k * NJ:(k + 1) * NJ],
                                           cc[:, :].rearrange("p (j e) -> p j e", e=E), AX.X, ALU.add))
                done(dve.tensor_copy(slot[:], slotf[:]))
                done(dve.tensor_scalar(hii[:], slot[:], 7, None, ALU.logical_shift_right))
                done(dve.tensor_copy(hif[:], hii[:]))
                done(dve.scalar_tensor_tensor(lof[:], hif[:], -float(P), slotf[:], ALU.mult, ALU.add))
                done(dve.tensor_copy(ghi[:], gain[:]))
                done(dve.tensor_tensor(glo[:], gain[:], ghi[:].bitcast(F32), ALU.subtract))

            def route_experts():
                done(dve.tensor_scalar(tile_exp[:], tile0[:], pbx[:, 1:2], None, ALU.is_ge))
                for e in range(2, E):
                    done(dve.scalar_tensor_tensor(tile_exp[:], tile0[:], pbx[:, e:e + 1], tile_exp[:],
                                                  ALU.is_ge, ALU.add))
                done(dve.tensor_scalar(tile_off[:], tile_exp[:], 2.0 * EW, None, ALU.mult))
                done(dve.tensor_scalar(tile_need[:], tile_exp[:], 1.0, None, ALU.add))

            def hot(g):
                u = g % 2
                dve.wait_ge(*r_perm.at(g - 1))
                for k in range(TOPK):
                    last = dve.tensor_tensor(onehi[u][k][:], to_each(lane[:, 0:NX], NX),
                                             each(hif[:, bass.ds(k * NJ + g * HG, HG)], NX), ALU.is_equal)
                last.then_inc(*r_one.one)
                for k in range(TOPK):
                    dve.tensor_tensor(onelo[u][k][:], to_each(lane[:, :], P),
                                      each(lof[:, bass.ds(k * NJ + g * HG, HG)], P), ALU.is_equal)
                dve.wait_ge(*r_one.at(g + 1))
                for k in range(TOPK):
                    last = dve.tensor_tensor(hirow[u][k][:, :, 0, :], onehi[u][k][:],
                                             each(tokid[:, bass.ds(g * HG, HG)], NX), ALU.mult)
                last.then_inc(*r_hot.one)

            def route_rows():
                tok1, empty = unx, uny
                dve.wait_ge(*r_perm.at(NJ // HG))
                done(dve.tensor_copy(slot_gain[:], ps[:, 7, NX:NX + NT]))
                done(dve.tensor_tensor(slot_gain[:], slot_gain[:], ps[:, 7, 2 * NX:2 * NX + NT], ALU.add))
                done(dve.tensor_copy(tok1[:], ps[:, 7, 0:NT]))
                done(dve.tensor_scalar(slot_from[:], tok1[:], -1.0, 0.0, ALU.add, ALU.max))
                done(dve.tensor_scalar(empty[:], tok1[:], 0.0, spare[:], ALU.is_equal, ALU.mult))
                done(dve.scalar_tensor_tensor(slot_to[:], tok1[:], -1.0, empty[:], ALU.add, ALU.add))
                dve.sem_inc(r_slots.sem, 1)

            def mixed(m, b, k, h):
                dve.wait_ge(*m_dif[k].at(b + 1))
                for c in range(HC):
                    last = dve.scalar_tensor_tensor(mixf[AT[m]][:, c, :], dif[:, c, :], vec[:, c, m:m + 1],
                                                    h[:, c, 0:BT], ALU.mult, ALU.add)
                last.then_inc(*m_mix[m].one)

            def low(m, b, dst, hi):
                dve.wait_ge(*m_high[m].at(b + 1))
                dve.tensor_tensor(dst[:], mixf[AT[m]][:], hi[:].bitcast(F32), ALU.subtract).then_inc(*m_low[m].one)

            def scales(e):
                if e == 0:
                    dve.memset(unx[:], 0.0)
                    done(dve.memset(uny[:], 0.0))
                    done(dve.tensor_tensor(un32[:], unscale[:, :, 1:2].rearrange("p a b -> p (a b)"),
                                           unscale[:, :, 2:3].rearrange("p a b -> p (a b)"), ALU.mult))
                for dst, by in ((unx, unscale[:, e, 0:1]), (uny, un32[:, e:e + 1])):
                    done(dve.tensor_scalar(picked[:], tile_exp[:], float(e), by, ALU.is_equal, ALU.mult))
                    done(dve.scalar_tensor_tensor(dst[:], picked[:], 1.0 / XS, dst[:], ALU.mult, ALU.add))
                if e == E - 1:
                    dve.tensor_tensor(uny[:], uny[:], slot_gain[:], ALU.mult).then_inc(*r_ready.one)

            def x_dve(s, u):
                i = 2 * s + u
                dve.wait_ge(*e_xthi.at(i + 1))
                dve.wait_ge(*e_up.at(i - 1))
                dve.scalar_tensor_tensor(xtlo[u][:], ps[:, 6, 0:H], XS, xthi[u][:], ALU.mult,
                                         ALU.subtract).then_inc(*e_xtlo.one)

            def mix_dve(s, u):
                p = 2 * s + u
                first, second = at_period(p, -1), at_period(p, 0)

                def keys(*qs):
                    for q in qs if there(p - 1) else ():
                        n = KQ * (p - 1) + q
                        dve.wait_ge(*m_sk.at(n + 1))
                        dve.wait_ge(*m_val.at(n - min(q, 2)))
                        dve.tensor_tensor(sklo[q % 3][:], skf[q % 2][:], skhi[q % 3][:].bitcast(F32),
                                          ALU.subtract).then_inc(*m_sklo.one)
                        if at_period(p, NB):
                            scales(q)

                def expert_low(k):
                    if there(p):
                        dve.wait_ge(*w_hi.at(3 * p + k + 1))
                        last = dve.scalar_tensor_tensor(elo[:, k, :], stage[:, k, :], scl[:, k:k + 1],
                                                        ehi[:, k, :], ALU.mult, ALU.subtract)
                        if k == 2:
                            last.then_inc(*w_lo.one)

                if there(p - 2):
                    dve.wait_ge(*m_tc.at(p - 1))
                    dve.wait_ge(*m_val.at(KQ * (p - 1)))
                    dve.wait_ge(*m_utp.at(p - 2))
                    dve.scalar_tensor_tensor(uu[:], tc[:], 1.0, ps[:, 0:2, :], ALU.add, ALU.mult).then_inc(*m_u.one)
                if at_period(p, NB + 1):
                    x_dve(0, 0)
                if there(p + 1):
                    dve.wait_ge(*m_ldn[1 - u].at(s + 1 + u))
                    spread(0, xn[1 - u], m_stats[0], m_mv[0], p + 2)
                if second:
                    hot(0)
                    hot(1)
                if there(p):
                    dve.wait_ge(*m_wo.at(p + 1))
                    dve.tensor_tensor(xn[u][:], rows(2), xn[u][:], ALU.add).then_inc(*m_x1.one)
                if there(p + 1):
                    dve.wait_ge(*m_tp[1].at(p))
                    normalise(0, xn[1 - u], hn, m_rstd[0], p + 2, m_hn[0])
                if first:
                    route_pick(0)
                if there(p - 2):
                    dve.wait_ge(*m_utp.at(p - 1))
                    dve.wait_ge(*m_acc.at(p - 1))
                    dve.scalar_tensor_tensor(xx[u][:], rows(0), 0.5, xx[u][:], ALU.mult, ALU.add).then_inc(*m_x2.one)
                if there(p):
                    dve.wait_ge(*m_x1.at(p + 1))
                    spread(1, xn[u], m_stats[1], m_mv[1], p + 1)
                if second:
                    hot(2)
                keys(0)
                if there(p):
                    if there(p + 1):
                        dve.wait_ge(*m_tp[0].at(p + 2))
                    dve.wait_ge(*m_tp[1].at(p))
                    normalise(1, xn[u], hn, m_rstd[1], p + 1, m_hn[1])
                if second:
                    hot(3)
                keys(1)
                if there(p + 1):
                    dve.wait_ge(*m_low[MR].at(p + 1))
                    mixed(MK, p + 1, 0, ht[1 - u])
                    dve.wait_ge(*m_low[MV].at(p + 1))
                    mixed(MV, p + 1, 0, ht[1 - u])
                keys(2)
                if there(p + 1):
                    dve.wait_ge(*m_r.at(p + 1))
                    low(MK, p + 1, flo[0], fhi[0])
                    dve.wait_ge(*m_low[MK].at(p + 2))
                    mixed(MR, p + 1, 0, ht[1 - u])
                if first:
                    route_gain(0)
                    route_pick(1)
                if second:
                    hot(4)
                keys(3)
                keys(4)
                if there(p + 1):
                    dve.wait_ge(*m_k.at(p + 2))
                    dve.wait_ge(*m_rw.at(p + 1))
                    for c in range(HC):
                        last = dve.tensor_scalar(e2[:, c, :], ps[:, 4 + c, :], tfp[:, c:c + 1], 0.0, ALU.add, ALU.min)
                    last.then_inc(*m_delta.one)
                if first or second:
                    low(MR, p + 1, flo[0], fhi[0])
                if first:
                    route_gain(1)
                if second:
                    hot(5)
                if there(p):
                    dve.wait_ge(*w_ld.at(p + 1))
                    dve.tensor_reduce(big[:], stage[:], AX.X, ALU.max, apply_absolute_value=True).then_inc(*w_big.one)
                if there(p):
                    dve.wait_ge(*m_low[CMK].at(p))
                    mixed(CMR, p, 1, h2t[u])
                if there(p):
                    e = p
                    dve.wait_ge(*w_sum.at(e + 1))
                    dve.tensor_scalar(pw2[:], ps[:, 4, 0:3], 1e-30, None, ALU.max).then_inc(*w_top.one)
                if there(p + 1):
                    dve.wait_ge(*m_exp.at(p + 2))
                    dve.wait_ge(*m_v.at(p + 2))
                    dve.wait_ge(*m_rwlo.at(p + 1))
                    dve.scalar_tensor_tensor(av[:], ps[:, 2:4, :], 0.5, e2[:], ALU.mult, ALU.mult).then_inc(*m_av.one)
                if there(p):
                    dve.wait_ge(*w_top.at(e + 1))
                    dve.tensor_scalar(pw2[:].bitcast(I32), pw2[:].bitcast(I32), 0x7F800000, None,
                                      ALU.bitwise_and).then_inc(*w_pow.one)
                    dve.wait_ge(*w_pow.at(e + 1))
                    dve.tensor_scalar(pwi[:], pw2[:], 2.0 ** -14, None, ALU.mult).then_inc(*w_inv.one)
                    dve.wait_ge(*w_inv.at(e + 1))
                    dve.reciprocal(scl[:], pwi[:]).then_inc(*w_scl.one)
                    dve.tensor_copy(unscale[:, bass.ds(e, 1), :].rearrange("p a b -> p (a b)"), pwi[:])
                keys(5)
                if first:
                    route_bases()
                if second:
                    hot(6)
                    hot(7)
                keys(6)
                expert_low(0)
                if there(p) and not second:
                    dve.wait_ge(*m_low[CMR].at(p + 1))
                    mixed(CMK, p, 1, h2t[u])
                if there(p + 1):
                    dve.wait_ge(*m_wkv.at(p + 2))
                    dve.wait_ge(*m_tr.at(p + 2))
                    dve.scalar_tensor_tensor(av[:], e2[:], 1.0, av[:], ALU.add, ALU.mult).then_inc(*m_rw.one)
                keys(7)
                if there(p + 1):
                    dve.wait_ge(*m_rwhi.at(p + 2))
                    dve.tensor_tensor(flo[1][:], av[:], fhi[1][:].bitcast(F32), ALU.subtract).then_inc(*m_rwlo.one)
                if first:
                    route_slots()
                    route_experts()
                expert_low(1)
                expert_low(2)
                if second:
                    route_rows()
                    dve.wait_ge(*m_low[CMR].at(p + 1))
                    mixed(CMK, p, 1, h2t[u])

            def rows(bank):
                return ps[:, bank:bank + 2, :].rearrange("p b (j n) -> p (b j) n", n=H)

            dve.wait_ge(*o_zero.at(1))
            periods(dve, mix_dve)

            def hidden_dve(s, u):
                i = 2 * s + u
                dve.wait_ge(*e_sa.at(i + 1))
                dve.wait_ge(*e_hlo.at(i - 1))
                dve.tensor_tensor(hh[u][:], ps[:, 4 - 2 * u, :], sa[u][:], ALU.mult).then_inc(*e_h.one)
                dve.wait_ge(*e_h.at(i + 1))
                dve.wait_ge(*e_inv.at(i - 1))
                dve.tensor_reduce(hmax[u][:], hh[u][:], AX.X, ALU.max,
                                  apply_absolute_value=True).then_inc(*e_max.one)
                dve.wait_ge(*e_max.at(2 * i + 1))
                dve.tensor_scalar(hmax[u][:], hmax[u][:], 1e-30, 2.0 ** -14, ALU.max, ALU.mult).then_inc(*e_max.one)
                dve.wait_ge(*e_max.at(2 * i + 2))
                dve.reciprocal(hinv[u][:], hmax[u][:])
                dve.tensor_tensor(yscl[:, bass.ds(i, 1)], hmax[u][:], uny[:, bass.ds(i, 1)],
                                  ALU.mult).then_inc(*e_inv.one)

            def hidden_low(s, u):
                i = 2 * s + u
                dve.wait_ge(*e_hhi.at(i + 1))
                dve.wait_ge(*e_htp.at(i - 1))
                dve.scalar_tensor_tensor(hlo[u][:], hh[u][:], hinv[u][:], hhi[u][:], ALU.mult,
                                         ALU.subtract).then_inc(*e_hlo.one)

            def step_dve(s, u, left):
                i = 2 * s + u
                dve.wait_ge(*e_htp.at(i + 1))
                dve.wait_ge(*e_dn.at(i - 1))
                dve.tensor_copy(htlo[u][:], ps[:, 0, :].bitcast(F16)[:, 0:F]).then_inc(*e_htlo.one)
                if left >= 1:
                    hidden_low(*tile_after(s, u, 1))
                if left >= 3:
                    x_dve(*tile_after(s, u, 3))
                if left >= 2:
                    hidden_dve(*tile_after(s, u, 2))

            x_dve(0, 1)
            hidden_dve(0, 0)
            hidden_low(0, 0)
            x_dve(1, 0)
            hidden_dve(0, 1)
            tiles(dve, step_dve, 3)

        @block.tensor
        def _(pe):
            credit(pe, n_tp, n_lg, r_perm, *m_tp, m_k, m_v, m_r, m_wo, m_cr, m_kk, m_val, m_utp, e_xtp, e_up, e_htp, e_dn)
            pe.wait_ge(*const_ok.at(N_CONST))
            pe.wait_ge(*const_ld.at(2))

            def turn(src, bank):
                for c in range(HC):
                    for j in range(BJ):
                        last = pe.transpose(ps[:, bank + c, j * P:(j + 1) * P], src[:, j, c * P:(c + 1) * P],
                                            id32[:])
                return last

            def norm_turn(g, v):
                pe.wait_ge(*n_xn.at(g + 1))
                pe.wait_ge(*n_xt.at(g - 1))
                turn(xq[v], 2 * (v % 2)).then_inc(*n_tp.one)

            def norm_gate(g, v):
                pe.wait_ge(*n_xt.at(g + 1))
                pe.wait_ge(*n_logit.at(g - 1))
                for j in range(BJ):
                    for c in range(HC):
                        last = pe.matmul(ps[:, 4 + v % 2, j * E:(j + 1) * E],
                                         (e2, rb)[v % 2][:, c, j * P:(j + 1) * P],
                                         gw[:, c, :], start=(c == 0), stop=(c == HC - 1))
                last.then_inc(*n_lg.one)

            with pe.Fori(0, NB // RING) as s:
                norm_turn(RING * s, 0)
                for v in range(1, RING):
                    norm_turn(RING * s + v, v)
                    norm_gate(RING * s + v - 1, v - 1)
                norm_gate(RING * s + RING - 1, RING - 1)

            def route_counts():
                pe.wait_ge(*r_dve.at(R_PICKS))
                pe.matmul(ps[:, 6, 0:NJ * E], before[:], cc[:], start=True, stop=True)
                pe.matmul(ps[:, 7, 0:NJ * E], ones[:, 0:P], cc[:], start=True, stop=True).then_inc(*r_pe.one)

            def permute(g):
                u = g % 2
                pe.wait_ge(*r_hot.at(g + 1))
                pe.wait_ge(*r_part.at(g + 1))
                for i in range(HG):
                    for k in range(TOPK):
                        mm = pe.matmul(ps[:, 7, 0:3 * NX], onelo[u][k][:, i, :],
                                       hirow[u][k][:, i, :, :].rearrange("p a b -> p (a b)"),
                                       start=g == 0 and i == 0 and k == 0,
                                       stop=g == NJ // HG - 1 and i == HG - 1 and k == TOPK - 1)
                mm.then_inc(*r_perm.one)

            pe.wait_ge(*wst_lo.at(1))

            def product(bank, w, width, m, hi, lo):
                for c in range(HC):
                    a = w + c * width + m * P
                    for i, (ww, t) in enumerate(((whi, hi), (whi, lo), (wlo, hi))):
                        last = pe.matmul(ps[:, bank, :], ww[:, a:a + P], t[:, c, :],
                                         start=(c == 0 and i == 0), stop=(c == HC - 1 and i == 2))
                return last

            def turn_slots(s, u):
                i = 2 * s + u
                pe.wait_ge(*e_g[u].at(s + 1))
                pe.wait_ge(*e_xtlo.at(i))
                for c in range(HC):
                    last = pe.transpose(ps[:, 6, c * P:(c + 1) * P], xg[u][:, c * P:(c + 1) * P], id32[:])
                last.then_inc(*e_xtp.one)

            def mix_pe(s, u):
                p = 2 * s + u
                first, second = at_period(p, -1), at_period(p, 0)

                def keys(q):
                    if there(p - 1):
                        if q == 0:
                            pe.wait_ge(*m_low[CMK].at(p))
                            pe.wait_ge(*m_tc.at(p))
                        if q >= 2:
                            pe.wait_ge(*m_sk.at(KQ * (p - 1) + q - 1))
                        product(6 + q % 2, WKEY, KEY, q, chi[0], clo[0]).then_inc(*m_kk.one)

                def value(q):
                    if there(p - 1):
                        if q == 0:
                            pe.wait_ge(*m_x2.at(p - 1))
                        pe.wait_ge(*m_sklo.at(KQ * (p - 1) + q + 1))
                        for m in range(HC):
                            a = WVAL + q * H + m * P
                            for i, (ww, t) in enumerate(((whi, skhi), (whi, sklo), (wlo, skhi))):
                                last = pe.matmul(ps[:, m, :], ww[:, a:a + P], t[q % 3][:],
                                                 start=(q == 0 and i == 0), stop=(q == KQ - 1 and i == 2))
                        last.then_inc(*m_val.one)

                if there(p):
                    pe.wait_ge(*m_av.at(p + 1))
                    pe.wait_ge(*m_rwlo.at(p + 1))
                    for j in range(BJ):
                        o = ps[:, 2 + j // 2, (j % 2) * H:(j % 2 + 1) * H]
                        for c in range(HC):
                            for i, (t, ww) in enumerate(((fhi[1], whi), (fhi[1], wlo), (flo[1], whi))):
                                last = pe.matmul(o, t[:, c, j * P:(j + 1) * P], ww[:, WO + c * H:WO + (c + 1) * H],
                                                 start=(c == 0 and i == 0), stop=(c == HC - 1 and i == 2))
                    last.then_inc(*m_wo.one)
                if second:
                    permute(0)
                    permute(1)
                if at_period(p, 1):
                    pe.wait_ge(*wst_lo.at(len(chunks)))
                    pe.wait_ge(*r_slots.at(1))
                if there(p - 1):
                    pe.wait_ge(*m_low[CMR].at(p))
                    pe.wait_ge(*m_sk.at(KQ * (p - 1)))
                    product(6, WCR, H, 0, chi[1], clo[1])
                    product(7, WCR, H, 1, chi[1], clo[1]).then_inc(*m_cr.one)
                if at_period(p, NB + 1):
                    turn_slots(0, 0)
                if there(p - 2):
                    pe.wait_ge(*m_u.at(p - 1))
                    for j in range(BJ):
                        for c in range(HC):
                            a = (j % 2) * H + c * P
                            last = pe.transpose(ps[:, j // 2, a:a + P], uu[:, c, j * P:(j + 1) * P], id32[:])
                    last.then_inc(*m_utp.one)
                keys(0)
                keys(1)
                if there(p + 1):
                    pe.wait_ge(*m_hn[0].at(p + 2))
                    pe.wait_ge(*m_x1.at(p + 1))
                    turn(hn, 2).then_inc(*m_tp[0].one)
                if second:
                    permute(2)
                keys(2)
                value(0)
                keys(3)
                value(1)
                if there(p):
                    pe.wait_ge(*m_hn[1].at(p + 1))
                    pe.wait_ge(*m_tr.at(p + 1))
                    turn(hn, 4).then_inc(*m_tp[1].one)
                if second:
                    permute(3)
                keys(4)
                value(2)
                if there(p + 1):
                    pe.wait_ge(*m_low[MK].at(p + 2))
                    if there(p):
                        pe.wait_ge(*m_ht[1].at(p + 1))
                    product(4, WK, H, 0, fhi[0], flo[0])
                    product(5, WK, H, 1, fhi[0], flo[0]).then_inc(*m_k.one)
                keys(5)
                value(3)
                if there(p + 1):
                    pe.wait_ge(*m_low[MV].at(p + 2))
                    pe.wait_ge(*m_ht[0].at(p + 2))
                    product(2, WV, H, 0, fhi[1], flo[1])
                    product(3, WV, H, 1, fhi[1], flo[1]).then_inc(*m_v.one)
                if second:
                    permute(4)
                    permute(5)
                keys(6)
                if there(p):
                    pe.wait_ge(*w_big.at(p + 1))
                    if there(p + 1):
                        pe.wait_ge(*m_delta.at(p + 2))
                    else:
                        pe.wait_ge(*m_ht[1].at(p + 1))
                    pe.matmul(ps[:, 4, 0:3], ones[:, 0:P], big[:], start=True, stop=True).then_inc(*w_sum.one)
                value(4)
                if there(p + 1):
                    pe.wait_ge(*m_low[MR].at(p + 2))
                    if there(p):
                        pe.wait_ge(*w_top.at(p + 1))
                    pe.wait_ge(*m_delta.at(p + 2))
                    product(4, WR, H, 0, fhi[0], flo[0])
                    product(5, WR, H, 1, fhi[0], flo[0]).then_inc(*m_r.one)
                if first:
                    route_counts()
                if second:
                    permute(6)
                    permute(7)
                keys(7)
                value(5)
                value(6)
                value(7)

            periods(pe, mix_pe)

            pe.wait_ge(*r_ready.at(1))
            alone(pe)

            def weights_of(s, u):
                return pe.value_load(tile_off[0:1, bass.ds(2 * s + u, 1)], min_val=0,
                                     max_val=(E - 1) * 2 * EW)

            def needed_by(s, u):
                return pe.value_load(tile_need[0:1, bass.ds(2 * s + u, 1)], min_val=1, max_val=E)

            def up(s, u, off, need):
                i = 2 * s + u
                if need is not None:
                    pe.wait_ge(e_here.sem, need)
                pe.wait_ge(*e_xtlo.at(i + 1))
                pe.wait_ge(*e_h.at(i - 1))
                for c in range(HC):
                    for n, (t, part) in enumerate(((xthi, 0), (xthi, EW), (xtlo, 0))):
                        for bank, w in ((3 - 2 * u, W1), (4 - 2 * u, W3)):
                            last = pe.matmul(ps[:, bank, :], t[u][:, c * P:(c + 1) * P],
                                             ew[:, bass.ds(off + (part + w + c * F), F)],
                                             start=(c == 0 and n == 0), stop=(c == HC - 1 and n == 2))
                last.then_inc(*e_up.one)

            def turn_hidden(s, u):
                i = 2 * s + u
                pe.wait_ge(*e_hlo.at(i + 1))
                pe.wait_ge(*e_hthi.at(i))
                pe.wait_ge(*e_htlo.at(i))
                for k in range(F // P):
                    for bank, t in ((5, hhi), (0, hlo)):
                        last = pe.transpose(ps[:, bank, :].bitcast(F16)[:, k * P:(k + 1) * P],
                                            t[u][:, k * P:(k + 1) * P], id16[:])
                last.then_inc(*e_htp.one)

            def down(s, u):
                i = 2 * s + u
                off = weights_of(s, u)
                pe.wait_ge(*e_hthi.at(i + 1))
                pe.wait_ge(*e_htlo.at(i + 1))
                pe.wait_ge(*e_y.at(i))
                for k in range(F // P):
                    for n, (t, part) in enumerate(((hthi, 0), (hthi, EW), (htlo, 0))):
                        last = pe.matmul(ps[:, 7, 0:H], t[u][:, k * P:(k + 1) * P],
                                         ew[:, bass.ds(off + (part + W2 + k * H), H)],
                                         start=(k == 0 and n == 0), stop=(k == F // P - 1 and n == 2))
                last.then_inc(*e_dn.one)

            def step_pe(s, u, left, check=False):
                if left >= 2:
                    ahead = tile_after(s, u, 2)
                    off, need = weights_of(*ahead), needed_by(*ahead) if check else None
                turn_hidden(s, u)
                if left >= 2:
                    up(*ahead, off, need)
                if left >= 3:
                    turn_slots(*tile_after(s, u, 3))
                down(s, u)

            turn_slots(0, 1)
            up(0, 0, weights_of(0, 0), needed_by(0, 0))
            pe.wait_ge(*m_x2.at(NB))
            up(0, 1, weights_of(0, 1), needed_by(0, 1))
            turn_slots(1, 0)
            tiles(pe, lambda s, u, left: step_pe(s, u, left, True), 3, rounds=(0, 1), rest=False)
            pe.wait_ge(*e_here.at(E))
            tiles(pe, step_pe, 3, rounds=(1, (NT - 3) // UNROLL))


def kernel(**inputs):
    import numpy as np
    import concourse.bacc as bacc
    from concourse.bass_utils import run_bass_kernel_spmd

    def row(name):
        return np.asarray(inputs["L0_attn_" + name])

    def halves(w):
        k, n = w.shape
        return w.reshape(k // P, P, n).transpose(1, 0, 2).reshape(P, -1)

    vecs = np.stack([row(n).reshape(HC, P) for n in
                     ("ln1_g", "ln1_b", "ln2_g", "ln2_b", "tm_first", "tm_mk", "tm_mv", "tm_mr",
                      "cm_mk", "cm_mr")], axis=-1).transpose(1, 0, 2)
    gate = np.asarray(inputs["L0_ffn_gate_w"]).T.reshape(HC, P, E).transpose(1, 0, 2)
    wmix = np.concatenate([halves(row(n).T) for n in ("Wk", "Wv", "Wr", "Wo", "Wcr", "Wkey", "Wval")], axis=1)
    w1, w2, w3 = (np.asarray(inputs["L0_ffn_" + n]) for n in ("w1", "w2", "w3"))
    wexp = np.concatenate([np.concatenate([halves(w1[e].T), halves(w3[e].T), halves(w2[e].T)], axis=1)
                           for e in range(E)], axis=0)
    arrays = {"x": row("x").reshape(T, H), "vecs": vecs, "gate": gate, "wmix": wmix, "wexp": wexp}
    arrays = {n: np.ascontiguousarray(a) for n, a in arrays.items()}

    nc = bacc.Bacc("TRN2", target_bir_lowering=False, num_devices=1)
    args = [nc.dram_tensor(n + "_in", a.shape, F32, kind="ExternalInput").ap() for n, a in arrays.items()]
    out = nc.dram_tensor("out_0", (T + P, H), F32, kind="ExternalOutput").ap()
    build(nc, *args, out)
    r = run_bass_kernel_spmd(nc, [{n + "_in": a for n, a in arrays.items()}], core_ids=[0])
    return np.asarray(r.results[0]["out_0"])[:T].reshape(NSEQ, SEQ, H)
```
